# Optimizing a Trainium2 kernel written in Bass

```python
import numpy as np
import jax
import jax.numpy as jnp

def _softmax(x, axis=-1):
    return jax.nn.softmax(x, axis=axis)

def _gelu(x):
    return jax.nn.gelu(x, approximate=True)

def _silu(x):
    return jax.nn.silu(x)

def _sigmoid(x):
    return jax.nn.sigmoid(x)

def _layernorm(x, axis=-1, eps=1e-05):
    m = jnp.mean(x, axis=axis, keepdims=True)
    v = jnp.var(x, axis=axis, keepdims=True)
    return (x - m) / jnp.sqrt(v + eps)

def _scatter_add(tgt, idx, src, axis=0):
    return tgt.at[idx].add(src)

def _segment_sum(src, seg, n):
    return jax.ops.segment_sum(src, seg, n)
kernel_name = 'mk_gps_d2_gnn_r32_3aa7dd'

def setup_inputs(seed: int=0):
    np.random.seed(seed)
    _w = jnp.asarray

    def _rec_inputs():
        import jax
        import jax.numpy as jnp
        _gk = jax.random.key(seed)
        x = -8.776e-05 + 1 * jax.random.normal(jax.random.fold_in(_gk, 1), (3125, 256), jnp.float32)
        src = jax.random.randint(jax.random.fold_in(_gk, 2), (50000,), 0, 3125, jnp.int32)
        dst = jax.random.randint(jax.random.fold_in(_gk, 3), (50000,), 0, 3125, jnp.int32)
        _o = jnp.argsort(dst, stable=True)
        src = src[_o]
        dst = dst[_o]
        edge_type_2 = jax.random.randint(jax.random.fold_in(_gk, 12), (50000,), 0, 2, jnp.int32)
        return (x, src, dst, edge_type_2)
    x, src, dst, edge_type_2 = _rec_inputs()

    def _L0_gnn_setup():
        import jax, jax.numpy as jnp
        import numpy as np
        N_NODES = 625
        N_EDGES = 10000
        D = 256
        N_LAYERS = 3
        N_RELS = 2
        LN_EPS = 1e-05

        def _layer_norm(h, gamma, beta):
            mu = jnp.mean(h, axis=-1, keepdims=True)
            var = jnp.mean(jnp.square(h - mu), axis=-1, keepdims=True)
            return (h - mu) * jax.lax.rsqrt(var + LN_EPS) * gamma + beta
        key = jax.random.key(seed)
        ks = jax.random.split(key, 10)
        x = jax.random.normal(ks[0], (N_NODES, D), dtype=jnp.float32)
        src = jax.random.randint(ks[1], (N_EDGES,), 0, N_NODES)
        dst = jax.random.randint(ks[2], (N_EDGES,), 0, N_NODES)
        etype = jnp.sort(jax.random.randint(ks[3], (N_EDGES,), 0, N_RELS))
        scale = 1.0 / np.sqrt(D)
        W = jax.random.normal(ks[4], (N_LAYERS, N_RELS, D, D), dtype=jnp.float32) * scale
        bias = jnp.zeros((N_LAYERS, D), dtype=jnp.float32)
        loop_w = jax.random.normal(ks[5], (N_LAYERS, D, D), dtype=jnp.float32) * scale
        ln_gamma = jnp.ones((N_LAYERS, D), dtype=jnp.float32)
        ln_beta = jnp.zeros((N_LAYERS, D), dtype=jnp.float32)
        return {'x': x, 'W': W, 'bias': bias, 'loop_w': loop_w, 'ln_gamma': ln_gamma, 'ln_beta': ln_beta, 'src': src, 'dst': dst, 'etype': etype}
    _L0_gnn_all = _L0_gnn_setup()
    _L0_gnn_in = {k: v for k, v in _L0_gnn_all.items() if k in ('W', 'bias', 'loop_w', 'ln_gamma', 'ln_beta')}
    del _L0_gnn_all

    def _L0_mix_setup():
        import jax, jax.numpy as jnp
        import numpy as np
        A, Bc, Cc = (0.5, 1.0, 1.0)
        H = 8
        EPS = 1e-12

        def _normalize(t):
            n = jnp.linalg.norm(t, axis=-1, keepdims=True)
            return t / jnp.maximum(n, EPS)
        key = jax.random.key(seed)
        ks = jax.random.split(key, 5)
        B, N, C = (8, 64, 256)
        D = C // H
        x = jax.random.normal(ks[0], (B, N, C), dtype=jnp.float32)
        Wqkv = jax.random.normal(ks[1], (3 * H * D, C), dtype=jnp.float32) * 0.02
        bqkv = jnp.zeros((3 * H * D,), dtype=jnp.float32)
        Wproj = jax.random.normal(ks[2], (C, H * D), dtype=jnp.float32) * 0.02
        bproj = jnp.zeros((C,), dtype=jnp.float32)
        temperature = jnp.ones((1, H, 1, 1), dtype=jnp.float32)
        return {'x': x, 'Wqkv': Wqkv, 'bqkv': bqkv, 'Wproj': Wproj, 'bproj': bproj, 'temperature': temperature}
    _L0_mix_all = _L0_mix_setup()
    _L0_mix_in = {k: v for k, v in _L0_mix_all.items() if k in ('Wqkv', 'bqkv', 'Wproj', 'bproj', 'temperature')}
    del _L0_mix_all

    def _L0_ffn_setup():
        import math
        import jax, jax.numpy as jnp
        import numpy as np
        CAPACITY_FACTOR = 1.25
        TOP_K = 2
        LN_EPS = 1e-05

        def _layer_norm(x, gamma, beta):
            mu = jnp.mean(x, axis=-1, keepdims=True)
            var = jnp.var(x, axis=-1, keepdims=True)
            return (x - mu) * jax.lax.rsqrt(var + LN_EPS) * gamma + beta
        key = jax.random.key(seed)
        ks = jax.random.split(key, 4)
        B, S, D, F, E = (8, 128, 256, 512, 8)
        x = jax.random.normal(ks[0], (B, S, D), dtype=jnp.float32)
        Wr = jax.random.normal(ks[1], (D, E), dtype=jnp.float32) / np.sqrt(D)
        br = jnp.zeros((E,), jnp.float32)
        W1 = jax.random.normal(ks[2], (E, D, F), dtype=jnp.float32) / np.sqrt(D)
        b1 = jnp.zeros((E, F), jnp.float32)
        W2 = jax.random.normal(ks[3], (E, F, D), dtype=jnp.float32) / np.sqrt(F)
        b2 = jnp.zeros((E, D), jnp.float32)
        gamma = jnp.ones((D,), jnp.float32)
        beta = jnp.zeros((D,), jnp.float32)
        return {'x': x, 'Wr': Wr, 'br': br, 'W1': W1, 'b1': b1, 'W2': W2, 'b2': b2, 'gamma': gamma, 'beta': beta}
    _L0_ffn_all = _L0_ffn_setup()
    _L0_ffn_in = {k: v for k, v in _L0_ffn_all.items() if k in ('Wr', 'br', 'W1', 'b1', 'W2', 'b2', 'gamma', 'beta')}
    del _L0_ffn_all

    def _L1_gnn_setup():
        import jax, jax.numpy as jnp
        import numpy as np
        N_NODES = 3125
        N_EDGES = 100000
        D_IN = 256
        D_OUT = 256
        key = jax.random.key(seed)
        k1, k2, k3, k4 = jax.random.split(key, 4)
        x = jax.random.normal(k1, (N_NODES, D_IN), dtype=jnp.float32)
        W = jax.random.normal(k2, (D_OUT, D_IN), dtype=jnp.float32) / np.sqrt(D_IN).astype(np.float32)
        bias = jnp.zeros((D_OUT,), dtype=jnp.float32)
        rows = jax.random.randint(k3, (N_EDGES,), 0, N_NODES, dtype=jnp.int32)
        cols = jax.random.randint(k4, (N_EDGES,), 0, N_NODES, dtype=jnp.int32)
        return {'x': x, 'W': W, 'bias': bias, 'rows': rows, 'cols': cols}
    _L1_gnn_all = _L1_gnn_setup()
    _L1_gnn_in = {k: v for k, v in _L1_gnn_all.items() if k in ('W', 'bias')}
    del _L1_gnn_all

    def _L1_mix_setup():
        import jax, jax.numpy as jnp
        import numpy as np
        import math
        EMBED = 256
        HEADS = 4
        HEAD_DIM = EMBED // HEADS
        OUT_DIM = 256
        LN_EPS = 1e-05

        def _qkv_init(key):
            spread = math.sqrt(3.0 / EMBED)
            gain, delta = (0.01, 0.01)
            w = jax.random.uniform(key, (EMBED, EMBED), minval=-spread, maxval=spread) * gain
            return w + delta * jnp.eye(EMBED, dtype=w.dtype)

        def _layer_norm(x, g, b):
            mu = jnp.mean(x, axis=-1, keepdims=True)
            var = jnp.mean(jnp.square(x - mu), axis=-1, keepdims=True)
            return (x - mu) * jax.lax.rsqrt(var + LN_EPS) * g + b

        def _split_heads(x, B, S):
            return x.reshape(B, S, HEADS, HEAD_DIM).transpose(0, 2, 1, 3)
        key = jax.random.key(seed)
        ks = jax.random.split(key, 6)
        seq = jax.random.normal(ks[0], (4, 256, EMBED), dtype=jnp.float32)
        wq = _qkv_init(ks[1])
        wk = _qkv_init(ks[2])
        wv = _qkv_init(ks[3])
        bound = 1.0 / math.sqrt(EMBED)
        wo = jax.random.uniform(ks[4], (OUT_DIM, EMBED), minval=-bound, maxval=bound)
        bo = jax.random.uniform(ks[5], (OUT_DIM,), minval=-bound, maxval=bound)
        ln_k_g = jnp.ones((HEAD_DIM,), jnp.float32)
        ln_k_b = jnp.zeros((HEAD_DIM,), jnp.float32)
        ln_v_g = jnp.ones((HEAD_DIM,), jnp.float32)
        ln_v_b = jnp.zeros((HEAD_DIM,), jnp.float32)
        return {'seq': seq, 'wq': wq, 'wk': wk, 'wv': wv, 'wo': wo, 'bo': bo, 'ln_k_g': ln_k_g, 'ln_k_b': ln_k_b, 'ln_v_g': ln_v_g, 'ln_v_b': ln_v_b}
    _L1_mix_all = _L1_mix_setup()
    _L1_mix_in = {k: v for k, v in _L1_mix_all.items() if k in ('wq', 'wk', 'wv', 'wo', 'bo', 'ln_k_g', 'ln_k_b', 'ln_v_g', 'ln_v_b')}
    del _L1_mix_all

    def _L1_ffn_setup():
        import jax, jax.numpy as jnp
        import numpy as np
        DIM = 256
        H = 8
        D = 64
        G = 64
        INNER = H * D
        SCALE = D ** (-0.5)
        key = jax.random.key(seed)
        ks = jax.random.split(key, 12)
        B, N = (4, 512)
        x = jax.random.normal(ks[0], (B, N, DIM), dtype=jnp.float32)
        s = lambda fan_in: 1.0 / np.sqrt(fan_in)
        W_fx = jax.random.normal(ks[1], (DIM, INNER), dtype=jnp.float32) * s(DIM)
        b_fx = jnp.zeros((INNER,), dtype=jnp.float32)
        W_x = jax.random.normal(ks[2], (DIM, INNER), dtype=jnp.float32) * s(DIM)
        b_x = jnp.zeros((INNER,), dtype=jnp.float32)
        A = jax.random.normal(ks[3], (G, D), dtype=jnp.float32)
        Q, _ = jnp.linalg.qr(A.T)
        W_slice = Q[:, :G].astype(jnp.float32)
        b_slice = jnp.zeros((G,), dtype=jnp.float32)
        W_q = jax.random.normal(ks[4], (D, D), dtype=jnp.float32) * s(D)
        W_k = jax.random.normal(ks[5], (D, D), dtype=jnp.float32) * s(D)
        W_v = jax.random.normal(ks[6], (D, D), dtype=jnp.float32) * s(D)
        W_out = jax.random.normal(ks[7], (INNER, DIM), dtype=jnp.float32) * s(INNER)
        b_out = jnp.zeros((DIM,), dtype=jnp.float32)
        temperature = jnp.ones((1, H, 1, 1), dtype=jnp.float32) * 0.5
        return {'x': x, 'W_fx': W_fx, 'b_fx': b_fx, 'W_x': W_x, 'b_x': b_x, 'W_slice': W_slice, 'b_slice': b_slice, 'W_q': W_q, 'W_k': W_k, 'W_v': W_v, 'W_out': W_out, 'b_out': b_out, 'temperature': temperature}
    _L1_ffn_all = _L1_ffn_setup()
    _L1_ffn_in = {k: v for k, v in _L1_ffn_all.items() if k in ('W_fx', 'b_fx', 'W_x', 'b_x', 'W_slice', 'b_slice', 'W_q', 'W_k', 'W_v', 'W_out', 'b_out', 'temperature')}
    del _L1_ffn_all
    return {'x': x, 'src': src, 'dst': dst, 'edge_type_2': edge_type_2, 'L0_gnn_W': _L0_gnn_in['W'], 'L0_gnn_bias': _L0_gnn_in['bias'], 'L0_gnn_loop_w': _L0_gnn_in['loop_w'], 'L0_gnn_ln_gamma': _L0_gnn_in['ln_gamma'], 'L0_gnn_ln_beta': _L0_gnn_in['ln_beta'], 'L0_mix_Wqkv': _L0_mix_in['Wqkv'], 'L0_mix_bqkv': _L0_mix_in['bqkv'], 'L0_mix_Wproj': _L0_mix_in['Wproj'], 'L0_mix_bproj': _L0_mix_in['bproj'], 'L0_mix_temperature': _L0_mix_in['temperature'], 'L0_ffn_Wr': _L0_ffn_in['Wr'], 'L0_ffn_br': _L0_ffn_in['br'], 'L0_ffn_W1': _L0_ffn_in['W1'], 'L0_ffn_b1': _L0_ffn_in['b1'], 'L0_ffn_W2': _L0_ffn_in['W2'], 'L0_ffn_b2': _L0_ffn_in['b2'], 'L0_ffn_gamma': _L0_ffn_in['gamma'], 'L0_ffn_beta': _L0_ffn_in['beta'], 'L1_gnn_W': _L1_gnn_in['W'], 'L1_gnn_bias': _L1_gnn_in['bias'], 'L1_mix_wq': _L1_mix_in['wq'], 'L1_mix_wk': _L1_mix_in['wk'], 'L1_mix_wv': _L1_mix_in['wv'], 'L1_mix_wo': _L1_mix_in['wo'], 'L1_mix_bo': _L1_mix_in['bo'], 'L1_mix_ln_k_g': _L1_mix_in['ln_k_g'], 'L1_mix_ln_k_b': _L1_mix_in['ln_k_b'], 'L1_mix_ln_v_g': _L1_mix_in['ln_v_g'], 'L1_mix_ln_v_b': _L1_mix_in['ln_v_b'], 'L1_ffn_W_fx': _L1_ffn_in['W_fx'], 'L1_ffn_b_fx': _L1_ffn_in['b_fx'], 'L1_ffn_W_x': _L1_ffn_in['W_x'], 'L1_ffn_b_x': _L1_ffn_in['b_x'], 'L1_ffn_W_slice': _L1_ffn_in['W_slice'], 'L1_ffn_b_slice': _L1_ffn_in['b_slice'], 'L1_ffn_W_q': _L1_ffn_in['W_q'], 'L1_ffn_W_k': _L1_ffn_in['W_k'], 'L1_ffn_W_v': _L1_ffn_in['W_v'], 'L1_ffn_W_out': _L1_ffn_in['W_out'], 'L1_ffn_b_out': _L1_ffn_in['b_out'], 'L1_ffn_temperature': _L1_ffn_in['temperature']}

def reference(x, src, dst, edge_type_2, L0_gnn_W, L0_gnn_bias, L0_gnn_loop_w, L0_gnn_ln_gamma, L0_gnn_ln_beta, L0_mix_Wqkv, L0_mix_bqkv, L0_mix_Wproj, L0_mix_bproj, L0_mix_temperature, L0_ffn_Wr, L0_ffn_br, L0_ffn_W1, L0_ffn_b1, L0_ffn_W2, L0_ffn_b2, L0_ffn_gamma, L0_ffn_beta, L1_gnn_W, L1_gnn_bias, L1_mix_wq, L1_mix_wk, L1_mix_wv, L1_mix_wo, L1_mix_bo, L1_mix_ln_k_g, L1_mix_ln_k_b, L1_mix_ln_v_g, L1_mix_ln_v_b, L1_ffn_W_fx, L1_ffn_b_fx, L1_ffn_W_x, L1_ffn_b_x, L1_ffn_W_slice, L1_ffn_b_slice, L1_ffn_W_q, L1_ffn_W_k, L1_ffn_W_v, L1_ffn_W_out, L1_ffn_b_out, L1_ffn_temperature):
    import jax
    import jax.numpy as jnp

    def _L0_gnn_ref(x, W, bias, loop_w, ln_gamma, ln_beta, src, dst, etype):
        import jax, jax.numpy as jnp
        import numpy as np
        N_NODES = 625
        N_EDGES = 10000
        D = 256
        N_LAYERS = 3
        N_RELS = 2
        LN_EPS = 1e-05

        def _layer_norm(h, gamma, beta):
            mu = jnp.mean(h, axis=-1, keepdims=True)
            var = jnp.mean(jnp.square(h - mu), axis=-1, keepdims=True)
            return (h - mu) * jax.lax.rsqrt(var + LN_EPS) * gamma + beta
        n = x.shape[0]
        is_r0 = (etype == 0)[:, None]
        h = x
        for l in range(N_LAYERS):
            xs = h[src]
            m = jnp.where(is_r0, xs @ W[l, 0], xs @ W[l, 1])
            agg = jax.ops.segment_sum(m, dst, num_segments=n)
            hn = _layer_norm(agg, ln_gamma[l], ln_beta[l])
            hn = hn + bias[l]
            hn = hn + h @ loop_w[l]
            if l < N_LAYERS - 1:
                hn = jax.nn.relu(hn)
            h = hn
        return h

    def _L0_mix_ref(x, Wqkv, bqkv, Wproj, bproj, temperature):
        import jax, jax.numpy as jnp
        import numpy as np
        A, Bc, Cc = (0.5, 1.0, 1.0)
        H = 8
        EPS = 1e-12

        def _normalize(t):
            n = jnp.linalg.norm(t, axis=-1, keepdims=True)
            return t / jnp.maximum(n, EPS)
        B, N, C = x.shape
        D = C // H
        scale = float(D) ** 0.25
        qkv = (x @ Wqkv.T + bqkv).reshape(B, N, 3, H, D)
        qkv = jnp.transpose(qkv, (2, 0, 3, 1, 4))
        q, k, v = (qkv[0], qkv[1], qkv[2])
        q = q * scale
        v1 = jnp.concatenate([jnp.ones((B, H, N, 1), dtype=v.dtype), v], axis=-1)
        qn = _normalize(q) * (scale * temperature)
        kn = _normalize(k) * scale
        vN = v1 / N
        kv_mod = jnp.einsum('bhni,bhnj,bhne->bhije', kn, kn, vN)
        kv = jnp.einsum('bhnd,bhne->bhde', kn, vN)
        vsum = jnp.sum(vN, axis=-2)[:, :, None, :]
        y = A * jnp.einsum('bhni,bhnj,bhije->bhne', qn, qn, kv_mod) + scale ** 2 * Bc * jnp.einsum('bhnd,bhde->bhne', qn, kv) + scale ** 4 * Cc * vsum
        y_norm, y = (y[..., :1], y[..., 1:])
        y = y / y_norm
        out = jnp.transpose(y, (0, 2, 1, 3)).reshape(B, N, H * D)
        return out @ Wproj.T + bproj

    def _L0_ffn_ref(x, Wr, br, W1, b1, W2, b2, gamma, beta):
        import math
        import jax, jax.numpy as jnp
        import numpy as np
        CAPACITY_FACTOR = 1.25
        TOP_K = 2
        LN_EPS = 1e-05

        def _layer_norm(x, gamma, beta):
            mu = jnp.mean(x, axis=-1, keepdims=True)
            var = jnp.var(x, axis=-1, keepdims=True)
            return (x - mu) * jax.lax.rsqrt(var + LN_EPS) * gamma + beta
        B, S, D = x.shape
        E = Wr.shape[1]
        N = B * S
        K = TOP_K
        logits = jnp.mean(x, axis=1) @ Wr + br
        routing_weights = jax.nn.softmax(logits, axis=-1)
        capacity = float(math.ceil(N * CAPACITY_FACTOR / E))
        expected_loads = routing_weights.sum(axis=0) * (N / B)
        scale = jnp.where(expected_loads > capacity, capacity / expected_loads, 1.0)
        routing_weights = jax.nn.softmax(routing_weights * scale, axis=-1)
        rw_tok = jnp.broadcast_to(routing_weights[:, None, :], (B, S, E)).reshape(N, E)
        top_w, top_i = jax.lax.top_k(rw_tok, K)
        top_w = jax.nn.softmax(top_w, axis=-1)
        xf = x.reshape(N, D)
        h = jax.nn.gelu(jnp.einsum('nd,edf->enf', xf, W1) + b1[:, None, :], approximate=False)
        y = jnp.einsum('enf,efd->end', h, W2) + b2[:, None, :]
        w_dense = jnp.zeros((N, E), x.dtype).at[jnp.arange(N)[:, None], top_i].add(top_w)
        out = jnp.einsum('ne,end->nd', w_dense, y).reshape(B, S, D)
        out = _layer_norm(out + x, gamma, beta)
        return out

    def _L1_gnn_ref(x, W, bias, rows, cols):
        import jax, jax.numpy as jnp
        import numpy as np
        N_NODES = 3125
        N_EDGES = 100000
        D_IN = 256
        D_OUT = 256
        n = x.shape[0]
        h = x @ W.T + bias
        deg = jax.ops.segment_sum(jnp.ones(rows.shape, x.dtype), rows, num_segments=n)
        norm = jax.lax.rsqrt(1.0 + deg)[:, None]
        h = norm * h
        agg = jax.ops.segment_sum(h[cols], rows, num_segments=n)
        h = agg + h
        return norm * h

    def _L1_mix_ref(seq, wq, wk, wv, wo, bo, ln_k_g, ln_k_b, ln_v_g, ln_v_b):
        import jax, jax.numpy as jnp
        import numpy as np
        import math
        EMBED = 256
        HEADS = 4
        HEAD_DIM = EMBED // HEADS
        OUT_DIM = 256
        LN_EPS = 1e-05

        def _qkv_init(key):
            spread = math.sqrt(3.0 / EMBED)
            gain, delta = (0.01, 0.01)
            w = jax.random.uniform(key, (EMBED, EMBED), minval=-spread, maxval=spread) * gain
            return w + delta * jnp.eye(EMBED, dtype=w.dtype)

        def _layer_norm(x, g, b):
            mu = jnp.mean(x, axis=-1, keepdims=True)
            var = jnp.mean(jnp.square(x - mu), axis=-1, keepdims=True)
            return (x - mu) * jax.lax.rsqrt(var + LN_EPS) * g + b

        def _split_heads(x, B, S):
            return x.reshape(B, S, HEADS, HEAD_DIM).transpose(0, 2, 1, 3)
        B, S, _ = seq.shape
        q = _split_heads(seq @ wq.T, B, S)
        k = _split_heads(seq @ wk.T, B, S)
        v = _split_heads(seq @ wv.T, B, S)
        k = _layer_norm(k, ln_k_g, ln_k_b)
        v = _layer_norm(v, ln_v_g, ln_v_b)
        kv = jnp.einsum('bhsd,bhse->bhde', k, v) / S
        ga = jnp.einsum('bhsd,bhde->bhse', q, kv)
        ga = ga.transpose(0, 2, 1, 3).reshape(B, S, EMBED)
        return ga @ wo.T + bo

    def _L1_ffn_ref(x, W_fx, b_fx, W_x, b_x, W_slice, b_slice, W_q, W_k, W_v, W_out, b_out, temperature):
        import jax, jax.numpy as jnp
        import numpy as np
        DIM = 256
        H = 8
        D = 64
        G = 64
        INNER = H * D
        SCALE = D ** (-0.5)
        B, N, _ = x.shape
        fx_mid = (x @ W_fx + b_fx).reshape(B, N, H, D).transpose(0, 2, 1, 3)
        x_mid = (x @ W_x + b_x).reshape(B, N, H, D).transpose(0, 2, 1, 3)
        temp = jnp.clip(temperature, 0.1, 5.0)
        slice_weights = jax.nn.softmax((x_mid @ W_slice + b_slice) / temp, axis=-1)
        slice_norm = slice_weights.sum(axis=2)
        slice_token = jnp.einsum('bhnc,bhng->bhgc', fx_mid, slice_weights)
        slice_token = slice_token / (slice_norm[..., None] + 1e-05)
        q = slice_token @ W_q
        k = slice_token @ W_k
        v = slice_token @ W_v
        attn = jax.nn.softmax(jnp.einsum('bhgc,bhkc->bhgk', q, k) * SCALE, axis=-1)
        out_slice = jnp.einsum('bhgk,bhkc->bhgc', attn, v)
        out_x = jnp.einsum('bhgc,bhng->bhnc', out_slice, slice_weights)
        out_x = out_x.transpose(0, 2, 1, 3).reshape(B, N, INNER)
        return out_x @ W_out + b_out
    xn = _layernorm(x, axis=-1)
    x = x + _L0_gnn_ref(xn, L0_gnn_W, L0_gnn_bias, L0_gnn_loop_w, L0_gnn_ln_gamma, L0_gnn_ln_beta, src, dst, edge_type_2) + _L0_mix_ref(xn[None], L0_mix_Wqkv, L0_mix_bqkv, L0_mix_Wproj, L0_mix_bproj, L0_mix_temperature)[0]
    x = x + _L0_ffn_ref(_layernorm(x, axis=-1)[None], L0_ffn_Wr, L0_ffn_br, L0_ffn_W1, L0_ffn_b1, L0_ffn_W2, L0_ffn_b2, L0_ffn_gamma, L0_ffn_beta)[0]
    xn = _layernorm(x, axis=-1)
    x = x + _L1_gnn_ref(xn, L1_gnn_W, L1_gnn_bias, src, dst) + _L1_mix_ref(xn[None], L1_mix_wq, L1_mix_wk, L1_mix_wv, L1_mix_wo, L1_mix_bo, L1_mix_ln_k_g, L1_mix_ln_k_b, L1_mix_ln_v_g, L1_mix_ln_v_b)[0]
    x = x + _L1_ffn_ref(_layernorm(x, axis=-1)[None], L1_ffn_W_fx, L1_ffn_b_fx, L1_ffn_W_x, L1_ffn_b_x, L1_ffn_W_slice, L1_ffn_b_slice, L1_ffn_W_q, L1_ffn_W_k, L1_ffn_W_v, L1_ffn_W_out, L1_ffn_b_out, L1_ffn_temperature)[0]
    return x

_drawn_inputs = setup_inputs


def setup_inputs(seed=0):
    import zlib

    import numpy as np

    out = dict(_drawn_inputs(seed))
    spreads = {'L0_gnn_bias': (0.0, 0.1),
     'L0_gnn_ln_gamma': (1.0, 0.2),
     'L0_gnn_ln_beta': (0.0, 0.1),
     'L0_mix_bqkv': (0.0, 0.444),
     'L0_mix_bproj': (0.0, 0.1),
     'L0_mix_temperature': (1.0, 0.6),
     'L0_ffn_br': (0.0, 0.1),
     'L0_ffn_b1': (0.0, 0.47),
     'L0_ffn_b2': (0.0, 0.289),
     'L0_ffn_gamma': (1.0, 0.2),
     'L0_ffn_beta': (0.0, 0.1),
     'L1_gnn_bias': (0.0, 0.1),
     'L1_mix_ln_k_g': (1.0, 0.6),
     'L1_mix_ln_k_b': (0.0, 0.8),
     'L1_mix_ln_v_g': (1.0, 0.6),
     'L1_mix_ln_v_b': (0.0, 0.8),
     'L1_ffn_b_fx': (0.0, 0.1),
     'L1_ffn_b_x': (0.0, 0.8),
     'L1_ffn_b_slice': (0.0, 2.0),
     'L1_ffn_b_out': (0.0, 0.1),
     'L1_ffn_temperature': (0.5, 0.6)}
    factors = {'L0_mix_Wqkv': 8.0,
     'L1_mix_wq': 3.259,
     'L1_mix_wk': 3.023,
     'L1_mix_bo': 4.094,
     'L1_ffn_W_x': 7.135,
     'L1_ffn_W_slice': 8.0,
     'L1_ffn_W_q': 8.0,
     'L1_ffn_W_k': 8.0}
    for name, (base, spread) in spreads.items():
        noise = np.random.default_rng([zlib.crc32(name.encode()), seed]).standard_normal(out[name].shape)
        drawn = base * np.exp(spread * noise) if base else spread * noise
        out[name] = jnp.asarray(drawn.astype(out[name].dtype))
    for name, factor in factors.items():
        out[name] = (out[name] * factor).astype(out[name].dtype)
    return out
```

```python
from contextlib import ExitStack, contextmanager

import concourse.bass as bass
from concourse import mybir

F32 = mybir.dt.float32
I32 = mybir.dt.int32
U32 = mybir.dt.uint32
I16 = mybir.dt.int16
ALU = mybir.AluOpType
ACT = mybir.ActivationFunctionType
AX = mybir.AxisListType
ds = bass.ds

P = 128
N = 3125
D = 256
E = 50000
TILES = (N + P - 1) // P
NP = TILES * P
LAST = N - (TILES - 1) * P
CHUNKS = (E + P - 1) // P
FULL = E // P
REST = E - FULL * P
PAIRS = CHUNKS + TILES - 1
TAB = 512
PAD_DST = 4095
RING = 32
STEP = 16
TURNS = TILES - 1
TAIL = PAIRS - TURNS * STEP
EPS = 1e-5


class Count:

    def __init__(self, sem):
        self.sem, self.base, self.n = sem, 0, 0

    def inc(self, ins, by=1):
        ins.then_inc(self.sem, by)
        self.n += by
        return ins

    def wait(self, eng):
        eng.wait_ge(self.sem, self.base + self.n)


@contextmanager
def turns(eng, first, end, counts):
    start = [c.base + c.n for c, _ in counts]
    with eng.Fori(first, end) as i:
        for (c, k), b in zip(counts, start):
            c.base, c.n = b + (i - first) * k, 0
        yield i
        for c, k in counts:
            assert c.n == k, (c.sem, c.n, k)
    for (c, k), b in zip(counts, start):
        c.base, c.n = b + (end - first) * k, 0


def tiles4(eng, body, counts=()):
    with turns(eng, 0, TURNS // 4, [(c, 4 * k) for c, k in counts]) as i:
        for j in range(4):
            body(i * 4 + j, j)
    body(TURNS, 0)


def stage_semaphores(nc, stack, prefix=""):
    taken = []

    @stack.callback
    def clear():
        if taken:
            nc.clear_and_free_semaphores(taken)
            nc.all_engine_barrier(sem_only=True)

    def sem(name):
        taken.append(nc.alloc_semaphore(prefix + name))
        return taken[-1]
    return sem


class Memory:

    SCRATCH = 18000

    def __init__(self, nc):
        self.stack = ExitStack()
        sb = lambda name, shape, dt=F32: self.stack.enter_context(nc.sbuf_tensor(name, shape, dt))
        self.X = sb("X", [P, TILES, D])
        self.AGG = sb("AGG", [P, TILES, D])
        self.big = sb("big", [P, RING * D + TILES * D])
        self.ring = self.big[:, 0:RING * D].rearrange("p (s d) -> p s d", s=RING)
        self.L = self.big[:, RING * D:].rearrange("p (t d) -> p t d", t=TILES)
        self.ident, self.ones = sb("ident", [P, P]), sb("ones", [P, P])
        self.pcol, self.valid, self.eps = sb("pcol", [P, 4]), sb("valid", [P, TILES]), sb("eps", [P, 1])
        self.zeros = sb("zeros", [P, D + 1])
        self.iota = sb("iota", [P, NP], I16)
        self.dstT = sb("dstT", [P, TAB])
        self.dloc = sb("dloc", [P, TAB])
        self.idx = sb("idx", [P, 2, TAB], I32)
        self.tab = sb("tab", [1, 4, TAB], I32)
        self.ir = sb("ir", [P, RING], I32)
        self.oh = sb("oh", [P, 8, P])
        self.iotaf = sb("iotaf", [P, P])
        self.bn, self.mv4, self.mv = sb("bn", [P, 5, 6]), sb("mv4", [P, 5, 2]), sb("mv", [P, TILES, 2])
        self.std, self.rstd, self.norm = sb("std", [P, TILES]), sb("rstd", [P, TILES]), sb("norm", [P, TILES])
        self.scratch = sb("scratch", [P, self.SCRATCH])
        self.used = 0
        dram = lambda name, shape, dt=F32: nc.dram_tensor(name, shape, dt, kind="Internal").ap()
        self.t_dram = dram("t_dram", [2, TILES, P, D])
        self.xt_dram = dram("xt_dram", [4, TILES, P, D])
        self.sorted_dram = dram("sorted_dram", [E, 2], I32)
        self.gathered = [self.stack.enter_context(nc.semaphore(f"gathered{j}")) for j in range(STEP)]
        self.gather_count = [0] * STEP
        self.woken_sp = self.stack.enter_context(nc.semaphore("woken_sp"))

    def take(self, shape, dt=F32):
        n = 1
        for d in shape[1:]:
            n *= d
        at, self.used = self.used, self.used + n
        assert self.used <= self.SCRATCH, self.used
        ap = self.scratch[0:shape[0], at:at + n]
        if dt != F32:
            ap = ap.bitcast(dt)
        names = "abcd"[:len(shape) - 1]
        return ap.rearrange(f"p ({' '.join(names)}) -> p {' '.join(names)}", **dict(zip(names, shape[1:]))) if len(shape) > 2 else ap

    def mark(self):
        return self.used

    def release(self, mark):
        self.used = mark

    def mean(self, t):
        return self.mv[:, ds(t, 1), 0:1].rearrange("p a b -> p (a b)")

    def rstd_of(self, t):
        return self.rstd[:, ds(t, 1)]

    def norm_of(self, t):
        return self.norm[:, ds(t, 1)]


def row(ap):
    return ap.rearrange("(o n) -> o n", o=1).to_broadcast([P, ap.shape[0]])


def by_half(ap):
    return ap.rearrange("(k p) n -> p k n", p=P)


def load_and_index(nc, m, a, name="li", second=False):
    with ExitStack() as c:
        sem = stage_semaphores(nc, c)
        in_nat, in_const, in_x = sem(name + "in_nat"), sem(name + "in_const"), sem(name + "in_x")
        s_cleared, s_own, s_tr = sem(name + "cleared"), sem(name + "dve_own"), sem(name + "turned")
        s_b, s_f = sem(name + "diag_ready"), sem(name + "rows_ready")
        mark = m.mark()
        nat = m.take([P, 4, 4, P], I32)
        key = 2
        if second:
            both = m.take([P, 4, 2 * P], I32)
            nat, key = both.rearrange("p q (e k) -> p k q e", k=2), 0
        natf = m.take([P, 3, 4, P], F32)
        inv = m.take([P, TAB], F32)
        small = m.take([P, 64], F32)
        smalli = m.take([P, 16], I32)
        gb = m.take([P, TAB], F32)
        trn = m.take([P, 4, P], F32)
        tab = m.take([P, 3, 4], F32)
        diag = m.take([P, 3, 4, P])
        psT = [c.enter_context(nc.psum_tensor(f"{name}_t{k}", [P, TAB], F32)) for k in range(3)]
        psG = c.enter_context(nc.psum_tensor(name + "_g", [P, TAB], F32))
        psD = c.enter_context(nc.psum_tensor(name + "_d", [P, TAB], F32))
        sel = m.take([P, 4, TAB])
        psF = c.enter_context(nc.psum_tensor(name + "_f", [P, 1], F32))
        last_p = FULL - 3 * P
        with nc.Block() as block:
            @block.sync
            def _(sp):
                if second:
                    sp.wait_ge(s_cleared, 1)
                    flat = m.sorted_dram.rearrange("e k -> (e k)")
                    n3, line = 3 * P * P * 2, 2 * P
                    sp.dma_start(both[:, 0:3, :], flat[0:n3].rearrange("(q p e) -> p q e", p=P, e=line)).then_inc(in_nat, 16)
                    sp.dma_start(both[0:last_p, 3, :], flat[n3:FULL * line].rearrange("(p e) -> p e", e=line)).then_inc(in_nat, 16)
                    sp.dma_start(both[last_p:last_p + 1, 3, 0:2 * REST],
                                 flat[FULL * line:2 * E].rearrange("(o e) -> o e", o=1)).then_inc(in_nat, 16)
                    return
                sp.dma_start(m.ident[:, :], a["ident"]).then_inc(in_const, 16)
                sp.dma_start(m.pcol[:, :], a["pcol"]).then_inc(in_const, 16)
                sp.dma_start(m.valid[:, :], a["valid"]).then_inc(in_const, 16)
                sp.wait_ge(s_cleared, 2)
                for k, (src, off) in enumerate(((a["src"], 0), (a["edge_type_2"], 0), (a["dst"], 0), (a["dst"], 1))):
                    n3, nr = 3 * P * P, E - off
                    if off:
                        sp.dma_start(nat[:, k, 0:3, :], src[off:off + n3].rearrange("(q p e) -> p q e", p=P, e=P)).then_inc(in_nat, 16)
                        sp.dma_start(nat[0:last_p, k, 3, :], src[off + n3:off + FULL * P].rearrange("(p e) -> p e", e=P)).then_inc(in_nat, 16)
                    else:
                        sp.dma_start(nat[:, k, 0:3, :], src[0:n3].rearrange("(q p e) -> p q e", p=P, e=P)).then_inc(in_nat, 16)
                        sp.dma_start(nat[0:last_p, k, 3, :], src[n3:FULL * P].rearrange("(p e) -> p e", e=P)).then_inc(in_nat, 16)
                    rest = REST - off
                    sp.dma_start(nat[last_p:last_p + 1, k, 3, 0:rest],
                                 src[FULL * P + off:E].rearrange("(o e) -> o e", o=1)).then_inc(in_nat, 16)
                sp.wait_ge(s_cleared, 5)
                sp.dma_start(m.X[:, 0:TILES - 1, :], a["x"][0:(TILES - 1) * P, :].rearrange("(t p) d -> p t d", p=P)).then_inc(in_x, 16)
                sp.dma_start(m.X[0:LAST, TILES - 1, :], a["x"][(TILES - 1) * P:N, :]).then_inc(in_x, 16)
                sp.wait_ge(in_x, 32)

            @block.gpsimd
            def _(pool):
                if second:
                    pool.memset(both[:, :, :], PAD_DST).then_inc(s_cleared, 1)
                    return
                pool.memset(nat[:, 2:4, :, :], PAD_DST).then_inc(s_cleared, 1)
                pool.memset(nat[:, 0:2, :, :], 0).then_inc(s_cleared, 1)
                pool.iota(m.iota[:, :], [[1, NP]], base=0, channel_multiplier=0).then_inc(s_cleared, 1)
                pool.memset(m.ring[:, :, :], 0.0).then_inc(s_cleared, 1)
                pool.memset(m.X[:, TILES - 1, :], 0.0).then_inc(s_cleared, 1)
                pool.memset(m.zeros[:, :], 0.0).then_inc(s_cleared, 1)
                pool.memset(m.AGG[:, :, :], 0.0).then_inc(s_cleared, 1)

            @block.vector
            def _(v):
                own = Count(s_own)
                if second:
                    v.wait_ge(in_nat, 16 * 3)
                    own.inc(v.tensor_scalar(natf[:, 1, :, :], nat[:, 1, :, :], float(NP - 1), None, ALU.min))
                    own.inc(v.memset(inv[:, :], 0.0))
                else:
                    own.inc(v.memset(m.ones[:, :], 1.0))
                    own.inc(v.memset(m.eps[:, :], EPS))
                    own.wait(v)
                    v.wait_ge(in_nat, 16 * 12)
                    v.wait_ge(s_cleared, 3)
                    own.inc(v.tensor_copy(m.iotaf[:, :], m.iota[:, 0:P]))
                    v.wait_ge(in_const, 48)
                    own.inc(v.tensor_copy(natf[:, 0, :, :], nat[:, 1, :, :]))
                    own.inc(v.tensor_copy(natf[:, 1, :, :], nat[:, 0, :, :]))
                    own.inc(v.tensor_copy(inv[:, :].rearrange("p (q e) -> p q e", q=4), nat[:, 3, :, :]))
                own.inc(v.tensor_copy(natf[:, 2, :, :], nat[:, key, :, :]))
                own.inc(v.tensor_single_scalar(smalli[:, 0:4], nat[:, key, :, P - 1], 7, ALU.arith_shift_right))
                own.wait(v)
                own.inc(v.tensor_copy(small[:, 0:4], smalli[:, 0:4]))
                if not second:
                    own.inc(v.scalar_tensor_tensor(natf[:, 0, :, :], natf[:, 0, :, :], float(NP), natf[:, 1, :, :], ALU.mult, ALU.add))
                    own.inc(v.tensor_tensor(inv[:, :].rearrange("p (q e) -> p q e", q=4), natf[:, 2, :, :],
                                            inv[:, :].rearrange("p (q e) -> p q e", q=4), ALU.is_gt))
                own.wait(v)
                own.inc(v.tensor_tensor(small[:, 4:8], small[:, 0:4], m.pcol[:, :], ALU.add))
                own.inc(v.tensor_reduce(small[:, 8:9], inv[:, :], AX.X, ALU.add))
                own.wait(v)
                for q in range(4):
                    own.inc(v.tensor_scalar(trn[:, q, :], m.ident[:, :], small[:, 4 + q:5 + q], None, ALU.mult))
                own.wait(v)
                v.sem_inc(s_b, 1)
                v.wait_ge(s_tr, 3)
                if not second:
                    own.inc(v.tensor_copy(m.idx[:, 0, :], psT[0][:, :]))
                own.inc(v.tensor_copy(m.idx[:, 1, :], psT[1][:, :]))
                own.inc(v.tensor_copy(m.dstT[:, :], psT[2][:, :]))
                v.wait_ge(s_f, 1)
                own.inc(v.tensor_copy(gb[:, :], psG[:, :]))
                own.inc(v.tensor_scalar(small[:, 9:10], psF[:, :], 1.0, None, ALU.min))
                own.wait(v)
                own.inc(v.tensor_scalar(small[:, 10:11], small[:, 9:10], -1.0, 1.0, ALU.mult, ALU.add))
                own.inc(v.tensor_scalar(small[:, 12:16], m.pcol[:, :], float(CHUNKS), None, ALU.min))
                for q in range(4):
                    own.inc(v.tensor_scalar(inv[:, :], gb[:, :], m.pcol[:, q:q + 1], 0.0, ALU.is_lt, ALU.add,
                                            accum_out=small[:, 16 + q:17 + q]))
                    own.wait(v)
                own.inc(v.tensor_scalar(small[:, 20:24], small[:, 16:20], float(CHUNKS), small[:, 10:11], ALU.min, ALU.mult))
                own.inc(v.tensor_tensor(small[:, 24:28], m.pcol[:, :], small[:, 16:20], ALU.subtract))
                own.wait(v)
                own.inc(v.scalar_tensor_tensor(tab[:, 0, :], small[:, 12:16], small[:, 9:10], small[:, 20:24], ALU.mult, ALU.add))
                own.inc(v.tensor_scalar(small[:, 24:28], small[:, 24:28], small[:, 10:11], None, ALU.mult))
                own.wait(v)
                own.inc(v.tensor_scalar(tab[:, 1, :], small[:, 24:28], 0.0, float(TILES - 1), ALU.max, ALU.min))
                own.inc(v.tensor_scalar(tab[:, 2, :], m.pcol[:, :], 0.0, small[:, 9:10], ALU.mult, ALU.add))
                own.wait(v)
                for k in range(3):
                    for q in range(4):
                        own.inc(v.tensor_scalar(diag[:, k, q, :], m.ident[:, :], tab[:, k, q:q + 1], None, ALU.mult))
                own.wait(v)
                v.sem_inc(s_b, 1)
                v.wait_ge(s_f, 2)
                for k in range(3):
                    own.inc(v.tensor_copy(m.tab[0:1, k, :], psT[k][0:1, :]))
                own.wait(v)
                own.inc(v.tensor_single_scalar(m.tab[0:1, 3, :], m.tab[0:1, 0, :], RING - 1, ALU.bitwise_and))
                for q in range(4):
                    own.inc(v.tensor_scalar(sel[:, q, :], psT[0][:, :], m.pcol[:, q:q + 1], None, ALU.is_equal))
                own.inc(v.tensor_scalar(inv[:, :], psT[1][:, :], -float(P), None, ALU.mult))
                own.wait(v)
                v.sem_inc(s_b, 1)
                v.wait_ge(s_f, 3)
                own.inc(v.tensor_tensor(m.dloc[:, :], psD[:, :], inv[:, :], ALU.add))

            @block.tensor
            def _(pe):
                if not second:
                    pe.wait_ge(in_const, 48)
                pe.wait_ge(s_b, 1)
                if second:
                    pe.sem_inc(s_tr, 1)
                for k in range(1 if second else 0, 3):
                    for q in range(4):
                        last = pe.transpose(psT[k][:, q * P:(q + 1) * P], natf[:, k, q, :], m.ident[:, :])
                    last.then_inc(s_tr, 1)
                for q in range(4):
                    pe.matmul(psG[:, q * P:(q + 1) * P], m.ones[:, :], trn[:, q, :], start=True, stop=True)
                pe.matmul(psF[:, :], m.ones[:, :], small[:, 8:9], start=True, stop=True).then_inc(s_f, 1)
                pe.wait_ge(s_b, 2)
                for k in range(3):
                    for q in range(4):
                        last = pe.matmul(psT[k][:, q * P:(q + 1) * P], m.ones[:, :], diag[:, k, q, :], start=True, stop=True)
                last.then_inc(s_f, 1)
                pe.wait_ge(s_b, 3)
                for q in range(4):
                    last = pe.matmul(psD[:, :], natf[:, 2, q, :], sel[:, q, :], start=(q == 0), stop=(q == 3))
                last.then_inc(s_f, 1)

            @block.scalar
            def _(act):
                act.wait_ge(s_cleared, 1 if second else 7)
        m.release(mark)


def sort_by_source(nc, m):
    GROUP = 16
    with ExitStack() as c:
        sem = stage_semaphores(nc, c, "so")
        b_ready, t_done, t_ready, base_done, dg_ready, w_done, w_taken, pos_ready, deg_done, root = (
            sem(x) for x in ("_b", "_t", "_t_ready", "_base", "_dg", "_w", "_w_taken", "_pos", "_deg", "_root"))
        oh_ready, oh_used, dve_own, pool_own, woken = (sem(x) for x in ("_oh", "_oh_used", "_own", "_pool", "_woken"))
        scattered = [sem(f"_scattered{k}") for k in range(2)]
        mark = m.mark()
        take = m.take
        hot = m.big[:, 0:CHUNKS * TILES].rearrange("p (c r) -> p c r", r=TILES)
        diag = m.big[:, CHUNKS * TILES:CHUNKS * TILES + P * TILES].rearrange("p (c r) -> p c r", r=TILES)
        tile_f, low, tile_i = take([P, TAB]), take([P, TAB]), take([P, TAB], I32)
        place, place_i, pairs = take([P, TAB]), take([P, TAB], I32), take([P, TAB, 2], I32)
        before = take([P, P])
        counts, base = take([P, 4, TILES]), take([P, 4, TILES])
        lower, lower_sum = take([P, TILES, TILES]), take([P, TILES])
        prod = take([P, 2, GROUP * TILES])
        send = take([P, 2 * STEP, 2], I32)
        ps = lambda x: c.enter_context(nc.psum_tensor("so" + x, [P, 512], F32))
        psW, psT, psB, psN = [ps(f"_w{k}") for k in range(4)], ps("_t"), ps("_b"), ps("_n")
        blocks = [(q, min(P, CHUNKS - q * P)) for q in range(4)]
        groups = [(q, c0, min(GROUP, q * P + nq - c0)) for q, nq in blocks for c0 in range(q * P, q * P + nq, GROUP)]
        over_r = lambda ap, n: ap.unsqueeze(2).to_broadcast([P, n, TILES])
        over_c = lambda ap, n: ap.unsqueeze(1).to_broadcast([P, n, TILES])
        with nc.Block() as block:
            @block.vector
            def _(v):
                own = Count(dve_own)
                src = m.idx[:, 1, :]
                own.inc(v.tensor_single_scalar(tile_i[:, :], src, 7, ALU.arith_shift_right))
                own.inc(v.tensor_copy(low[:, :], src))
                own.inc(v.tensor_copy(pairs[:, :, 0:1].rearrange("p c o -> p (c o)"), src))
                own.inc(v.tensor_copy(pairs[:, :, 1:2].rearrange("p c o -> p (c o)"), m.dstT[:, :]))
                own.inc(v.tensor_scalar(before[:, :], m.iotaf[:, :], m.pcol[:, 0:1], None, ALU.is_gt))
                own.inc(v.tensor_scalar(place[:, :], m.dstT[:, :], float(PAD_DST), 64.0, ALU.is_equal, ALU.mult))
                own.inc(v.memset(counts[:, :, :], 0.0))
                own.wait(v)
                own.inc(v.tensor_copy(tile_f[:, :], tile_i[:, :]))
                own.wait(v)
                own.inc(v.scalar_tensor_tensor(low[:, :], tile_f[:, :], -float(P), low[:, :], ALU.mult, ALU.add))
                own.inc(v.tensor_tensor(tile_f[:, :], tile_f[:, :], place[:, :], ALU.add))
                own.wait(v)
                for q, nq in blocks:
                    v.tensor_tensor(hot[:, q * P:q * P + nq, :], over_r(tile_f[:, q * P:q * P + nq], nq),
                                    over_c(m.iotaf[:, 0:TILES], nq), ALU.is_equal).then_inc(b_ready, 1)
                v.wait_ge(t_done, 1)
                for q, nq in blocks:
                    own.inc(v.tensor_copy(counts[0:nq, q, :], psT[0:nq, q * TILES:(q + 1) * TILES]))
                own.inc(v.tensor_tensor(lower[:, :, :], over_r(m.iotaf[:, 0:TILES], TILES), over_c(m.iotaf[:, 0:TILES], TILES), ALU.is_gt))
                own.wait(v)
                v.sem_inc(t_ready, 1)
                v.wait_ge(base_done, 1)
                own.inc(v.tensor_tensor(lower[:, :, :], lower[:, :, :], over_c(psB[:, 4 * TILES:5 * TILES], TILES), ALU.mult))
                own.wait(v)
                own.inc(v.tensor_reduce(lower_sum[:, :], lower[:, :, :], AX.X, ALU.add))
                own.wait(v)
                own.inc(v.tensor_tensor(base[:, :, :], psB[:, 0:4 * TILES].rearrange("p (q r) -> p q r", q=4), over_c(lower_sum[:, :], 4), ALU.add))
                own.wait(v)
                g = 0
                for q, nq in blocks:
                    if g:
                        v.wait_ge(w_done, g)
                    v.tensor_tensor(diag[:, 0:nq, :], over_r(m.ident[:, 0:nq], nq), over_c(base[:, q, :], nq), ALU.mult).then_inc(dg_ready, 1)
                    for _, c0, n in [x for x in groups if x[0] == q]:
                        v.wait_ge(w_done, g + 1)
                        pr = prod[:, g % 2, 0:n * TILES].rearrange("p (c r) -> p c r", r=TILES)
                        v.tensor_tensor(pr, hot[:, c0:c0 + n, :], psW[g % 4][:, 0:n * TILES].rearrange("p (c r) -> p c r", r=TILES),
                                        ALU.mult).then_inc(w_taken, 1)
                        v.wait_ge(w_taken, g + 5)
                        own.inc(v.tensor_reduce(place[:, c0:c0 + n], pr, AX.X, ALU.add))
                        g += 1
                own.wait(v)
                v.tensor_copy(place_i[:, 0:CHUNKS], place[:, 0:CHUNKS]).then_inc(pos_ready, 1)
                for g in range((CHUNKS + 3) // 4):
                    n = min(4, CHUNKS - 4 * g)
                    v.wait_ge(oh_used, g + 1)
                    v.tensor_tensor(m.oh[:, 4 * (g % 2):4 * (g % 2) + n, :], m.iotaf[:, :].unsqueeze(1).to_broadcast([P, n, P]),
                                    low[:, 4 * g:4 * g + n].unsqueeze(2).to_broadcast([P, n, P]), ALU.is_equal).then_inc(oh_ready, 1)
                v.wait_ge(root, 1)
                v.reciprocal(m.norm[:, :], m.norm[:, :])

            @block.tensor
            def _(pe):
                pe.sem_inc(w_taken, 4)
                pe.sem_inc(oh_used, 2)
                for q, nq in blocks:
                    pe.wait_ge(b_ready, q + 1)
                    for r in range(TILES):
                        last = pe.matmul(psT[0:nq, q * TILES + r:q * TILES + r + 1], hot[:, q * P:q * P + nq, r:r + 1].rearrange("p c o -> p (c o)"),
                                         m.ones[:, 0:1], start=True, stop=True)
                last.then_inc(t_done, 1)
                pe.wait_ge(t_ready, 1)
                for q in range(4):
                    for k in range(q + 1):
                        pe.matmul(psB[:, q * TILES:(q + 1) * TILES], m.ones[:, :] if k < q else before[:, :], counts[:, k, :], start=(k == 0), stop=(k == q))
                for k in range(4):
                    last = pe.matmul(psB[:, 4 * TILES:5 * TILES], m.ones[:, :], counts[:, k, :], start=(k == 0), stop=(k == 3))
                last.then_inc(base_done, 1)
                for g, (q, c0, n) in enumerate(groups):
                    pe.wait_ge(dg_ready, q + 1)
                    pe.wait_ge(w_taken, g + 1)
                    rows = lambda ap: ap.rearrange("p c r -> p (c r)")
                    pe.matmul(psW[g % 4][:, 0:n * TILES], before[:, :], rows(hot[:, c0:c0 + n, :]), start=True, stop=False)
                    pe.matmul(psW[g % 4][:, 0:n * TILES], m.ones[:, :], rows(diag[:, c0 - q * P:c0 - q * P + n, :]), start=False, stop=True).then_inc(w_done, 1)
                for ch in range(CHUNKS):
                    if ch % 4 == 0:
                        pe.wait_ge(oh_ready, ch // 4 + 1)
                    last = pe.matmul(psN[:, 0:TILES], m.oh[:, ch % 8, :], hot[:, ch, :], start=(ch == 0), stop=(ch == CHUNKS - 1))
                    if ch % 4 == 3:
                        last.then_inc(oh_used, 1)
                last.then_inc(deg_done, 1)

            @block.scalar
            def _(act):
                act.wait_ge(deg_done, 1)
                act.activation(m.norm[:, :], psN[:, 0:TILES], ACT.Sqrt, bias=m.ones[:, 0:1]).then_inc(root, 1)

            @block.gpsimd
            def _(pool):
                own = Count(pool_own)
                pool.wait_ge(pos_ready, 1)

                def half(c0, k, n, turn):
                    if turn is not None:
                        pool.wait_ge(scattered[k], turn * (16 * STEP))
                        pool.sem_inc(woken, 1)
                    own.inc(pool.tensor_copy(m.ir[:, k * STEP:k * STEP + n], place_i[:, ds(c0, n)]))
                    own.inc(pool.tensor_copy(send[:, k * STEP:k * STEP + n, :], pairs[:, ds(c0, n), :]))
                    own.wait(pool)
                    pool.sem_inc(woken, 1)
                    for j in range(n):
                        rows = REST if isinstance(c0, int) and c0 + j == CHUNKS - 1 and REST else P
                        pool.indirect_dma_start(m.sorted_dram, bass.IndirectOffsetOnAxis(ap=m.ir[0:rows, k * STEP + j:k * STEP + j + 1], axis=0),
                                                send[0:rows, k * STEP + j, :], None).then_inc(scattered[k], 16)
                half(0, 0, STEP, None)
                half(STEP, 1, STEP, None)
                with turns(pool, 1, CHUNKS // RING, [(own, 4)]) as i:
                    half(i * RING, 0, STEP, i)
                    half(i * RING + STEP, 1, STEP, i)
                half(CHUNKS // RING * RING, 0, CHUNKS % RING, CHUNKS // RING)
                pool.wait_ge(scattered[0], 16 * (STEP * (CHUNKS // RING) + CHUNKS % RING))
                pool.wait_ge(scattered[1], 16 * STEP * (CHUNKS // RING))
        m.release(mark)


def stats(nc, m, source, name):
    with ExitStack() as c:
        s_own, s_var, s_sq, s_woken = map(stage_semaphores(nc, c, name), ("_own", "_var", "_sqrt", "_woken"))
        with nc.Block() as block:
            @block.vector
            def _(v):
                own = Count(s_own)

                def group(t0, n):
                    for j in range(n):
                        own.inc(v.bn_stats(m.bn[:, j, :], tile_of(source, t0 + j)))
                    own.wait(v)
                    v.sem_inc(s_woken, 1)
                    for j in range(n):
                        own.inc(v.bn_aggr(m.mv4[:, j, :], m.bn[:, j, :]))
                    own.wait(v)
                    own.inc(v.tensor_copy(m.mv[:, ds(t0, n), :], m.mv4[:, 0:n, :]))
                with turns(v, 0, TILES // 5, [(own, 11)]) as i:
                    group(i * 5, 5)
                own.wait(v)
                v.sem_inc(s_var, 1)
                v.wait_ge(s_sq, 1)
                v.reciprocal(m.rstd[:, :], m.std[:, :])

            @block.scalar
            def _(act):
                act.wait_ge(s_var, 1)
                act.activation(m.std[:, :], m.mv[:, :, 1], ACT.Sqrt, bias=m.eps[:, 0:1]).then_inc(s_sq, 1)


def tile_of(buf, t, cols=D):
    return buf[:, ds(t, 1), 0:cols].rearrange("p o d -> p (o d)")


def is_last(t):
    return isinstance(t, int) and t == TILES - 1


def project(nc, m, name, layer_no, kind, weights, vector=None):
    cols = D * len(weights)
    gcn, layer = kind == "gcn", kind == "layer"
    with ExitStack() as c:
        sem = stage_semaphores(nc, c, name)
        w_in, dve_own, h_ready, h_free = sem("_w_in"), sem("_dve"), sem("_h_ready"), sem("_h_free")
        xt_done, prod_done, st_done = sem("_xt_done"), sem("_prod_done"), sem("_st_done")
        st_out = [sem(f"_st_out{j}") for j in range(4)]
        xt_out = [sem(f"_xt_out{j}") for j in range(4)]
        mark = m.mark()
        w = m.take([P, 2, cols])
        vec = m.take([P, D]) if vector is not None else None
        h = m.take([P, 2, D])
        tmp = m.take([P, 2, D])
        xt = m.take([P, 4, D])
        stage = None if gcn else m.take([P, 4, cols])
        psT = [c.enter_context(nc.psum_tensor(f"{name}_t{k}", [P, 512], F32)) for k in range(2)]
        psW = [c.enter_context(nc.psum_tensor(f"{name}_w{k}", [P, 512], F32)) for k in range(2)]
        n_in = 16 * (len(weights) + (vector is not None))
        with nc.Block() as block:
            @block.sync
            def _(sp):
                for k, wk in enumerate(weights):
                    sp.dma_start(w[:, :, k * D:(k + 1) * D], by_half(wk)).then_inc(w_in, 16)
                if vector is not None:
                    sp.dma_start(vec[:, :], row(vector)).then_inc(w_in, 16)

                def body(t, j):
                    sp.wait_ge(xt_done, t + 3)
                    sp.sem_inc(m.woken_sp, 1)
                    sp.dma_start(m.xt_dram[layer_no, ds(t, 1), :, :].rearrange("o p d -> (o p) d"), xt[:, j, :]).then_inc(xt_out[j], 16)
                    sp.wait_ge(st_done, t + 3)
                    sp.sem_inc(m.woken_sp, 1)
                    if gcn:
                        sp.dma_start(m.t_dram[0, ds(t, 1), :, :].rearrange("o p d -> (o p) d"), tile_of(m.AGG, t)).then_inc(st_out[j], 16)
                    else:
                        sp.dma_start(m.t_dram[:, ds(t, 1), :, :].rearrange("r o p d -> p (r o) d"),
                                     stage[:, j, :].rearrange("p (r d) -> p r d", r=2)).then_inc(st_out[j], 16)
                tiles4(sp, body)
                for j in range(4):
                    sp.wait_ge(xt_out[j], 16 * (TURNS // 4 + (j == 0) + 1))
                    sp.wait_ge(st_out[j], 16 * (TURNS // 4 + (j == 0) + 1))

            @block.vector
            def _(v):
                own = Count(dve_own)
                v.wait_ge(w_in, n_in)
                if gcn:
                    v.sem_inc(st_done, 2)

                def make_h(t, j):
                    src = tile_of(m.AGG if layer else m.X, t)
                    v.wait_ge(h_free, t + 1)
                    if layer:
                        own.inc(v.tensor_scalar(tmp[:, 0, :], src, m.mean(t), m.rstd_of(t), ALU.subtract, ALU.mult))
                        own.wait(v)
                        own.inc(v.tensor_tensor(tmp[:, 1, :], tmp[:, 0, :], vec[:, :], ALU.mult))
                        v.tensor_copy(tile_of(m.AGG, t), m.zeros[:, 0:D])
                        own.wait(v)
                        v.tensor_tensor(h[:, j % 2, :], tmp[:, 1, :], tile_of(m.L, t), ALU.add).then_inc(h_ready, 1)
                    else:
                        v.tensor_scalar(h[:, j % 2, :], src, m.mean(t), m.rstd_of(t), ALU.subtract, ALU.mult).then_inc(h_ready, 1)

                def scale_rows(t, j):
                    if not is_last(t):
                        make_h(t + 1, (j + 1) % 4)
                    v.wait_ge(prod_done, t + 1)
                    own.inc(v.tensor_tensor(tmp[:, j % 2, :], psW[j % 2][:, 0:D], vec[:, :], ALU.add))
                    own.wait(v)
                    v.tensor_scalar(tile_of(m.AGG, t), tmp[:, j % 2, :], m.norm_of(t), None, ALU.mult).then_inc(st_done, 1)

                if gcn:
                    make_h(0, 0)
                    tiles4(v, scale_rows, [(own, 1)])
                else:
                    tiles4(v, make_h, [(own, 2)] if layer else [])

            @block.tensor
            def _(pe):
                pe.sem_inc(h_free, 2)
                pe.wait_ge(w_in, n_in)

                def transposes(t, j):
                    pe.wait_ge(h_ready, t + 1)
                    pe.wait_ge(xt_done, t + 1)
                    for k in range(2):
                        last = pe.transpose(psT[j % 2][:, k * P:(k + 1) * P], h[:, j % 2, k * P:(k + 1) * P], m.ident[:, :])
                    last.then_inc(h_free, 1)

                def product(t, j):
                    if not is_last(t):
                        transposes(t + 1, (j + 1) % 4)
                    pe.wait_ge(xt_done, t + 3)
                    pe.wait_ge(st_done, t + 1)
                    for k in range(2):
                        last = pe.matmul(psW[j % 2][:, 0:cols], xt[:, j, k * P:(k + 1) * P], w[:, k, :], start=(k == 0), stop=(k == 1))
                    last.then_inc(prod_done, 1)
                transposes(0, 0)
                tiles4(pe, product)

            @block.scalar
            def _(act):
                act.sem_inc(xt_done, 2)
                if not gcn:
                    act.sem_inc(st_done, 2)
                for j in range(4):
                    act.sem_inc(xt_out[j], 16)
                    act.sem_inc(st_out[j], 16)

                def copy_xt(t, j):
                    act.wait_ge(h_free, t + 3)
                    act.wait_ge(xt_out[j], 16 * (t // 4 + 1) if isinstance(t, int) else (t - j) * 4 + 16)
                    act.activation(xt[:, j, :], psT[j % 2][:, 0:D], ACT.Relu if layer else ACT.Copy).then_inc(xt_done, 1)

                def copy_rows(t, j):
                    if not is_last(t):
                        copy_xt(t + 1, (j + 1) % 4)
                    if not gcn:
                        act.wait_ge(prod_done, t + 1)
                        act.wait_ge(st_out[j], 16 * (t // 4 + 1) if isinstance(t, int) else (t - j) * 4 + 16)
                        act.activation(stage[:, j, :], psW[j % 2][:, :], ACT.Copy).then_inc(st_done, 1)
                    else:
                        act.wait_ge(prod_done, t + 1)
                copy_xt(0, 0)
                tiles4(act, copy_rows)
        m.release(mark)


def gather_sum(nc, m, name, src_col, side, general=True):
    width = D
    gathered = m.gathered
    with ExitStack() as c:
        sem = stage_semaphores(nc, c, name)
        oh_ready, mm_done, agg_done = sem("_oh_ready"), sem("_mm_done"), sem("_agg_done")
        pool_own, woken = sem("_pool"), sem("_woken")
        g_idx, g_in, g_oh, g_mm, g_add = (sem(x) for x in ("_g_idx", "_g_in", "_g_oh", "_g_mm", "_g_add"))
        mark = m.mark()
        pp = [c.enter_context(nc.psum_tensor(f"{name}_pair{k}", [P, 512], F32))[:, 0:width] for k in range(2)]
        side = side(nc, m, name, c)
        rows = m.t_dram.rearrange("r t p d -> (r t p) d")
        base = [m.gather_count[j] for j in range(STEP)]
        for j in range(STEP):
            m.gather_count[j] += 16 * (CHUNKS // STEP + (j < CHUNKS % STEP))
        with nc.Block() as block:
            @block.gpsimd
            def _(pool):
                own = Count(pool_own)

                def half(c0, k, n):
                    pool.wait_ge(mm_done, c0 + 1)
                    pool.sem_inc(woken, 1)
                    own.inc(pool.tensor_copy(m.ir[:, k * STEP:(k + 1) * STEP], m.idx[:, src_col, ds(c0, STEP)]))
                    own.wait(pool)
                    for j in range(n):
                        pool.wait_ge(mm_done, c0 + j + 1)
                        pool.sem_inc(woken, 1)
                        pool.indirect_dma_start(m.ring[:, k * STEP + j, 0:D], None, rows,
                                                bass.IndirectOffsetOnAxis(ap=m.ir[:, k * STEP + j:k * STEP + j + 1], axis=0)
                                                ).then_inc(gathered[j], 16)
                with turns(pool, 0, CHUNKS // RING, [(own, 2)]) as i:
                    half(i * RING, 0, STEP)
                    half(i * RING + STEP, 1, STEP)
                half(CHUNKS // RING * RING, 0, CHUNKS % RING)

                if general:
                    unsorted = pool.value_load(m.tab[0:1, 2, 0:1], min_val=0, max_val=1)
                    with pool.If(unsorted > 0):
                        pool.wait_ge(g_add, 1)
                        with pool.Fori(0, TILES - 1) as r:
                            with pool.Fori(0, CHUNKS) as ch:
                                done = r * CHUNKS + ch
                                pool.wait_ge(g_mm, done + 1)
                                pool.sem_inc(woken, 1)
                                pool.tensor_copy(m.ir[:, 0:1], m.idx[:, src_col, ds(ch, 1)]).then_inc(g_idx, 1)
                                pool.wait_ge(g_idx, done + 1)
                                pool.sem_inc(woken, 1)
                                pool.indirect_dma_start(m.ring[:, 0, 0:D], None, rows,
                                                        bass.IndirectOffsetOnAxis(ap=m.ir[:, 0:1], axis=0)).then_inc(g_in, 16)

            @block.vector
            def _(v):
                v.sem_inc(agg_done, 2)

                def one_hots(p, g):
                    v.tensor_tensor(m.oh[:, 4 * (g % 2):4 * (g % 2) + 4, :], m.iotaf[:, :].unsqueeze(1).to_broadcast([P, 4, P]),
                                    m.dloc[:, ds(p, 4)].unsqueeze(2).to_broadcast([P, 4, P]), ALU.is_equal).then_inc(oh_ready, 1)

                def add(p, j, t):
                    v.wait_ge(mm_done, p + 9)
                    v.wait_ge(agg_done, p + 2)
                    v.tensor_tensor(tile_of(m.AGG, t, width), tile_of(m.AGG, t, width), pp[j % 2], ALU.add).then_inc(agg_done, 1)

                def pairs(i, n):
                    p = i * STEP
                    tiles = load_row(nc, v, m.tab[0:1, 1, ds(p, STEP)], TILES - 1)
                    for j in range(n):
                        if j % 4 == 0 and (not isinstance(i, int) or p + j + 4 < PAIRS):
                            one_hots(p + j + 4, j // 4 + 1)
                        add(p + j, j, tiles[j])
                        if side and not (isinstance(i, int) and i > TURNS):
                            side.vector(v, i, j)
                one_hots(0, 0)
                if side:
                    side.before_vector(v)
                with turns(v, 0, TURNS, side.vector_counts if side else []) as i:
                    pairs(i, STEP)
                pairs(TURNS, STEP)
                pairs(TURNS + 1, TAIL - STEP)
                if side:
                    side.after_vector(v)
                v.wait_ge(agg_done, PAIRS + 2)

                if general:
                    unsorted = v.value_load(m.tab[0:1, 2, 0:1], min_val=0, max_val=1)
                    with v.If(unsorted > 0):
                        v.sem_inc(g_add, 1)
                        with v.Fori(0, TILES - 1) as r:
                            with v.Fori(0, CHUNKS) as ch:
                                done = r * CHUNKS + ch
                                v.wait_ge(g_mm, done + 1)
                                v.tensor_scalar(m.oh[:, 0, :], m.iota[:, ds(r * P + P, P)], m.dstT[:, ds(ch, 1)], None,
                                                ALU.is_equal).then_inc(g_oh, 1)
                                v.wait_ge(g_mm, done + 2)
                                v.wait_ge(g_add, done + 1)
                                v.tensor_tensor(tile_of(m.AGG, r + 1, width), tile_of(m.AGG, r + 1, width), pp[0], ALU.add).then_inc(g_add, 1)

            @block.tensor
            def _(pe):
                pe.sem_inc(mm_done, 8)

                def pair(p, i, j, slot):
                    if j % 4 == 0:
                        pe.wait_ge(oh_ready, i * (STEP // 4) + j // 4 + 1)
                    if not isinstance(p, int) or p < CHUNKS:
                        pe.wait_ge(gathered[j % STEP], base[j % STEP] + 16 * (i + j // STEP + 1))
                    pe.wait_ge(agg_done, p + 1)
                    pe.matmul(pp[j % 2], m.oh[:, j % 8, :], m.ring[:, ds(slot, 1), 0:width].rearrange("p o d -> p (o d)"),
                              start=True, stop=True).then_inc(mm_done, 1)

                if side:
                    side.before_tensor(pe)
                with turns(pe, 0, TURNS, []) as i:
                    slots = load_row(nc, pe, m.tab[0:1, 3, ds(i * STEP, STEP)], RING - 1)
                    for j in range(STEP):
                        pair(i * STEP + j, i, j, slots[j])
                        if side:
                            side.tensor(pe, i, j)
                for j in range(TAIL):
                    if j % STEP == 0:
                        slots = load_row(nc, pe, m.tab[0:1, 3, ds(TURNS * STEP + j, STEP)], RING - 1)
                    pair(TURNS * STEP + j, TURNS, j, slots[j % STEP])
                    if side and j < STEP:
                        side.tensor(pe, TURNS, j)
                if side:
                    side.after_tensor(pe)

                if general:
                    unsorted = pe.value_load(m.tab[0:1, 2, 0:1], min_val=0, max_val=1)
                    with pe.If(unsorted > 0):
                        pe.sem_inc(g_mm, 1)
                        with pe.Fori(0, TILES - 1) as r:
                            with pe.Fori(0, CHUNKS) as ch:
                                done = r * CHUNKS + ch
                                pe.wait_ge(g_oh, done + 1)
                                pe.wait_ge(g_in, 16 * done + 16)
                                pe.wait_ge(g_add, done + 1)
                                pe.matmul(pp[0], m.oh[:, 0, :], m.ring[:, 0, 0:width], start=True, stop=True).then_inc(g_mm, 1)

            if side:
                @block.scalar
                def _(act):
                    side.before_scalar(act)
                    with turns(act, 0, TURNS, side.scalar_counts) as i:
                        for j in range(STEP):
                            side.scalar(act, i, j)
                    for j in range(STEP):
                        side.scalar(act, TURNS, j)

                @block.sync
                def _(sp):
                    side.before_sync(sp)
                    with sp.Fori(0, TURNS) as i:
                        side.sync(sp, i)
                    side.sync(sp, TURNS)
        m.release(mark)


def load_row(nc, eng, ap, top):
    return nc.values_load_multi_w_load_instructions(ap, engines=(eng.engine,), min_val=0, max_val=top,
                                                      skip_runtime_bounds_check_because="the tables hold clipped values")[1]


def one_row(ap):
    return ap.rearrange("(o n) -> o n", o=1)


class Side:
    vector_counts, scalar_counts = (), ()

    def __init__(self, *parts):
        self.parts = parts
        self.vector_counts = [x for p in parts for x in p.vector_counts]
        self.scalar_counts = [x for p in parts for x in p.scalar_counts]

    def before_sync(self, sp):
        for p in self.parts:
            p.before_sync(sp)

    def sync(self, sp, i):
        for p in self.parts:
            p.sync(sp, i)

    def before_tensor(self, pe):
        for p in self.parts:
            p.before_tensor(pe)

    def tensor(self, pe, i, j):
        for p in self.parts:
            p.tensor(pe, i, j)

    def after_tensor(self, pe):
        for p in self.parts:
            p.after_tensor(pe)

    def before_vector(self, v):
        for p in self.parts:
            p.before_vector(v)

    def vector(self, v, i, j):
        for p in self.parts:
            p.vector(v, i, j)

    def after_vector(self, v):
        for p in self.parts:
            p.after_vector(v)

    def before_scalar(self, act):
        for p in self.parts:
            p.before_scalar(act)

    def scalar(self, act, i, j):
        for p in self.parts:
            p.scalar(act, i, j)


class LoopPart(Side):
    AT = 6

    def __init__(self, nc, m, name, c, layer, loop_w, beta, bias, bank, bank_taken=None):
        super().__init__()
        sem = stage_semaphores(nc, c, name)
        self.m, self.layer, self.loop_w, self.beta, self.bias, self.bank, self.bank_taken = m, layer, loop_w, beta, bias, bank, bank_taken
        self.w_in, self.tile_in, self.tile_used = sem("_lw_in"), sem("_lt_in"), sem("_lt_used")
        self.l_ready, self.l_copied = sem("_l_ready"), sem("_l_copied")
        self.w, self.xt, self.bb = m.take([P, 2, D]), m.take([P, D]), m.take([P, 2, D])

    def before_sync(self, sp):
        sp.dma_start(self.w[:, :, :], by_half(self.loop_w)).then_inc(self.w_in, 16)
        sp.dma_start(self.bb[0:1, 0, :], one_row(self.beta)).then_inc(self.w_in, 16)
        sp.dma_start(self.bb[0:1, 1, :], one_row(self.bias)).then_inc(self.w_in, 16)

    def sync(self, sp, i):
        sp.wait_ge(self.tile_used, i + 1)
        sp.sem_inc(self.m.woken_sp, 1)
        sp.dma_start(self.xt[:, :], self.m.xt_dram[self.layer, ds(i, 1), :, :].rearrange("o p d -> (o p) d")).then_inc(self.tile_in, 16)

    def before_tensor(self, pe):
        pe.wait_ge(self.w_in, 48)

    def tensor(self, pe, i, j):
        if j == self.AT:
            pe.wait_ge(self.tile_in, 16 * (i + 1))
            if self.bank_taken:
                sem, per, first = self.bank_taken
                pe.wait_ge(sem, i * per + first)
            else:
                pe.wait_ge(self.l_copied, i + 1)
            for k in range(2):
                pe.matmul(self.bank[:, 0:D], self.xt[:, k * P:(k + 1) * P], self.w[:, k, :], start=(k == 0), stop=False)
            for k in range(2):
                last = pe.matmul(self.bank[:, 0:D], self.m.ones[0:1, :], self.bb[0:1, k, :], start=False, stop=(k == 1))
            last.then_inc(self.l_ready, 1)

    def after_tensor(self, pe):
        pass

    before_vector = after_vector = lambda self, v: None

    def vector(self, v, i, j):
        pass

    def before_scalar(self, act):
        act.sem_inc(self.tile_used, 1)
        act.sem_inc(self.l_copied, 1)

    def scalar(self, act, i, j):
        if j == self.AT:
            act.wait_ge(self.l_ready, i + 1)
            act.sem_inc(self.tile_used, 1)
            act.activation(tile_of(self.m.L, i), self.bank[:, 0:D], ACT.Copy).then_inc(self.l_copied, 1)


HEADS, HD = 8, 32
DIST = HD // 2 + 1
FEAT = (DIST + 1) * HD
BLOCKS = HEADS * FEAT // P
VW = HD + 1
WIN = 2 * VW
PER_BANK = 512 // WIN
HSCALE = float(HD) ** 0.25
MIX_A, MIX_B, MIX_C = 0.5, 1.0, 1.0


def window(b):
    return min(b * P // FEAT, HEADS - 2)


def blocks_of(h):
    return [b for b in range(BLOCKS) if (b * P + P - 1) // FEAT == h]


def map_coefficients(np):
    co = np.zeros((P, BLOCKS, WIN), np.float32)
    for b in range(BLOCKS):
        for p in range(P):
            h, f = divmod(b * P + p, FEAT)
            d = f // HD
            if d == DIST:
                x = MIX_B * HSCALE ** 2
            else:
                x = MIX_A * (2.0 if 0 < d < HD // 2 else 1.0)
            at = (h - window(b)) * VW
            co[p, b, at:at + VW] = x
    return co.reshape(P, BLOCKS * WIN)


def make_map(v, own, m, ext, phi, h):
    e = ext[:, h, :]
    window_ap = bass.AP(e.tensor, e.offset, [list(e.ap[0]), [1, DIST], [1, HD]])
    base = e[:, 0:HD].unsqueeze(1).to_broadcast([P, DIST, HD])
    out = phi[:, h * FEAT:h * FEAT + DIST * HD].rearrange("p (d i) -> p d i", d=DIST)
    v.tensor_tensor(out, base, window_ap, ALU.mult)
    return v.tensor_copy(phi[:, h * FEAT + DIST * HD:(h + 1) * FEAT], e[:, 0:HD])


class MixKeys(Side):

    def __init__(self, nc, m, name, c, a, bank, loop):
        super().__init__()
        sem = stage_semaphores(nc, c, name)
        self.m, self.a, self.bank, self.loop = m, a, bank, loop
        self.w_in, self.coef_in = sem("_kw_in"), sem("_coef_in")
        self.kv_ready, self.kv_taken, self.phi_ready, self.phi_used = sem("_kv_ready"), sem("_kv_taken"), sem("_phi_ready"), sem("_phi_used")
        self.k_taken, self.sq_ready, self.ss_ready, self.n_ready, self.v_ready = sem("_k_taken"), sem("_sq_ready"), sem("_ss_ready"), sem("_n_ready"), sem("_v_ready")
        self.tail_ready, self.tail_taken, self.sums_ready = sem("_tail_ready"), sem("_tail_taken"), sem("_sums_ready")
        self.own, self.cleared = Count(sem("_k_own")), sem("_cleared")
        self.vector_counts = [(self.own, 7)]
        self.w = m.take([P, 2, 2 * D])
        self.b = m.take([P, 2 * D])
        self.kb, self.sq, self.vb = m.take([P, D]), m.take([P, D]), m.take([P, D])
        self.ss, self.n, self.r = m.take([P, HEADS]), m.take([P, HEADS]), m.take([P, HEADS])
        self.ext = m.take([P, HEADS, 48])
        self.v1 = m.take([P, HEADS * VW])
        self.phi = m.take([P, HEADS * FEAT])
        self.sums = [c.enter_context(nc.psum_tensor(f"{name}_sum{k}", [P, 512], F32)) for k in range(BLOCKS // PER_BANK)]

    def before_sync(self, sp):
        sp.dma_start(self.w[:, :, :], by_half(self.a["L0_mix_Wqkv"][:, D:3 * D])).then_inc(self.w_in, 16)
        sp.dma_start(self.b[:, :], row(self.a["L0_mix_bqkv"][D:3 * D])).then_inc(self.w_in, 16)
        sp.dma_start(self.m.kvs[:, :], self.a["coef"]).then_inc(self.coef_in, 16)
        sp.wait_ge(self.coef_in, 16)

    def sync(self, sp, i):
        pass

    def before_tensor(self, pe):
        pe.wait_ge(self.w_in, 32)
        for s in self.sums:
            pe.matmul(s[:, 0:PER_BANK * WIN], self.m.zeros[:, 0:P], self.w[:, 0, 0:PER_BANK * WIN], start=True, stop=False, skip_group_check=True)

    def tensor(self, pe, i, j):
        xt, bank, m = self.loop.xt, self.bank, self.m
        if j == 0:
            pe.wait_ge(self.loop.tile_in, 16 * (i + 1))
            pe.wait_ge(self.tail_taken, i + 1)
        if j in (0, 2):
            half = j // 2
            if half:
                pe.wait_ge(self.kv_taken, 2 * i + 1)
            for k in range(2):
                last = pe.matmul(bank[:, 0:D], xt[:, k * P:(k + 1) * P], self.w[:, k, half * D:(half + 1) * D], start=(k == 0), stop=(k == 1))
            last.then_inc(self.kv_ready, 1)
        h = j - 7
        if 0 <= h < HEADS:
            pe.wait_ge(self.phi_ready, i * HEADS + h + 1)
            for b in blocks_of(h):
                if b < PER_BANK * len(self.sums):
                    at = (b % PER_BANK) * WIN
                    w = window(b) * VW
                    pe.matmul(self.sums[b // PER_BANK][:, at:at + WIN], self.phi[:, b * P:(b + 1) * P], self.v1[:, w:w + WIN],
                              start=False, stop=False, skip_group_check=True)
        if h == HEADS - 1:
            pe.wait_ge(self.loop.l_copied, i + 2)
            pe.matmul(bank[:, 0:HEADS * VW], m.ones[:, :], self.v1[:, :], start=True, stop=True, skip_group_check=True)
            w = window(BLOCKS - 1) * VW
            pe.matmul(bank[:, HEADS * VW:HEADS * VW + WIN], self.phi[:, (BLOCKS - 1) * P:BLOCKS * P], self.v1[:, w:w + WIN],
                      start=True, stop=True, skip_group_check=True).then_inc(self.tail_ready, 1)

    def after_tensor(self, pe):
        for s in self.sums:
            last = pe.matmul(s[:, 0:PER_BANK * WIN], self.m.zeros[:, 0:P], self.w[:, 0, 0:PER_BANK * WIN], start=False, stop=True, skip_group_check=True)
        last.then_inc(self.sums_ready, 1)

    def before_vector(self, v):
        v.sem_inc(self.tail_taken, 1)
        v.wait_ge(self.w_in, 32)
        v.memset(self.m.kvtail[:, :], 0.0).then_inc(self.cleared, 1)
        v.wait_ge(self.cleared, 1)

    def vector(self, v, i, j):
        own, m = self.own, self.m
        if j == 1:
            v.wait_ge(self.kv_ready, 2 * i + 1)
            v.tensor_tensor(self.kb[:, :], self.bank[:, 0:D], self.b[:, 0:D], ALU.add).then_inc(self.kv_taken, 1)
        if j == 2:
            v.wait_ge(self.sq_ready, i + 1)
            v.tensor_reduce(self.ss[:, :], self.sq[:, :].rearrange("p (h d) -> p h d", h=HEADS), AX.X, ALU.add).then_inc(self.ss_ready, 1)
        if j == 3:
            v.wait_ge(self.kv_ready, 2 * i + 2)
            v.tensor_tensor(self.vb[:, :], self.bank[:, 0:D], self.b[:, D:2 * D], ALU.add).then_inc(self.kv_taken, 1)
        if j == 4:
            v.wait_ge(self.n_ready, i + 1)
            own.inc(v.tensor_scalar(self.r[:, :], self.n[:, :], 1e-12, None, ALU.max))
            own.wait(v)
            own.inc(v.reciprocal(self.r[:, :], self.r[:, :]))
            own.wait(v)
            v.wait_ge(self.phi_used, i + 1)
            own.inc(v.tensor_scalar(self.r[:, :], self.r[:, :], HSCALE, None, ALU.mult))
            own.wait(v)
            own.inc(v.tensor_tensor(self.ext[:, :, 0:HD], self.kb[:, :].rearrange("p (h d) -> p h d", h=HEADS),
                                    self.r[:, :].unsqueeze(2).to_broadcast([P, HEADS, HD]), ALU.mult))
            v1 = self.v1[:, :].rearrange("p (h e) -> p h e", h=HEADS)
            own.wait(v)
            own.inc(v.tensor_copy(self.ext[:, :, HD:48], self.ext[:, :, 0:16]))
            v.wait_ge(self.kv_taken, 2 * i + 2)
            own.inc(v.tensor_scalar(v1[:, :, 1:VW], self.vb[:, :].rearrange("p (h d) -> p h d", h=HEADS),
                                    m.valid[:, ds(i, 1)], 1.0 / N, ALU.mult, ALU.mult))
            own.inc(v.tensor_scalar(v1[:, :, 0:1], m.ones[:, 0:HEADS].unsqueeze(2), m.valid[:, ds(i, 1)], 1.0 / N, ALU.mult, ALU.mult))
            own.wait(v)
        if 5 <= j < 5 + HEADS:
            make_map(v, own, m, self.ext, self.phi, j - 5).then_inc(self.phi_ready, 1)
        if j == 15:
            v.wait_ge(self.tail_ready, i + 1)
            v.wait_ge(self.tail_taken, i + 1)
            v.tensor_tensor(m.kvtail[:, :], m.kvtail[:, :], self.bank[:, 0:HEADS * VW + WIN], ALU.add).then_inc(self.tail_taken, 1)

    def after_vector(self, v):
        m = self.m
        v.wait_ge(self.coef_in, 16)
        v.wait_ge(self.sums_ready, 1)
        v.wait_ge(self.tail_taken, TILES + 1)
        for k, s in enumerate(self.sums):
            kv = m.kvs[:, k * PER_BANK * WIN:(k + 1) * PER_BANK * WIN]
            v.tensor_tensor(kv, s[:, 0:PER_BANK * WIN], kv, ALU.mult)
        kv = m.kvs[:, (BLOCKS - 1) * WIN:BLOCKS * WIN]
        v.tensor_tensor(kv, m.kvtail[:, HEADS * VW:], kv, ALU.mult)
        v.tensor_scalar(m.kvconst[0:1, :], m.kvtail[0:1, 0:HEADS * VW], MIX_C * HSCALE ** 4, None, ALU.mult)

    def before_scalar(self, act):
        act.sem_inc(self.phi_used, 1)

    def scalar(self, act, i, j):
        if j == 1:
            act.wait_ge(self.kv_taken, 2 * i + 1)
            act.activation(self.sq[:, :], self.kb[:, :], ACT.Square).then_inc(self.sq_ready, 1)
        if j == 2:
            act.wait_ge(self.ss_ready, i + 1)
            act.activation(self.n[:, :], self.ss[:, :], ACT.Sqrt).then_inc(self.n_ready, 1)
        if j == 15:
            act.wait_ge(self.tail_ready, i + 1)
            act.sem_inc(self.phi_used, 1)


class MixQueries(Side):
    GROUP = 4
    GROUPS = BLOCKS // GROUP

    def __init__(self, nc, m, name, c, a, bank, loop):
        super().__init__()
        sem = stage_semaphores(nc, c, name)
        self.m, self.a, self.bank, self.loop = m, a, bank, loop
        self.w_in, self.q_in, self.q_used = sem("_qw_in"), sem("_q_in"), sem("_q_used")
        self.q_ready, self.q_taken, self.sq_ready, self.ss_ready, self.n_ready = (sem(x) for x in ("_q_ready", "_q_taken", "_sq_ready", "_ss_ready", "_n_ready"))
        self.phi_ready, self.t_ready, self.t_copied, self.t_used = (sem(x) for x in ("_phi_ready", "_t_ready", "_t_copied", "_t_used"))
        self.o_ready, self.ot_ready, self.ot_copied, self.out_ready, self.x_done = (sem(x) for x in ("_o_ready", "_ot_ready", "_ot_copied", "_out_ready", "_x_done"))
        self.own = Count(sem("_q_own"))
        self.vector_counts = [(self.own, 6)]
        self.w, self.wp = m.take([P, 2, D]), m.take([P, 2, D])
        self.b, self.bp = m.take([P, D]), m.take([P, D])
        self.temp = m.take([P, HEADS])
        self.xt = m.take([P, D])
        self.qb, self.sq = m.take([P, D]), m.take([P, D])
        self.ss, self.n, self.r, self.yr = (m.take([P, HEADS]) for _ in range(4))
        self.ext = m.take([P, HEADS, 48])
        self.phi = m.take([P, HEADS * FEAT])
        self.phiT = m.take([P, 2, 512])
        self.o, self.oT = m.take([P, D]), m.take([P, D])
        ps = lambda x: c.enter_context(nc.psum_tensor(name + x, [P, 512], F32))
        self.psT, self.y, self.out = [ps("_pt0"), ps("_pt1")], ps("_y"), ps("_out")

    def before_sync(self, sp):
        a = self.a
        sp.dma_start(self.w[:, :, :], by_half(a["L0_mix_Wqkv"][:, 0:D])).then_inc(self.w_in, 16)
        sp.dma_start(self.wp[:, :, :], by_half(a["L0_mix_Wproj"])).then_inc(self.w_in, 16)
        sp.dma_start(self.b[:, :], row(a["L0_mix_bqkv"][0:D])).then_inc(self.w_in, 16)
        sp.dma_start(self.bp[0:1, :], one_row(a["L0_mix_bproj"])).then_inc(self.w_in, 16)
        sp.dma_start(self.temp[:, :], row(a["L0_mix_temperature"].rearrange("a h b c -> (a h b c)"))).then_inc(self.w_in, 16)
        self.load(sp, 0)

    def load(self, sp, t):
        sp.wait_ge(self.q_used, t + 1)
        sp.sem_inc(self.m.woken_sp, 1)
        sp.dma_start(self.xt[:, :], self.m.xt_dram[0, ds(t, 1), :, :].rearrange("o p d -> (o p) d")).then_inc(self.q_in, 16)

    def sync(self, sp, i):
        if not is_last(i):
            self.load(sp, i + 1)

    def project_queries(self, pe, t):
        pe.wait_ge(self.q_in, 16 * (t + 1))
        pe.wait_ge(self.loop.l_copied, t + 1)
        for k in range(2):
            last = pe.matmul(self.bank[:, 0:D], self.xt[:, k * P:(k + 1) * P], self.w[:, k, :], start=(k == 0), stop=(k == 1))
        last.then_inc(self.q_ready, 1)

    def before_tensor(self, pe):
        pe.wait_ge(self.w_in, 80)
        self.project_queries(pe, 0)
        pe.sem_inc(self.t_used, 1)

    def tensor(self, pe, i, j):
        m, G = self.m, self.GROUPS
        g = j - 1
        if 0 <= g < G:
            head = min(((g + 1) * self.GROUP * P - 1) // FEAT, HEADS - 1)
            pe.wait_ge(self.phi_ready, i * HEADS + head + 1)
            if g != 1:
                pe.wait_ge(self.t_copied, i * G + (g if g else 1))
            for k in range(self.GROUP):
                b = g * self.GROUP + k
                last = pe.transpose(self.psT[g % 2][:, k * P:(k + 1) * P], self.phi[:, b * P:(b + 1) * P], m.ident[:, :])
            last.then_inc(self.t_ready, 1)
        g = j - 2
        if 0 <= g < G:
            if g == 0:
                pe.wait_ge(self.o_ready, i + 1)
                pe.matmul(self.y[:, 0:HEADS * VW], m.ones[0:1, :], m.kvconst[0:1, :], start=True, stop=False, skip_group_check=True)
            pe.wait_ge(self.t_copied, i * G + g + 2)
            for k in range(self.GROUP):
                b = g * self.GROUP + k
                w = window(b) * VW
                last = pe.matmul(self.y[:, w:w + WIN], self.phiT[:, g % 2, k * P:(k + 1) * P], m.kvs[:, b * WIN:(b + 1) * WIN],
                                 start=False, stop=(b == BLOCKS - 1), skip_group_check=True)
            last.then_inc(self.t_used, 1)
        if j == 11 and not is_last(i):
            self.project_queries(pe, i + 1)
        if j == 12:
            pe.wait_ge(self.o_ready, i + 2)
            pe.wait_ge(self.x_done, i + 1)
            for k in range(2):
                last = pe.transpose(self.out[:, k * P:(k + 1) * P], self.o[:, k * P:(k + 1) * P], m.ident[:, :])
            last.then_inc(self.ot_ready, 1)
        if j == 14:
            pe.wait_ge(self.ot_copied, i + 1)
            for k in range(2):
                pe.matmul(self.out[:, 0:D], self.oT[:, k * P:(k + 1) * P], self.wp[:, k, :], start=(k == 0), stop=False)
            pe.matmul(self.out[:, 0:D], m.ones[0:1, :], self.bp[0:1, :], start=False, stop=True).then_inc(self.out_ready, 1)

    def front(self, v, step, t):
        own = self.own
        if step == 0:
            v.wait_ge(self.q_ready, t + 1)
            v.tensor_tensor(self.qb[:, :], self.bank[:, 0:D], self.b[:, :], ALU.add).then_inc(self.q_taken, 1)
        if step == 1:
            v.wait_ge(self.sq_ready, t + 1)
            v.tensor_reduce(self.ss[:, :], self.sq[:, :].rearrange("p (h d) -> p h d", h=HEADS), AX.X, ALU.add).then_inc(self.ss_ready, 1)
        if step == 2:
            v.wait_ge(self.n_ready, t + 1)
            own.inc(v.tensor_scalar(self.r[:, :], self.n[:, :], 1e-12, None, ALU.max))
            own.wait(v)
            own.inc(v.reciprocal(self.r[:, :], self.r[:, :]))
            own.wait(v)
            own.inc(v.tensor_tensor(self.r[:, :], self.r[:, :], self.temp[:, :], ALU.mult))
            own.wait(v)
            own.inc(v.tensor_tensor(self.ext[:, :, 0:HD], self.qb[:, :].rearrange("p (h d) -> p h d", h=HEADS),
                                    self.r[:, :].unsqueeze(2).to_broadcast([P, HEADS, HD]), ALU.mult))
            own.wait(v)
            own.inc(v.tensor_copy(self.ext[:, :, HD:48], self.ext[:, :, 0:16]))
            own.wait(v)

    def before_vector(self, v):
        v.sem_inc(self.o_ready, 1)
        v.sem_inc(self.x_done, 1)
        v.wait_ge(self.w_in, 80)
        self.own.inc(v.tensor_scalar(self.temp[:, :], self.temp[:, :], HSCALE ** 2, None, ALU.mult))
        self.own.wait(v)
        for step in range(3):
            self.front(v, step, 0)

    def vector(self, v, i, j):
        own, m = self.own, self.m
        if j < HEADS:
            make_map(v, own, m, self.ext, self.phi, j).then_inc(self.phi_ready, 1)
        if j == 11:
            v.wait_ge(self.t_used, (i + 1) * self.GROUPS + 1)
            y = self.y[:, 0:HEADS * VW].rearrange("p (h e) -> p h e", h=HEADS)
            own.inc(v.reciprocal(self.yr[:, :].unsqueeze(2), y[:, :, 0:1]))
            own.wait(v)
            v.tensor_tensor(self.o[:, :].rearrange("p (h d) -> p h d", h=HEADS), y[:, :, 1:VW],
                            self.yr[:, :].unsqueeze(2).to_broadcast([P, HEADS, HD]), ALU.mult).then_inc(self.o_ready, 1)
        if 12 <= j < 15 and not is_last(i):
            self.front(v, j - 12, i + 1)
        if j == 15:
            v.wait_ge(self.out_ready, i + 1)
            v.tensor_tensor(tile_of(m.X, i), tile_of(m.X, i), self.out[:, 0:D], ALU.add).then_inc(self.x_done, 1)

    def before_scalar(self, act):
        act.sem_inc(self.q_used, 1)
        act.sem_inc(self.t_copied, 1)
        self.square(act, 0)
        self.root(act, 0)

    def square(self, act, t):
        act.wait_ge(self.q_taken, t + 1)
        act.sem_inc(self.q_used, 1)
        act.activation(self.sq[:, :], self.qb[:, :], ACT.Square).then_inc(self.sq_ready, 1)

    def root(self, act, t):
        act.wait_ge(self.ss_ready, t + 1)
        act.activation(self.n[:, :], self.ss[:, :], ACT.Sqrt, scale=HSCALE ** 2).then_inc(self.n_ready, 1)

    def scalar(self, act, i, j):
        G, g = self.GROUPS, j - 1
        if 0 <= g < G:
            act.wait_ge(self.t_ready, i * G + g + 1)
            if g != 1:
                act.wait_ge(self.t_used, i * G + (g if g else 1))
            act.activation(self.phiT[:, g % 2, :], self.psT[g % 2][:, :], ACT.Copy).then_inc(self.t_copied, 1)
        if j == 12:
            if not is_last(i):
                self.square(act, i + 1)
            act.wait_ge(self.ot_ready, i + 1)
            act.activation(self.oT[:, :], self.out[:, 0:D], ACT.Copy).then_inc(self.ot_copied, 1)
        if j == 13 and not is_last(i):
            self.root(act, i + 1)


def finish(nc, m, name, gamma, beta=None):
    with ExitStack() as c:
        v_in, dve = map(stage_semaphores(nc, c, name), ("_in", "_dve"))
        mark = m.mark()
        gam, bet, tmp = m.take([P, D]), m.take([P, D]), m.take([P, 4, D])
        with nc.Block() as block:
            @block.sync
            def _(sp):
                sp.dma_start(gam[:, :], row(gamma)).then_inc(v_in, 16)
                if beta is not None:
                    sp.dma_start(bet[:, :], row(beta)).then_inc(v_in, 16)

            @block.vector
            def _(v):
                own = Count(dve)
                v.wait_ge(v_in, 16 if beta is None else 32)

                def body(t, j):
                    own.inc(v.tensor_scalar(tmp[:, j, :], tile_of(m.AGG, t), m.mean(t), m.rstd_of(t), ALU.subtract, ALU.mult))
                    own.inc(v.tensor_tensor(tile_of(m.X, t), tile_of(m.X, t), bet[:, :] if beta is not None else tile_of(m.L, t), ALU.add))
                    own.wait(v)
                    own.inc(v.tensor_tensor(tmp[:, j, :], tmp[:, j, :], gam[:, :], ALU.mult))
                    own.wait(v)
                    own.inc(v.tensor_tensor(tile_of(m.X, t), tile_of(m.X, t), tmp[:, j, :], ALU.add))
                tiles4(v, body, [(own, 4)])
        m.release(mark)


EXPERTS, FF, TOP = 8, 512, 2
FB = FF // P
CAPACITY = float(-(-N * 5 // (4 * EXPERTS)))


def route(nc, m, a):
    with ExitStack() as c:
        sem = stage_semaphores(nc, c, "rt")
        w_in, x_in, dve_own, h_ready, h_free = sem("_w"), sem("_x"), sem("_dve"), sem("_h_ready"), sem("_h_free")
        sums, mean_ready, logits, e_ready, ex_done, idx_ready = sem("_sums"), sem("_mean"), sem("_logits"), sem("_e"), sem("_exp"), sem("_idx")
        b1_ready = sem("_b1")
        wr, br = m.take([P, 2, EXPERTS]), m.take([P, EXPERTS])
        h, mc, mb = m.take([P, 2, D]), m.take([P, 2]), m.take([P, 2, P])
        lg, ex, col = m.take([P, EXPERTS]), m.take([P, EXPERTS]), m.take([P, 16])
        top, idx = m.take([P, EXPERTS]), m.take([P, EXPERTS], U32)
        b1n, b2r = m.take([P, P]), m.take([P, 2, D])
        psS = [c.enter_context(nc.psum_tensor(f"rt_s{k}", [P, 512], F32)) for k in range(2)]
        psL = c.enter_context(nc.psum_tensor("rt_l", [P, 512], F32))
        psB = c.enter_context(nc.psum_tensor("rt_b", [P, 512], F32))
        with nc.Block() as block:
            @block.sync
            def _(sp):
                sp.dma_start(wr[:, :, :], by_half(a["L0_ffn_Wr"])).then_inc(w_in, 16)
                sp.dma_start(br[:, :], row(a["L0_ffn_br"])).then_inc(w_in, 16)
                sp.wait_ge(idx_ready, 1)
                for k in range(TOP):
                    e = sp.value_load(idx[0:1, k:k + 1], min_val=0, max_val=EXPERTS - 1)
                    one = lambda ap: ap[ds(e, 1)]
                    sp.dma_start(m.w1[:, k, :, :], one(a["L0_ffn_W1"]).rearrange("o (k p) f -> p (o k) f", p=P)).then_inc(x_in, 16)
                    sp.dma_start(m.w2[:, k, :, :], one(a["L0_ffn_W2"]).rearrange("o (b p) d -> p (o b) d", p=P)).then_inc(x_in, 16)
                    sp.dma_start(b1n[k * FB:(k + 1) * FB, :], one(a["L0_ffn_b1"]).rearrange("o (b p) -> (o b) p", p=P)).then_inc(x_in, 16)
                    sp.dma_start(b2r[:, k, :], one(a["L0_ffn_b2"]).to_broadcast([P, D])).then_inc(x_in, 16)

            @block.vector
            def _(v):
                own = Count(dve_own)

                def step(ins):
                    own.inc(ins)
                    own.wait(v)

                def body(t, j):
                    v.wait_ge(h_free, t + 1)
                    v.tensor_scalar(h[:, j % 2, :], tile_of(m.X, t), m.mean(t), m.rstd_of(t), ALU.subtract, ALU.mult).then_inc(h_ready, 1)
                tiles4(v, body)
                v.wait_ge(sums, 1)
                for k in range(2):
                    own.inc(v.tensor_scalar(mc[:, k:k + 1], psS[k][:, 0:1], 1.0 / N, None, ALU.mult))
                own.wait(v)
                v.tensor_copy(mb[:, :, :], mc[:, :].unsqueeze(2).to_broadcast([P, 2, P])).then_inc(mean_ready, 1)
                v.wait_ge(logits, 1)
                step(v.tensor_tensor(lg[:, :], psL[:, 0:EXPERTS], br[:, :], ALU.add))

                def softmax(turn):
                    step(v.tensor_reduce(col[:, 0:1], lg[:, :], AX.X, ALU.max))
                    step(v.tensor_scalar(lg[:, :], lg[:, :], col[:, 0:1], None, ALU.subtract))
                    v.sem_inc(e_ready, 1)
                    v.wait_ge(ex_done, turn)
                    step(v.tensor_reduce(col[:, 1:2], ex[:, :], AX.X, ALU.add))
                    step(v.reciprocal(col[:, 2:3], col[:, 1:2]))
                    step(v.tensor_scalar(lg[:, :], ex[:, :], col[:, 2:3], None, ALU.mult))
                softmax(1)
                step(v.tensor_scalar(ex[:, :], lg[:, :], float(N), None, ALU.mult))
                step(v.reciprocal(ex[:, :], ex[:, :]))
                step(v.tensor_scalar(ex[:, :], ex[:, :], CAPACITY, 1.0, ALU.mult, ALU.min))
                step(v.tensor_tensor(lg[:, :], lg[:, :], ex[:, :], ALU.mult))
                softmax(2)
                step(v.max(top[:, :], lg[:, :]))
                v.max_index(idx[:, :], top[:, :], lg[:, :]).then_inc(idx_ready, 1)
                v.wait_ge(idx_ready, 1)
                step(v.tensor_scalar(lg[:, :], top[:, :], top[:, 0:1], None, ALU.subtract))
                v.sem_inc(e_ready, 1)
                v.wait_ge(ex_done, 3)
                step(v.tensor_tensor(col[:, 3:4], ex[:, 0:1], ex[:, 1:2], ALU.add))
                step(v.reciprocal(col[:, 4:5], col[:, 3:4]))
                step(v.tensor_scalar(m.gate[:, :], ex[:, 0:TOP], col[:, 4:5], None, ALU.mult))
                v.wait_ge(x_in, 16 * 4 * TOP)
                for k in range(TOP):
                    own.inc(v.tensor_scalar(m.w2[:, k, :, :], m.w2[:, k, :, :], m.gate[:, k:k + 1], None, ALU.mult))
                own.inc(v.tensor_scalar(b2r[:, 0, :], b2r[:, 0, :], m.gate[:, 0:1], None, ALU.mult))
                own.wait(v)
                v.scalar_tensor_tensor(m.b2[:, :], b2r[:, 1, :], m.gate[:, 1:2], b2r[:, 0, :], ALU.mult, ALU.add)
                v.wait_ge(b1_ready, 1)
                v.tensor_copy(m.b1[:, :], psB[:, 0:TOP * FB])

            @block.scalar
            def _(act):
                for turn in range(3):
                    act.wait_ge(e_ready, turn + 1)
                    act.activation(ex[:, :], lg[:, :], ACT.Exp).then_inc(ex_done, 1)

            @block.tensor
            def _(pe):
                pe.sem_inc(h_free, 2)
                for k in range(2):
                    pe.matmul(psS[k][:, 0:1], m.zeros[:, 0:P], m.ones[:, 0:1], start=True, stop=False, skip_group_check=True)

                def body(t, j):
                    pe.wait_ge(h_ready, t + 1)
                    for k in range(2):
                        last = pe.matmul(psS[k][:, 0:1], h[:, j % 2, k * P:(k + 1) * P], m.valid[:, ds(t, 1)], start=False, stop=is_last(t), skip_group_check=True)
                    last.then_inc(h_free, 1)
                tiles4(pe, body)
                pe.wait_ge(h_free, TILES + 2)
                pe.sem_inc(sums, 1)
                pe.wait_ge(mean_ready, 1)
                pe.wait_ge(w_in, 32)
                for k in range(2):
                    last = pe.matmul(psL[:, 0:EXPERTS], mb[:, k, :], wr[:, k, :], start=(k == 0), stop=(k == 1))
                last.then_inc(logits, 1)
                pe.wait_ge(x_in, 16 * 4 * TOP)
                pe.transpose(psB[:, 0:TOP * FB], b1n[0:TOP * FB, :], m.ident[0:TOP * FB, 0:TOP * FB]).then_inc(b1_ready, 1)


def experts(nc, m):
    HB = TOP * FB
    with ExitStack() as c:
        sem = stage_semaphores(nc, c, "ex")
        h_ready, h_free, xt_done, hid_ready, hid_done, y_ready, y_taken, dve_own = (
            sem(x) for x in ("_h_ready", "_h_free", "_xt", "_hid_ready", "_hid_done", "_y_ready", "_y_taken", "_dve"))
        mark = m.mark()
        h, xt, tmp = m.take([P, 2, D]), m.take([P, 2, D]), m.take([P, 2, D])
        hid = m.take([P, 2, HB * P])
        ps = lambda x: c.enter_context(nc.psum_tensor("ex" + x, [P, 512], F32))
        psT, psY = [ps("_t0"), ps("_t1")], [ps("_y0"), ps("_y1")]
        psH = [[ps(f"_h{s}{k}") for k in range(2)] for s in range(2)]
        with nc.Block() as block:
            @block.vector
            def _(v):
                own = Count(dve_own)
                v.sem_inc(y_taken, 2)

                def make_h(t, j):
                    v.wait_ge(h_free, t + 1)
                    v.tensor_scalar(h[:, j % 2, :], tile_of(m.X, t), m.mean(t), m.rstd_of(t), ALU.subtract, ALU.mult).then_inc(h_ready, 1)

                def body(t, j):
                    if not is_last(t):
                        make_h(t + 1, j + 1)
                    v.wait_ge(y_ready, t + 1)
                    v.tensor_tensor(tmp[:, j % 2, :], psY[j % 2][:, 0:D], h[:, j % 2, :], ALU.add).then_inc(y_taken, 1)
                    v.wait_ge(y_taken, t + 3)
                    v.tensor_tensor(tile_of(m.AGG, t), tmp[:, j % 2, :], m.b2[:, :], ALU.add)
                make_h(0, 0)
                tiles4(v, body)

            @block.tensor
            def _(pe):
                pe.sem_inc(h_free, 2)

                def transposes(t, j):
                    pe.wait_ge(h_ready, t + 1)
                    pe.wait_ge(xt_done, t + 1)
                    for k in range(2):
                        last = pe.transpose(psT[j % 2][:, k * P:(k + 1) * P], h[:, j % 2, k * P:(k + 1) * P], m.ident[:, :])
                    last.then_inc(h_free, 1)

                def hidden(t, j):
                    pe.wait_ge(xt_done, t + 3)
                    pe.wait_ge(hid_done, HB * t + HB)
                    for b in range(HB):
                        e, f = divmod(b, FB)
                        for k in range(2):
                            last = pe.matmul(psH[j % 2][e][:, f * P:(f + 1) * P], m.w1[:, e, k, f * P:(f + 1) * P],
                                             xt[:, j % 2, k * P:(k + 1) * P], start=(k == 0), stop=(k == 1))
                        if f == FB - 1:
                            last.then_inc(hid_ready, 1)

                def out(t, j):
                    pe.wait_ge(hid_done, HB * t + 3 * HB)
                    pe.wait_ge(y_taken, t + 1)
                    for b in range(HB):
                        e, f = divmod(b, FB)
                        last = pe.matmul(psY[j % 2][:, 0:D], hid[:, j % 2, b * P:(b + 1) * P], m.w2[:, e, f, :], start=(b == 0), stop=(b == HB - 1))
                    last.then_inc(y_ready, 1)

                def body(t, j):
                    if not is_last(t):
                        transposes(t + 1, j + 1)
                    out(t, j)
                    if not is_last(t):
                        hidden(t + 1, j + 1)
                transposes(0, 0)
                hidden(0, 0)
                tiles4(pe, body)

            @block.scalar
            def _(act):
                act.sem_inc(xt_done, 2)
                act.sem_inc(hid_done, 2 * HB)

                def copy_xt(t, j):
                    act.wait_ge(h_free, t + 3)
                    act.activation(xt[:, j % 2, :], psT[j % 2][:, 0:D], ACT.Copy).then_inc(xt_done, 1)

                def gelu(t, j):
                    for b in range(HB):
                        e, f = divmod(b, FB)
                        if f == 0:
                            act.wait_ge(hid_ready, TOP * t + e + 1)
                        act.activation(hid[:, j % 2, b * P:(b + 1) * P], psH[j % 2][e][:, f * P:(f + 1) * P], ACT.Gelu,
                                       bias=m.b1[:, b:b + 1]).then_inc(hid_done, 1)

                def body(t, j):
                    gelu(t, j)
                    if not is_last(t):
                        copy_xt(t + 1, j + 1)
                copy_xt(0, 0)
                tiles4(act, body)
        m.release(mark)


HEADS1, HD1 = 4, 64
HALF = P // 2


def use16(t, j):
    return 16 * (t // 4 + 1) if isinstance(t, int) else (t - j) * 4 + 16


class LinearMix(Side):

    def __init__(self, nc, m, name, c, a):
        super().__init__()
        sem = stage_semaphores(nc, c, name)
        self.m, self.a = m, a
        self.w_in, self.w_ready, self.t_in, self.t_used = sem("_w_in"), sem("_w_ready"), sem("_t_in"), sem("_t_used")
        self.p_ready, self.p_taken, self.sq_ready, self.ss_ready, self.sd_ready = (
            sem("_p_ready"), sem("_p_taken"), sem("_sq_ready"), sem("_ss_ready"), sem("_sd_ready"))
        self.kv_ready, self.kv_used, self.sum_ready = sem("_kv_ready"), sem("_kv_used"), sem("_sum_ready")
        self.own = Count(sem("_own"))
        self.vector_counts = [(self.own, 4)]
        self.w, self.mean = m.take([P, 2, 2 * D]), m.take([P, 2, 2 * HEADS1])
        self.g, self.b = m.take([P, 2 * D]), m.take([P, 2 * D])
        self.xt, self.sq, self.kv = m.take([P, D]), m.take([P, 2 * D]), m.take([P, 2 * D])
        self.ss, self.sd, self.r = m.take([P, 2 * HEADS1]), m.take([P, 2 * HEADS1]), m.take([P, 2 * HEADS1])
        ps = lambda x: c.enter_context(nc.psum_tensor(name + x, [P, 512], F32))
        self.p, self.sum = ps("_kv"), ps("_sum")

    def heads(self, ap):
        return ap.rearrange("p (h d) -> p h d", d=HD1)

    def before_sync(self, sp):
        a = self.a
        sp.dma_start(self.w[:, :, 0:D], by_half(a["L1_mix_wk"])).then_inc(self.w_in, 16)
        sp.dma_start(self.w[:, :, D:2 * D], by_half(a["L1_mix_wv"])).then_inc(self.w_in, 16)
        for vec, k, v in ((self.g, "L1_mix_ln_k_g", "L1_mix_ln_v_g"), (self.b, "L1_mix_ln_k_b", "L1_mix_ln_v_b")):
            for at, name in ((0, k), (D, v)):
                for h in range(HEADS1):
                    sp.dma_start(vec[:, at + h * HD1:at + (h + 1) * HD1], row(a[name])).then_inc(self.w_in, 16)

    def sync(self, sp, i):
        sp.wait_ge(self.t_used, i + 1)
        sp.sem_inc(self.m.woken_sp, 1)
        sp.dma_start(self.xt[:, :], self.m.xt_dram[3, ds(i, 1), :, :].rearrange("o p d -> (o p) d")).then_inc(self.t_in, 16)

    def before_tensor(self, pe):
        pe.wait_ge(self.w_ready, 1)
        pe.matmul(self.sum[:, 0:D], self.m.zeros[:, 0:P], self.m.zeros[:, 0:D], start=True, stop=False, skip_group_check=True)

    def tensor(self, pe, i, j):
        if j == 0:
            pe.wait_ge(self.t_in, 16 * (i + 1))
            pe.wait_ge(self.p_taken, i + 1)
            for k in range(2):
                last = pe.matmul(self.p[:, :], self.xt[:, k * P:(k + 1) * P], self.w[:, k, :], start=(k == 0), stop=(k == 1))
            last.then_inc(self.p_ready, 1)
        if j == 10:
            pe.wait_ge(self.kv_ready, i + 2)
            for k in range(2):
                last = pe.matmul(self.sum[:, k * P:(k + 1) * P], self.kv[:, k * P:(k + 1) * P], self.kv[:, D + k * P:D + (k + 1) * P],
                                 start=False, stop=False, skip_group_check=True)
            last.then_inc(self.kv_used, 1)

    def after_tensor(self, pe):
        pe.matmul(self.sum[:, 0:D], self.m.zeros[:, 0:P], self.m.zeros[:, 0:D], start=False, stop=True,
                  skip_group_check=True).then_inc(self.sum_ready, 1)

    def before_vector(self, v):
        own = self.own
        v.sem_inc(self.p_taken, 1)
        v.sem_inc(self.kv_used, 1)
        v.sem_inc(self.kv_ready, 1)
        v.memset(self.m.kv[:, :, :], 0.0)
        v.wait_ge(self.w_in, 16 * (2 + 4 * HEADS1))
        for k in range(2):
            own.inc(v.tensor_reduce(self.mean[:, k, :], self.heads(self.w[:, k, :]), AX.X, ALU.add))
        own.wait(v)
        own.inc(v.tensor_scalar(self.mean[:, :, :], self.mean[:, :, :], -1.0 / HD1, None, ALU.mult))
        own.wait(v)
        for k in range(2):
            own.inc(v.tensor_tensor(self.heads(self.w[:, k, :]), self.heads(self.w[:, k, :]),
                                    self.mean[:, k, :].unsqueeze(2).to_broadcast([P, 2 * HEADS1, HD1]), ALU.add))
        own.wait(v)
        v.sem_inc(self.w_ready, 1)

    def vector(self, v, i, j):
        own, m = self.own, self.m
        if j == 3:
            v.wait_ge(self.sq_ready, i + 1)
            v.tensor_reduce(self.ss[:, :], self.heads(self.sq[:, :]), AX.X, ALU.add).then_inc(self.ss_ready, 1)
        if j == 5:
            v.wait_ge(self.sd_ready, i + 1)
            own.inc(v.reciprocal(self.r[:, :], self.sd[:, :]))
            own.wait(v)
            own.inc(v.tensor_tensor(self.heads(self.sq[:, :]), self.heads(self.p[:, :]),
                                    self.r[:, :].unsqueeze(2).to_broadcast([P, 2 * HEADS1, HD1]), ALU.mult))
            own.wait(v)
            v.sem_inc(self.p_taken, 1)
        if j == 6:
            v.wait_ge(self.kv_used, i + 1)
            own.inc(v.tensor_tensor(self.kv[:, :], self.sq[:, :], self.g[:, :], ALU.mult))
            own.wait(v)
        if j == 7:
            own.inc(v.tensor_tensor(self.kv[:, :], self.kv[:, :], self.b[:, :], ALU.add))
            own.wait(v)
            v.tensor_scalar(self.kv[:, 0:D], self.kv[:, 0:D], m.valid[:, ds(i, 1)], 1.0 / N, ALU.mult, ALU.mult).then_inc(self.kv_ready, 1)

    def after_vector(self, v):
        v.wait_ge(self.sum_ready, 1)
        for k in range(2):
            for r in (0, HALF):
                v.tensor_copy(self.m.kv[r:r + HALF, k, r:r + HALF], self.sum[r:r + HALF, k * P + r:k * P + r + HALF])

    def before_scalar(self, act):
        act.sem_inc(self.t_used, 1)

    def scalar(self, act, i, j):
        if j == 1:
            act.wait_ge(self.p_ready, i + 1)
            act.sem_inc(self.t_used, 1)
            act.wait_ge(self.kv_ready, i + 1)
            act.activation(self.sq[:, :], self.p[:, :], ACT.Square).then_inc(self.sq_ready, 1)
        if j == 4:
            act.wait_ge(self.ss_ready, i + 1)
            act.activation(self.sd[:, :], self.ss[:, :], ACT.Sqrt, bias=self.m.eps[:, 0:1], scale=1.0 / HD1).then_inc(self.sd_ready, 1)


def combine(nc, m, a):
    with ExitStack() as c:
        sem = stage_semaphores(nc, c, "cb")
        w_in, a_ready, a_taken, out_ready, x_done, own_sem = (sem(x) for x in ("_w_in", "_a_ready", "_a_taken", "_out_ready", "_x_done", "_own"))
        t_in = [sem(f"_t_in{j}") for j in range(4)]
        mark = m.mark()
        wq, wo, bo = m.take([P, 2, D]), m.take([P, 2, D]), m.take([P, D])
        kq, prod = m.take([P, 2, D]), m.take([P, 2, D])
        xt = m.take([P, 4, D])
        ps = [c.enter_context(nc.psum_tensor(f"cb_a{k}", [P, 512], F32)) for k in range(2)]
        out = [c.enter_context(nc.psum_tensor(f"cb_o{k}", [P, 512], F32)) for k in range(2)]
        with nc.Block() as block:
            @block.sync
            def _(sp):
                sp.dma_start(wq[:, :, :], by_half(a["L1_mix_wq"])).then_inc(w_in, 16)
                sp.dma_start(wo[:, :, :], by_half(a["L1_mix_wo"])).then_inc(w_in, 16)
                sp.dma_start(bo[:, :], row(a["L1_mix_bo"])).then_inc(w_in, 16)

                def load(t, j):
                    sp.wait_ge(out_ready, t + 1)
                    sp.sem_inc(m.woken_sp, 1)
                    sp.dma_start(xt[:, j, :], m.xt_dram[3, ds(t, 1), :, :].rearrange("o p d -> (o p) d")).then_inc(t_in[j], 16)
                tiles4(sp, load)

            @block.tensor
            def _(pe):
                pe.sem_inc(out_ready, 4)
                pe.wait_ge(w_in, 48)
                for k in range(2):
                    last = pe.matmul(ps[0][:, k * D:(k + 1) * D], m.kv[:, k, :], wq[:, k, :], start=True, stop=True)
                last.then_inc(a_ready, 1)
                pe.wait_ge(a_taken, 1)
                for half in range(2):
                    for k in range(2):
                        last = pe.matmul(ps[1][:, half * D:(half + 1) * D], kq[:, k, half * P:(half + 1) * P], wo[:, k, :],
                                         start=(k == 0), stop=(k == 1))
                last.then_inc(a_ready, 1)
                pe.wait_ge(a_taken, 2)

                def product(t, j):
                    pe.wait_ge(t_in[j], use16(t, j))
                    pe.wait_ge(x_done, t + 1)
                    for k in range(2):
                        last = pe.matmul(out[j % 2][:, 0:D], xt[:, j, k * P:(k + 1) * P], prod[:, k, :], start=(k == 0), stop=(k == 1))
                    last.then_inc(out_ready, 1)
                tiles4(pe, product)

            @block.scalar
            def _(act):
                for turn, to in ((1, kq), (2, prod)):
                    act.wait_ge(a_ready, turn)
                    act.activation(to.rearrange("p k d -> p (k d)"), ps[turn - 1][:, :], ACT.Copy).then_inc(a_taken, 1)

            @block.vector
            def _(v):
                own = Count(own_sem)
                v.sem_inc(x_done, 2)
                v.wait_ge(w_in, 48)

                def body(t, j):
                    own.inc(v.scalar_tensor_tensor(tile_of(m.X, t), tile_of(m.AGG, t), m.norm_of(t), tile_of(m.X, t), ALU.mult, ALU.add))
                    own.wait(v)
                    own.inc(v.tensor_tensor(tile_of(m.X, t), tile_of(m.X, t), bo[:, :], ALU.add))
                    own.wait(v)
                    v.wait_ge(out_ready, t + 5)
                    v.tensor_tensor(tile_of(m.X, t), tile_of(m.X, t), out[j % 2][:, 0:D], ALU.add).then_inc(x_done, 1)
                tiles4(v, body, [(own, 2)])
        m.release(mark)


HEADS2, HD2, SLICES = 8, 64, 64
INNER = HEADS2 * HD2
QUARTERS = INNER // P


def slice_weights(nc, m, a):
    with ExitStack() as c:
        sem = stage_semaphores(nc, c, "sw")
        w_in, clear, ready, bias_ready, own_sem = (sem(x) for x in ("_in", "_clear", "_ready", "_bias", "_own"))
        mark = m.mark()
        wx, ws = m.take([P, QUARTERS, D]), m.take([P, P])
        bx, bxb = m.take([P, QUARTERS]), m.take([P, QUARTERS, P])
        bs, temp = m.take([P, SLICES]), m.take([P, HEADS2])
        ps = [c.enter_context(nc.psum_tensor(f"sw_{k}", [P, 512], F32)) for k in range(3)]
        with nc.Block() as block:
            @block.sync
            def _(sp):
                sp.dma_start(wx[:, :, :], a["L1_ffn_W_x"].rearrange("(q p) c -> p q c", p=P)).then_inc(w_in, 16)
                sp.dma_start(bx[:, :], a["b_x_pairs"]).then_inc(w_in, 16)
                sp.dma_start(bs[:, :], row(a["L1_ffn_b_slice"])).then_inc(w_in, 16)
                sp.dma_start(temp[:, :], row(a["L1_ffn_temperature"].rearrange("a h b c -> (a h b c)"))).then_inc(w_in, 16)
                sp.wait_ge(clear, 1)
                for r in (0, HALF):
                    sp.dma_start(ws[r:r + HALF, r:r + HALF], a["L1_ffn_W_slice"]).then_inc(w_in, 16)

            @block.vector
            def _(v):
                own = Count(own_sem)
                v.memset(ws[:, :], 0.0).then_inc(clear, 1)
                v.wait_ge(w_in, 96)
                v.tensor_copy(bxb[:, :, :], bx[:, :].unsqueeze(2).to_broadcast([P, QUARTERS, P])).then_inc(bias_ready, 1)
                own.inc(v.tensor_scalar(temp[:, :], temp[:, :], 0.1, 5.0, ALU.max, ALU.min))
                own.wait(v)
                own.inc(v.reciprocal(temp[:, :], temp[:, :]))
                own.wait(v)
                v.wait_ge(ready, 1)
                by_head = lambda ap: ap.rearrange("p (h g) -> p h g", h=HEADS2)
                scale = temp[:, :].unsqueeze(2).to_broadcast([P, HEADS2, SLICES])
                for k in range(2):
                    v.tensor_tensor(by_head(m.wxs[:, k, :]), by_head(ps[k][:, :]), scale, ALU.mult)
                own.inc(v.tensor_tensor(by_head(m.bxs[:, :]), by_head(ps[2][:, :]),
                                        bs[:, :].unsqueeze(1).to_broadcast([P, HEADS2, SLICES]), ALU.add))
                own.wait(v)
                v.tensor_tensor(by_head(m.bxs[:, :]), by_head(m.bxs[:, :]), scale, ALU.mult)

            @block.tensor
            def _(pe):
                pe.wait_ge(w_in, 96)
                for q in range(QUARTERS):
                    for k in range(2):
                        pe.matmul(ps[k][:, q * P:(q + 1) * P], wx[:, q, k * P:(k + 1) * P], ws[:, :], start=True, stop=True)
                pe.wait_ge(bias_ready, 1)
                for q in range(QUARTERS):
                    last = pe.matmul(ps[2][:, q * P:(q + 1) * P], bxb[:, q, :], ws[:, :], start=True, stop=True)
                last.then_inc(ready, 1)
        m.release(mark)


def slice_sums(nc, m, name="ss"):
    with ExitStack() as c:
        sem = stage_semaphores(nc, c, name)
        h_ready, t_ready, xt_ready, l_ready, l_taken, e_ready, ex_ready, sw_ready, swt_ready, swt_taken, g_done, own_sem, sums = (
            sem(x) for x in ("_h_ready", "_t_ready", "_xt_ready", "_l_ready", "_l_taken", "_e_ready", "_ex_ready", "_sw_ready",
                             "_swt_ready", "_swt_taken", "_g_done", "_own", "_sums"))
        mark = m.mark()
        h, xt = m.take([P, 4, D + 1]), m.take([P, 2, D])
        lg, ex, sw = m.take([P, INNER]), m.take([P, INNER]), m.take([P, 2, INNER])
        mx, sm = m.take([P, HEADS2]), m.take([P, HEADS2])
        ps = lambda x: c.enter_context(nc.psum_tensor(name + x, [P, 512], F32))
        psT, psL, psW, psG = ps("_t"), [ps("_l0"), ps("_l1")], ps("_w"), [ps(f"_g{q}") for q in range(QUARTERS)]
        by_head = lambda ap: ap.rearrange("p (h g) -> p h g", h=HEADS2)
        per_head = lambda ap: ap.unsqueeze(2).to_broadcast([P, HEADS2, SLICES])
        with nc.Block() as block:
            @block.vector
            def _(v):
                own = Count(own_sem)
                own.inc(v.memset(h[:, :, D:D + 1], 1.0))
                own.wait(v)
                v.sem_inc(l_taken, 2)

                def make_h(t, j):
                    v.wait_ge(g_done, t + 1)
                    v.tensor_scalar(h[:, j, 0:D], tile_of(m.X, t), m.mean(t), m.rstd_of(t), ALU.subtract, ALU.mult).then_inc(h_ready, 1)

                def body(t, j):
                    if not is_last(t):
                        make_h(t + 1, (j + 1) % 4)
                    v.wait_ge(l_ready, t + 1)
                    v.tensor_tensor(lg[:, :], psL[j % 2][:, :], m.bxs[:, :], ALU.add).then_inc(l_taken, 1)
                    v.wait_ge(l_taken, t + 3)
                    own.inc(v.tensor_reduce(mx[:, :], by_head(lg[:, :]), AX.X, ALU.max))
                    own.wait(v)
                    v.tensor_tensor(by_head(lg[:, :]), by_head(lg[:, :]), per_head(mx[:, :]), ALU.subtract).then_inc(e_ready, 1)
                    v.wait_ge(ex_ready, t + 1)
                    own.inc(v.tensor_reduce(sm[:, :], by_head(ex[:, :]), AX.X, ALU.add))
                    own.wait(v)
                    own.inc(v.reciprocal(sm[:, :], sm[:, :]))
                    own.wait(v)
                    own.inc(v.tensor_scalar(sm[:, :], sm[:, :], m.valid[:, ds(t, 1)], None, ALU.mult))
                    own.wait(v)
                    v.wait_ge(g_done, t + 3)
                    v.tensor_tensor(by_head(sw[:, j % 2, :]), by_head(ex[:, :]), per_head(sm[:, :]), ALU.mult).then_inc(sw_ready, 1)
                make_h(0, 0)
                tiles4(v, body, [(own, 4)])
                v.wait_ge(sums, 1)
                for q in range(QUARTERS):
                    v.tensor_copy(m.G[:, q, :], psG[q][:, 0:D + 1])

            @block.tensor
            def _(pe):
                pe.sem_inc(g_done, 4)
                for q in range(QUARTERS):
                    pe.matmul(psG[q][:, 0:D + 1], m.zeros[:, 0:P], m.zeros[:, :], start=True, stop=False, skip_group_check=True)

                def transposes(t, j):
                    pe.wait_ge(h_ready, t + 1)
                    pe.wait_ge(xt_ready, t + 1)
                    for k in range(2):
                        last = pe.transpose(psT[:, k * P:(k + 1) * P], h[:, j, k * P:(k + 1) * P], m.ident[:, :])
                    last.then_inc(t_ready, 1)

                def logits(t, j):
                    pe.wait_ge(xt_ready, t + 2)
                    pe.wait_ge(l_taken, t + 1)
                    for k in range(2):
                        last = pe.matmul(psL[j % 2][:, :], xt[:, j % 2, k * P:(k + 1) * P], m.wxs[:, k, :], start=(k == 0), stop=(k == 1))
                    last.then_inc(l_ready, 1)

                def body(t, j):
                    if not is_last(t):
                        transposes(t + 1, (j + 1) % 4)
                    pe.wait_ge(sw_ready, t + 1)
                    pe.wait_ge(swt_taken, t + 1)
                    for q in range(QUARTERS):
                        last = pe.transpose(psW[:, q * P:(q + 1) * P], sw[:, j % 2, q * P:(q + 1) * P], m.ident[:, :])
                    last.then_inc(swt_ready, 1)
                    if not is_last(t):
                        logits(t + 1, (j + 1) % 4)
                    for q in range(QUARTERS):
                        last = pe.matmul(psG[q][:, 0:D + 1], sw[:, j % 2, q * P:(q + 1) * P], h[:, j, :], start=False, stop=False, skip_group_check=True)
                    last.then_inc(g_done, 1)
                transposes(0, 0)
                logits(0, 0)
                tiles4(pe, body)
                for q in range(QUARTERS):
                    last = pe.matmul(psG[q][:, 0:D + 1], m.zeros[:, 0:P], m.zeros[:, :], start=False, stop=True, skip_group_check=True)
                last.then_inc(sums, 1)

            @block.scalar
            def _(act):
                act.sem_inc(xt_ready, 1)
                act.sem_inc(swt_taken, 1)

                def copy_xt(t, j):
                    act.wait_ge(t_ready, t + 1)
                    act.activation(xt[:, j % 2, :], psT[:, 0:D], ACT.Copy).then_inc(xt_ready, 1)

                def body(t, j):
                    if not is_last(t):
                        copy_xt(t + 1, (j + 1) % 4)
                    act.wait_ge(e_ready, t + 1)
                    act.activation(ex[:, :], lg[:, :], ACT.Exp).then_inc(ex_ready, 1)
                    act.wait_ge(swt_ready, t + 1)
                    act.activation(m.swT[:, ds(t, 1), :].rearrange("p o n -> p (o n)"), psW[:, :], ACT.Copy).then_inc(swt_taken, 1)
                copy_xt(0, 0)
                tiles4(act, body)
        m.release(mark)


def slice_attention(nc, m, a):
    with ExitStack() as c:
        sem = stage_semaphores(nc, c, "sa")
        w_in, clear, pe_done, cp_done, e_ready, ex_ready, own_sem = (sem(x) for x in ("_in", "_clear", "_pe", "_cp", "_e", "_ex", "_own"))
        mark = m.mark()
        wfx, bfx, wout = m.take([P, 2, INNER]), m.take([P, INNER]), m.take([P, QUARTERS, D])
        wq, wk, wv = m.take([P, P]), m.take([P, P]), m.take([P, P])
        block4 = lambda: m.take([P, QUARTERS, P])
        gT = m.take([P, 2, INNER])
        tok, tokT, qT, kT, val, attn, attnT, osT = (block4() for _ in range(8))
        raw, dots, ex = block4(), m.take([P, QUARTERS, SLICES]), m.take([P, QUARTERS, SLICES])
        rn, mx = m.take([P, QUARTERS]), m.take([P, QUARTERS])
        ps = [c.enter_context(nc.psum_tensor(f"sa_{k}", [P, 512], F32)) for k in range(8)]
        flat = lambda ap: ap.rearrange("p q n -> p (q n)")
        quarter = lambda ap, q: ap[:, q * P:(q + 1) * P]
        with nc.Block() as block:
            @block.sync
            def _(sp):
                sp.dma_start(wfx[:, :, :], by_half(a["L1_ffn_W_fx"])).then_inc(w_in, 16)
                sp.dma_start(bfx[:, :], row(a["L1_ffn_b_fx"])).then_inc(w_in, 16)
                sp.dma_start(wout[:, :, :], a["L1_ffn_W_out"].rearrange("(q p) d -> p q d", p=P)).then_inc(w_in, 16)
                sp.wait_ge(clear, 3)
                for w, name in ((wq, "L1_ffn_W_q"), (wk, "L1_ffn_W_k"), (wv, "L1_ffn_W_v")):
                    for r in (0, HALF):
                        sp.dma_start(w[r:r + HALF, r:r + HALF], a[name]).then_inc(w_in, 16)

            @block.tensor
            def _(pe):
                pe.wait_ge(w_in, 16 * 9)
                for k in range(2):
                    for q in range(QUARTERS):
                        last = pe.transpose(quarter(ps[k], q), m.G[:, q, k * P:(k + 1) * P], m.ident[:, :])
                last.then_inc(pe_done, 1)
                pe.wait_ge(cp_done, 1)
                for q in range(QUARTERS):
                    for k in range(2):
                        last = pe.matmul(quarter(ps[2], q), gT[:, k, q * P:(q + 1) * P], wfx[:, k, q * P:(q + 1) * P], start=(k == 0), stop=(k == 1))
                last.then_inc(pe_done, 1)
                pe.wait_ge(cp_done, 2)
                for q in range(QUARTERS):
                    last = pe.transpose(quarter(ps[3], q), tok[:, q, :], m.ident[:, :])
                last.then_inc(pe_done, 1)
                pe.wait_ge(cp_done, 3)
                pe.matmul(ps[4][:, :], wq[:, :], flat(tokT), start=True, stop=True)
                pe.matmul(ps[5][:, :], wk[:, :], flat(tokT), start=True, stop=True)
                for q in range(QUARTERS):
                    last = pe.matmul(quarter(ps[6], q), tokT[:, q, :], wv[:, :], start=True, stop=True)
                last.then_inc(pe_done, 1)
                pe.wait_ge(cp_done, 4)
                for q in range(QUARTERS):
                    last = pe.matmul(quarter(ps[7], q), qT[:, q, :], kT[:, q, :], start=True, stop=True)
                last.then_inc(pe_done, 1)
                pe.wait_ge(cp_done, 5)
                for q in range(QUARTERS):
                    last = pe.transpose(quarter(ps[0], q), attn[:, q, :], m.ident[:, :])
                last.then_inc(pe_done, 1)
                pe.wait_ge(cp_done, 6)
                for q in range(QUARTERS):
                    last = pe.matmul(quarter(ps[1], q), val[:, q, :], attnT[:, q, :], start=True, stop=True)
                last.then_inc(pe_done, 1)
                pe.wait_ge(cp_done, 7)
                for q in range(QUARTERS):
                    last = pe.matmul(ps[2 + q // 2][:, (q % 2) * D:(q % 2 + 1) * D], osT[:, q, :], wout[:, q, :], start=True, stop=True)
                last.then_inc(pe_done, 1)

            @block.vector
            def _(v):
                own = Count(own_sem)
                for w in (wq, wk, wv):
                    v.memset(w[:, :], 0.0).then_inc(clear, 1)
                own.inc(v.memset(flat(tok), 0.0))
                own.inc(v.memset(flat(attn), 0.0))
                own.inc(v.tensor_scalar(rn[:, :].unsqueeze(2), m.G[:, :, D:D + 1], 1e-5, None, ALU.add))
                own.wait(v)
                own.inc(v.reciprocal(rn[:, :], rn[:, :]))
                own.wait(v)
                v.wait_ge(pe_done, 1)
                for k in range(2):
                    own.inc(v.tensor_copy(gT[:, k, :], ps[k][:, :]))
                own.wait(v)
                v.sem_inc(cp_done, 1)
                v.wait_ge(pe_done, 2)
                for q in range(QUARTERS):
                    own.inc(v.scalar_tensor_tensor(raw[:, q, :], bfx[:, q * P:(q + 1) * P], m.G[:, q, D:D + 1], quarter(ps[2], q), ALU.mult, ALU.add))
                own.wait(v)
                for q in range(QUARTERS):
                    for r in (0, HALF):
                        own.inc(v.tensor_scalar(tok[r:r + HALF, q, r:r + HALF], raw[r:r + HALF, q, r:r + HALF], rn[r:r + HALF, q:q + 1], None, ALU.mult))
                own.wait(v)
                v.sem_inc(cp_done, 1)
                v.wait_ge(pe_done, 3)
                v.tensor_copy(flat(tokT), ps[3][:, :]).then_inc(cp_done, 1)
                v.wait_ge(pe_done, 4)
                own.inc(v.tensor_copy(flat(qT), ps[4][:, :]))
                own.inc(v.tensor_copy(flat(kT), ps[5][:, :]))
                own.inc(v.tensor_copy(flat(val), ps[6][:, :]))
                own.wait(v)
                v.sem_inc(cp_done, 1)
                v.wait_ge(pe_done, 5)
                scores = ps[7][:, :].rearrange("p (q n) -> p q n", q=QUARTERS)
                for r in (0, HALF):
                    own.inc(v.tensor_copy(dots[r:r + HALF, :, :], scores[r:r + HALF, :, r:r + HALF]))
                own.wait(v)
                own.inc(v.tensor_reduce(mx[:, :], dots[:, :, :], AX.X, ALU.max))
                own.wait(v)
                per = lambda ap: ap.unsqueeze(2).to_broadcast([P, QUARTERS, SLICES])
                v.tensor_tensor(dots[:, :, :], dots[:, :, :], per(mx[:, :]), ALU.subtract).then_inc(e_ready, 1)
                v.wait_ge(ex_ready, 1)
                own.inc(v.tensor_reduce(mx[:, :], ex[:, :, :], AX.X, ALU.add))
                own.wait(v)
                own.inc(v.reciprocal(mx[:, :], mx[:, :]))
                own.wait(v)
                for r in (0, HALF):
                    own.inc(v.tensor_tensor(attn[r:r + HALF, :, r:r + HALF], ex[r:r + HALF, :, :], per(mx[:, :])[r:r + HALF, :, :], ALU.mult))
                own.wait(v)
                v.sem_inc(cp_done, 1)
                v.wait_ge(pe_done, 6)
                v.tensor_copy(flat(attnT), ps[0][:, :]).then_inc(cp_done, 1)
                v.wait_ge(pe_done, 7)
                v.tensor_copy(flat(osT), ps[1][:, :]).then_inc(cp_done, 1)
                v.wait_ge(pe_done, 8)
                for k in range(2):
                    v.tensor_copy(m.mm[:, 2 * k:2 * k + 2, :].rearrange("p q d -> p (q d)"), ps[2 + k][:, :])

            @block.scalar
            def _(act):
                act.wait_ge(e_ready, 1)
                act.activation(flat(ex), flat(dots), ACT.Exp, scale=float(HD2) ** -0.5).then_inc(ex_ready, 1)
        m.release(mark)


def deslice(nc, m, a, out):
    with ExitStack() as c:
        sem = stage_semaphores(nc, c, "de")
        b_in, sw_ready, out_ready, x_done, own_sem, written = (sem(x) for x in ("_b", "_sw_ready", "_out_ready", "_x_done", "_own", "_written"))
        mark = m.mark()
        bo, sw = m.take([P, D]), m.take([P, 4, INNER])
        ps = [c.enter_context(nc.psum_tensor(f"de_{k}", [P, 512], F32)) for k in range(2)]
        with nc.Block() as block:
            @block.sync
            def _(sp):
                sp.dma_start(bo[:, :], row(a["L1_ffn_b_out"])).then_inc(b_in, 16)
                with sp.Fori(0, TURNS // 4) as i:
                    sp.wait_ge(x_done, i * 4 + 6)
                    sp.sem_inc(m.woken_sp, 1)
                    sp.dma_start(out[ds(i * (4 * P), 4 * P), :].rearrange("(t p) d -> p t d", p=P), m.X[:, ds(i * 4, 4), :]).then_inc(written, 16)
                sp.wait_ge(x_done, TILES + 2)
                sp.dma_start(out[(TILES - 1) * P:N, :], m.X[0:LAST, TILES - 1, :]).then_inc(written, 16)
                sp.wait_ge(written, 16 * (TURNS // 4 + 1))

            @block.scalar
            def _(act):
                def body(t, j):
                    act.wait_ge(out_ready, t + 1)
                    act.activation(sw[:, j, :], m.swT[:, ds(t, 1), :].rearrange("p o n -> p (o n)"), ACT.Copy).then_inc(sw_ready, 1)
                tiles4(act, body)

            @block.tensor
            def _(pe):
                pe.sem_inc(out_ready, 4)

                def body(t, j):
                    pe.wait_ge(sw_ready, t + 1)
                    pe.wait_ge(x_done, t + 1)
                    for q in range(QUARTERS):
                        last = pe.matmul(ps[j % 2][:, 0:D], sw[:, j, q * P:(q + 1) * P], m.mm[:, q, :], start=(q == 0), stop=(q == QUARTERS - 1))
                    last.then_inc(out_ready, 1)
                tiles4(pe, body)

            @block.vector
            def _(v):
                own = Count(own_sem)
                v.sem_inc(x_done, 2)
                v.wait_ge(b_in, 16)

                def body(t, j):
                    own.inc(v.tensor_tensor(tile_of(m.X, t), tile_of(m.X, t), bo[:, :], ALU.add))
                    own.wait(v)
                    v.wait_ge(out_ready, t + 5)
                    v.tensor_tensor(tile_of(m.X, t), tile_of(m.X, t), ps[j % 2][:, 0:D], ALU.add).then_inc(x_done, 1)
                tiles4(v, body, [(own, 1)])
        m.release(mark)


def gps_program(nc, a, out):
    m = Memory(nc)
    with m.stack:
        load_and_index(nc, m, a)
        sort_by_source(nc, m)
        stats(nc, m, m.X, "sx")
        W, lw = a["L0_gnn_W"], a["L0_gnn_loop_w"]
        mark = m.mark()
        m.kvs = m.take([P, BLOCKS * WIN])
        m.kvtail = m.take([P, HEADS * VW + WIN])
        m.kvconst = m.take([P, HEADS * VW])

        def sides(l):
            def make(nc, m, name, c):
                bank = c.enter_context(nc.psum_tensor(name + "_shared", [P, 512], F32))
                loop = LoopPart(nc, m, name, c, l, lw[l], a["L0_gnn_ln_beta"][l], a["L0_gnn_bias"][l], bank)
                if l == 0:
                    mix = MixKeys(nc, m, name, c, a, bank, loop)
                    loop.bank_taken = (mix.kv_taken, 2, 2)
                    return Side(mix, loop)
                if l == 1:
                    mix = MixQueries(nc, m, name, c, a, bank, loop)
                    loop.bank_taken = (mix.q_taken, 1, 1)
                    return Side(loop, mix)
                return Side(loop)
            return make
        for l in range(3):
            if l:
                stats(nc, m, m.AGG, f"s{l}")
            project(nc, m, f"p{l}", l, "layer" if l else "norm", [W[l, 0], W[l, 1]], a["L0_gnn_ln_gamma"][l - 1] if l else None)
            gather_sum(nc, m, f"g{l}", 0, sides(l))
        stats(nc, m, m.AGG, "s3")
        finish(nc, m, "f0", a["L0_gnn_ln_gamma"][2])
        m.release(mark)

        stats(nc, m, m.X, "sr")
        m.w1, m.w2 = m.take([P, TOP, 2, FF]), m.take([P, TOP, FB, D])
        m.gate, m.b1, m.b2 = m.take([P, TOP]), m.take([P, TOP * FB]), m.take([P, D])
        experts_mark = m.mark()
        route(nc, m, a)
        m.release(experts_mark)
        experts(nc, m)
        stats(nc, m, m.AGG, "se")
        finish(nc, m, "f1", a["L0_ffn_gamma"], a["L0_ffn_beta"])
        m.release(mark)

        m.kv = m.take([P, 2, P])
        stats(nc, m, m.X, "s4")
        project(nc, m, "p3", 3, "gcn", [a["L1_gnn_W"]], a["L1_gnn_bias"])
        load_and_index(nc, m, a, "li2", second=True)
        gather_sum(nc, m, "g3", 1, lambda nc, m, name, c: Side(LinearMix(nc, m, name, c, a)), general=False)
        combine(nc, m, a)
        m.release(mark)
        stats(nc, m, m.X, "s5")
        m.wxs, m.bxs = m.take([P, 2, INNER]), m.take([P, INNER])
        m.G, m.mm = m.take([P, QUARTERS, D + 1]), m.take([P, QUARTERS, D])
        m.swT = m.big[:, 0:TILES * INNER].rearrange("p (t n) -> p t n", t=TILES)
        slice_weights(nc, m, a)
        slice_sums(nc, m)
        slice_attention(nc, m, a)
        deslice(nc, m, a, out)


_INS = [
    "x", "src", "dst", "edge_type_2", "L0_gnn_W", "L0_gnn_bias", "L0_gnn_loop_w", "L0_gnn_ln_gamma",
    "L0_gnn_ln_beta", "L0_mix_Wqkv", "L0_mix_bqkv", "L0_mix_Wproj", "L0_mix_bproj", "L0_mix_temperature",
    "L0_ffn_Wr", "L0_ffn_br", "L0_ffn_W1", "L0_ffn_b1", "L0_ffn_W2", "L0_ffn_b2", "L0_ffn_gamma", "L0_ffn_beta",
    "L1_gnn_W", "L1_gnn_bias", "L1_mix_wq", "L1_mix_wk", "L1_mix_wv", "L1_mix_wo", "L1_mix_bo", "L1_mix_ln_k_g",
    "L1_mix_ln_k_b", "L1_mix_ln_v_g", "L1_mix_ln_v_b", "L1_ffn_W_fx", "L1_ffn_b_fx", "L1_ffn_W_x", "L1_ffn_b_x",
    "L1_ffn_W_slice", "L1_ffn_b_slice", "L1_ffn_W_q", "L1_ffn_W_k", "L1_ffn_W_v", "L1_ffn_W_out", "L1_ffn_b_out",
    "L1_ffn_temperature",
]


def kernel(**inputs):
    import numpy as _np
    import concourse.bacc as _bacc
    from concourse import mybir as _mybir
    from concourse.bass_utils import run_bass_kernel_spmd as _run

    turned = {"L0_mix_Wqkv", "L0_mix_Wproj", "L1_gnn_W", "L1_mix_wk", "L1_mix_wv", "L1_mix_wo", "L1_ffn_W_x"}
    nc = _bacc.Bacc("TRN2", target_bir_lowering=False, num_devices=1)
    arrays, args = {}, {}

    def give(name, x):
        x = _np.ascontiguousarray(x)
        arrays[f"in_{name}_dram"] = x
        args[name] = nc.dram_tensor(f"in_{name}_dram", x.shape, _mybir.dt.from_np(x.dtype), kind="ExternalInput").ap()

    for name in _INS:
        x = _np.asarray(inputs[name])
        give(name, x.T if name in turned else x)
    give("b_x_pairs", _np.asarray(inputs["L1_ffn_b_x"]).reshape(QUARTERS, P).T)
    give("ident", _np.eye(P, dtype=_np.float32))
    give("pcol", _np.arange(4 * P, dtype=_np.float32).reshape(4, P).T)
    give("valid", (_np.arange(TILES * P) < N).astype(_np.float32).reshape(TILES, P).T)
    give("coef", map_coefficients(_np))
    out = nc.dram_tensor("out_0_dram", (N, D), _mybir.dt.float32, kind="ExternalOutput").ap()
    gps_program(nc, args, out)
    r = _run(nc, [arrays], core_ids=[0])
    return r.results[0]["out_0_dram"]
```

```python
from contextlib import ExitStack, contextmanager

import concourse.bass as bass
from concourse import mybir

F32 = mybir.dt.float32
I32 = mybir.dt.int32
U32 = mybir.dt.uint32
I16 = mybir.dt.int16
BF16 = mybir.dt.bfloat16
ALU = mybir.AluOpType
ACT = mybir.ActivationFunctionType
AX = mybir.AxisListType
ds = bass.ds

P = 128
N = 3125
D = 256
E = 50000
TILES = (N + P - 1) // P
NP = TILES * P
LAST = N - (TILES - 1) * P
CHUNKS = (E + P - 1) // P
FULL = E // P
REST = E - FULL * P
PAIRS = CHUNKS + TILES - 1
TAB = 512
PAD_DST = 4095
RING = 32
STEP = 16
TURNS = TILES - 1
TAIL = PAIRS - TURNS * STEP
EPS = 1e-5


class Count:

    def __init__(self, sem):
        self.sem, self.base, self.n = sem, 0, 0

    def inc(self, ins, by=1):
        ins.then_inc(self.sem, by)
        self.n += by
        return ins

    def wait(self, eng):
        eng.wait_ge(self.sem, self.base + self.n)


@contextmanager
def turns(eng, first, end, counts):
    start = [c.base + c.n for c, _ in counts]
    with eng.Fori(first, end) as i:
        for (c, k), b in zip(counts, start):
            c.base, c.n = b + (i - first) * k, 0
        yield i
        for c, k in counts:
            assert c.n == k, (c.sem, c.n, k)
    for (c, k), b in zip(counts, start):
        c.base, c.n = b + (end - first) * k, 0


def tiles4(eng, body, counts=(), peel=1):
    looped = (TILES - peel) // 4
    with turns(eng, 0, looped, [(c, 4 * k) for c, k in counts]) as i:
        for j in range(4):
            body(i * 4 + j, j)
    for t in range(4 * looped, TILES):
        body(t, t % 4)


def is_tile(t):
    return not isinstance(t, int) or t < TILES


def stage_semaphores(nc, stack, prefix=""):
    taken = []

    @stack.callback
    def clear():
        if taken:
            nc.clear_and_free_semaphores(taken)
            nc.all_engine_barrier(sem_only=True)

    def sem(name):
        taken.append(nc.alloc_semaphore(prefix + name))
        return taken[-1]
    return sem


class Memory:

    SCRATCH = 18000

    def __init__(self, nc):
        self.nc = nc
        self.stack = ExitStack()
        sb = lambda name, shape, dt=F32: self.stack.enter_context(nc.sbuf_tensor(name, shape, dt))
        self.X = sb("X", [P, TILES, D])
        self.AGG = sb("AGG", [P, TILES, D])
        self.big = sb("big", [P, RING * D + TILES * D])
        self.ring = self.big[:, 0:RING * D].rearrange("p (s d) -> p s d", s=RING)
        self.L = self.big[:, RING * D:].rearrange("p (t d) -> p t d", t=TILES)
        self.ident, self.ones = sb("ident", [P, P]), sb("ones", [P, P])
        self.pcol, self.valid, self.eps = sb("pcol", [P, 4]), sb("valid", [P, TILES]), sb("eps", [P, 1])
        self.zeros = sb("zeros", [P, D + 1])
        self.iota = sb("iota", [P, NP], I16)
        self.dstT = sb("dstT", [P, TAB])
        self.dloc = sb("dloc", [P, TAB])
        self.idx = sb("idx", [P, 2, TAB], I32)
        self.tab = sb("tab", [1, 4, TAB], I32)
        self.ir = sb("ir", [P, RING], I32)
        self.oh = sb("oh", [P, 8, P])
        self.iotaf = sb("iotaf", [P, P])
        self.bn, self.mv4, self.mv = sb("bn", [P, 5, 6]), sb("mv4", [P, 5, 2]), sb("mv", [P, TILES, 2])
        self.std, self.rstd, self.norm = sb("std", [P, TILES]), sb("rstd", [P, TILES]), sb("norm", [P, TILES])
        self.scratch = sb("scratch", [P, self.SCRATCH])
        self.used = 0
        dram = lambda name, shape, dt=F32: nc.dram_tensor(name, shape, dt, kind="Internal").ap()
        self.t_dram = dram("t_dram", [2, TILES, P, D])
        self.xt_dram = dram("xt_dram", [4, TILES, P, D])
        self.sorted_dram = dram("sorted_dram", [E, 2], I32)
        self.gathered = [self.stack.enter_context(nc.semaphore(f"gathered{j}")) for j in range(STEP)]
        self.gather_count = [0] * STEP
        self.woken_sp = self.stack.enter_context(nc.semaphore("woken_sp"))

    def take(self, shape, dt=F32):
        n = 1
        for d in shape[1:]:
            n *= d
        n = n // 2 if dt == BF16 else n
        at, self.used = self.used, self.used + n
        assert self.used <= self.SCRATCH, self.used
        ap = self.scratch[0:shape[0], at:at + n]
        if dt != F32:
            ap = ap.bitcast(dt)
        names = "abcd"[:len(shape) - 1]
        return ap.rearrange(f"p ({' '.join(names)}) -> p {' '.join(names)}", **dict(zip(names, shape[1:]))) if len(shape) > 2 else ap

    def mark(self):
        return self.used

    def release(self, mark):
        self.used = mark

    def mean(self, t):
        return self.mv[:, ds(t, 1), 0:1].rearrange("p a b -> p (a b)")

    def rstd_of(self, t):
        return self.rstd[:, ds(t, 1)]

    def norm_of(self, t):
        return self.norm[:, ds(t, 1)]


def row(ap):
    return ap.rearrange("(o n) -> o n", o=1).to_broadcast([P, ap.shape[0]])


def by_half(ap):
    return ap.rearrange("(k p) n -> p k n", p=P)


def load_and_index(nc, m, a, name="li", second=False):
    with ExitStack() as c:
        sem = stage_semaphores(nc, c)
        in_nat, in_const, in_x = sem(name + "in_nat"), sem(name + "in_const"), sem(name + "in_x")
        s_cleared, s_own, s_tr = sem(name + "cleared"), sem(name + "dve_own"), sem(name + "turned")
        s_b, s_f = sem(name + "diag_ready"), sem(name + "rows_ready")
        mark = m.mark()
        nat = m.take([P, 4, 4, P], I32)
        key = 2
        if second:
            both = m.take([P, 4, 2 * P], I32)
            nat, key = both.rearrange("p q (e k) -> p k q e", k=2), 0
        natf = m.take([P, 3, 4, P], F32)
        inv = m.take([P, TAB], F32)
        small = m.take([P, 64], F32)
        smalli = m.take([P, 16], I32)
        gb = m.take([P, TAB], F32)
        trn = m.take([P, 4, P], F32)
        tab = m.take([P, 3, 4], F32)
        diag = m.take([P, 3, 4, P])
        psT = [c.enter_context(nc.psum_tensor(f"{name}_t{k}", [P, TAB], F32)) for k in range(3)]
        psG = c.enter_context(nc.psum_tensor(name + "_g", [P, TAB], F32))
        psD = c.enter_context(nc.psum_tensor(name + "_d", [P, TAB], F32))
        sel = m.take([P, 4, TAB])
        psF = c.enter_context(nc.psum_tensor(name + "_f", [P, 1], F32))
        last_p = FULL - 3 * P
        with nc.Block() as block:
            @block.sync
            def _(sp):
                if second:
                    sp.wait_ge(s_cleared, 1)
                    flat = m.sorted_dram.rearrange("e k -> (e k)")
                    n3, line = 3 * P * P * 2, 2 * P
                    sp.dma_start(both[:, 0:3, :], flat[0:n3].rearrange("(q p e) -> p q e", p=P, e=line)).then_inc(in_nat, 16)
                    sp.dma_start(both[0:last_p, 3, :], flat[n3:FULL * line].rearrange("(p e) -> p e", e=line)).then_inc(in_nat, 16)
                    sp.dma_start(both[last_p:last_p + 1, 3, 0:2 * REST],
                                 flat[FULL * line:2 * E].rearrange("(o e) -> o e", o=1)).then_inc(in_nat, 16)
                    return
                sp.dma_start(m.ident[:, :], a["ident"]).then_inc(in_const, 16)
                sp.dma_start(m.pcol[:, :], a["pcol"]).then_inc(in_const, 16)
                sp.dma_start(m.valid[:, :], a["valid"]).then_inc(in_const, 16)
                sp.wait_ge(s_cleared, 2)
                for k, (src, off) in enumerate(((a["src"], 0), (a["edge_type_2"], 0), (a["dst"], 0), (a["dst"], 1))):
                    n3, nr = 3 * P * P, E - off
                    if off:
                        sp.dma_start(nat[:, k, 0:3, :], src[off:off + n3].rearrange("(q p e) -> p q e", p=P, e=P)).then_inc(in_nat, 16)
                        sp.dma_start(nat[0:last_p, k, 3, :], src[off + n3:off + FULL * P].rearrange("(p e) -> p e", e=P)).then_inc(in_nat, 16)
                    else:
                        sp.dma_start(nat[:, k, 0:3, :], src[0:n3].rearrange("(q p e) -> p q e", p=P, e=P)).then_inc(in_nat, 16)
                        sp.dma_start(nat[0:last_p, k, 3, :], src[n3:FULL * P].rearrange("(p e) -> p e", e=P)).then_inc(in_nat, 16)
                    rest = REST - off
                    sp.dma_start(nat[last_p:last_p + 1, k, 3, 0:rest],
                                 src[FULL * P + off:E].rearrange("(o e) -> o e", o=1)).then_inc(in_nat, 16)
                sp.wait_ge(s_cleared, 5)
                sp.dma_start(m.X[:, 0:TILES - 1, :], a["x"][0:(TILES - 1) * P, :].rearrange("(t p) d -> p t d", p=P)).then_inc(in_x, 16)
                sp.dma_start(m.X[0:LAST, TILES - 1, :], a["x"][(TILES - 1) * P:N, :]).then_inc(in_x, 16)
                sp.wait_ge(in_x, 32)

            @block.gpsimd
            def _(pool):
                if second:
                    pool.memset(both[:, :, :], PAD_DST).then_inc(s_cleared, 1)
                    return
                pool.memset(nat[:, 2:4, :, :], PAD_DST).then_inc(s_cleared, 1)
                pool.memset(nat[:, 0:2, :, :], 0).then_inc(s_cleared, 1)
                pool.iota(m.iota[:, :], [[1, NP]], base=0, channel_multiplier=0).then_inc(s_cleared, 1)
                pool.memset(m.ring[:, :, :], 0.0).then_inc(s_cleared, 1)
                pool.memset(m.X[:, TILES - 1, :], 0.0).then_inc(s_cleared, 1)
                pool.memset(m.zeros[:, :], 0.0).then_inc(s_cleared, 1)
                pool.memset(m.AGG[:, :, :], 0.0).then_inc(s_cleared, 1)

            @block.vector
            def _(v):
                own = Count(s_own)
                if second:
                    v.wait_ge(in_nat, 16 * 3)
                    own.inc(v.tensor_scalar(natf[:, 1, :, :], nat[:, 1, :, :], float(NP - 1), None, ALU.min))
                    own.inc(v.memset(inv[:, :], 0.0))
                else:
                    own.inc(v.memset(m.ones[:, :], 1.0))
                    own.inc(v.memset(m.eps[:, :], EPS))
                    own.wait(v)
                    v.wait_ge(in_nat, 16 * 12)
                    v.wait_ge(s_cleared, 3)
                    own.inc(v.tensor_copy(m.iotaf[:, :], m.iota[:, 0:P]))
                    v.wait_ge(in_const, 48)
                    own.inc(v.tensor_copy(natf[:, 0, :, :], nat[:, 1, :, :]))
                    own.inc(v.tensor_copy(natf[:, 1, :, :], nat[:, 0, :, :]))
                    own.inc(v.tensor_copy(inv[:, :].rearrange("p (q e) -> p q e", q=4), nat[:, 3, :, :]))
                own.inc(v.tensor_copy(natf[:, 2, :, :], nat[:, key, :, :]))
                own.inc(v.tensor_single_scalar(smalli[:, 0:4], nat[:, key, :, P - 1], 7, ALU.arith_shift_right))
                own.wait(v)
                own.inc(v.tensor_copy(small[:, 0:4], smalli[:, 0:4]))
                if not second:
                    own.inc(v.scalar_tensor_tensor(natf[:, 0, :, :], natf[:, 0, :, :], float(NP), natf[:, 1, :, :], ALU.mult, ALU.add))
                    own.inc(v.tensor_tensor(inv[:, :].rearrange("p (q e) -> p q e", q=4), natf[:, 2, :, :],
                                            inv[:, :].rearrange("p (q e) -> p q e", q=4), ALU.is_gt))
                own.wait(v)
                own.inc(v.tensor_tensor(small[:, 4:8], small[:, 0:4], m.pcol[:, :], ALU.add))
                own.inc(v.tensor_reduce(small[:, 8:9], inv[:, :], AX.X, ALU.add))
                own.wait(v)
                for q in range(4):
                    own.inc(v.tensor_scalar(trn[:, q, :], m.ident[:, :], small[:, 4 + q:5 + q], None, ALU.mult))
                own.wait(v)
                v.sem_inc(s_b, 1)
                v.wait_ge(s_tr, 3)
                if not second:
                    own.inc(v.tensor_copy(m.idx[:, 0, :], psT[0][:, :]))
                own.inc(v.tensor_copy(m.idx[:, 1, :], psT[1][:, :]))
                own.inc(v.tensor_copy(m.dstT[:, :], psT[2][:, :]))
                v.wait_ge(s_f, 1)
                own.inc(v.tensor_copy(gb[:, :], psG[:, :]))
                own.inc(v.tensor_scalar(small[:, 9:10], psF[:, :], 1.0, None, ALU.min))
                own.wait(v)
                own.inc(v.tensor_scalar(small[:, 10:11], small[:, 9:10], -1.0, 1.0, ALU.mult, ALU.add))
                own.inc(v.tensor_scalar(small[:, 12:16], m.pcol[:, :], float(CHUNKS), None, ALU.min))
                for q in range(4):
                    own.inc(v.tensor_scalar(inv[:, :], gb[:, :], m.pcol[:, q:q + 1], 0.0, ALU.is_lt, ALU.add,
                                            accum_out=small[:, 16 + q:17 + q]))
                    own.wait(v)
                own.inc(v.tensor_scalar(small[:, 20:24], small[:, 16:20], float(CHUNKS), small[:, 10:11], ALU.min, ALU.mult))
                own.inc(v.tensor_tensor(small[:, 24:28], m.pcol[:, :], small[:, 16:20], ALU.subtract))
                own.wait(v)
                own.inc(v.scalar_tensor_tensor(tab[:, 0, :], small[:, 12:16], small[:, 9:10], small[:, 20:24], ALU.mult, ALU.add))
                own.inc(v.tensor_scalar(small[:, 24:28], small[:, 24:28], small[:, 10:11], None, ALU.mult))
                own.wait(v)
                own.inc(v.tensor_scalar(tab[:, 1, :], small[:, 24:28], 0.0, float(TILES - 1), ALU.max, ALU.min))
                own.inc(v.tensor_scalar(tab[:, 2, :], m.pcol[:, :], 0.0, small[:, 9:10], ALU.mult, ALU.add))
                own.wait(v)
                for k in range(3):
                    for q in range(4):
                        own.inc(v.tensor_scalar(diag[:, k, q, :], m.ident[:, :], tab[:, k, q:q + 1], None, ALU.mult))
                own.wait(v)
                v.sem_inc(s_b, 1)
                v.wait_ge(s_f, 2)
                for k in range(3):
                    own.inc(v.tensor_copy(m.tab[0:1, k, :], psT[k][0:1, :]))
                own.wait(v)
                own.inc(v.tensor_single_scalar(m.tab[0:1, 3, :], m.tab[0:1, 0, :], RING - 1, ALU.bitwise_and))
                for q in range(4):
                    own.inc(v.tensor_scalar(sel[:, q, :], psT[0][:, :], m.pcol[:, q:q + 1], None, ALU.is_equal))
                own.inc(v.tensor_scalar(inv[:, :], psT[1][:, :], -float(P), None, ALU.mult))
                own.wait(v)
                v.sem_inc(s_b, 1)
                v.wait_ge(s_f, 3)
                own.inc(v.tensor_tensor(m.dloc[:, :], psD[:, :], inv[:, :], ALU.add))

            @block.tensor
            def _(pe):
                if not second:
                    pe.wait_ge(in_const, 48)
                pe.wait_ge(s_b, 1)
                if second:
                    pe.sem_inc(s_tr, 1)
                for k in range(1 if second else 0, 3):
                    for q in range(4):
                        last = pe.transpose(psT[k][:, q * P:(q + 1) * P], natf[:, k, q, :], m.ident[:, :])
                    last.then_inc(s_tr, 1)
                for q in range(4):
                    pe.matmul(psG[:, q * P:(q + 1) * P], m.ones[:, :], trn[:, q, :], start=True, stop=True)
                pe.matmul(psF[:, :], m.ones[:, :], small[:, 8:9], start=True, stop=True).then_inc(s_f, 1)
                pe.wait_ge(s_b, 2)
                for k in range(3):
                    for q in range(4):
                        last = pe.matmul(psT[k][:, q * P:(q + 1) * P], m.ones[:, :], diag[:, k, q, :], start=True, stop=True)
                last.then_inc(s_f, 1)
                pe.wait_ge(s_b, 3)
                for q in range(4):
                    last = pe.matmul(psD[:, :], natf[:, 2, q, :], sel[:, q, :], start=(q == 0), stop=(q == 3))
                last.then_inc(s_f, 1)

            @block.scalar
            def _(act):
                act.wait_ge(s_cleared, 1 if second else 7)
        m.release(mark)


class Send:
    SCATTER = 8

    def __init__(self, m):
        self.m, self.blocks = m, 0
        self.all, self.place = m.take([P, TAB, 2], I32), m.take([P, TAB], I32)
        self.now, self.at = m.take([P, 2, self.SCATTER, 2], I32), m.take([P, 2, self.SCATTER], I32)
        sem = lambda name: m.stack.enter_context(m.nc.semaphore(name))
        self.left, self.ready, self.woken = [sem(f"edges_left{k}") for k in range(2)], Count(sem("send_ready")), sem("woken_send")

    def prepare(self, pool, block, k, n=SCATTER):
        if not isinstance(block, int) or block >= 2:
            pool.wait_ge(self.left[k], (block - k) * (16 * self.SCATTER // 2))
            pool.sem_inc(self.woken, 1)
        self.ready.inc(pool.tensor_copy(self.at[:, k, 0:n], self.place[:, ds(block * self.SCATTER, n)]))
        self.ready.inc(pool.tensor_copy(self.now[:, k, 0:n, :], self.all[:, ds(block * self.SCATTER, n), :]))
        self.ready.wait(pool)
        pool.sem_inc(self.woken, 1)

    def chunk(self, pool, k, j, rows=P):
        pool.indirect_dma_start(self.m.sorted_dram, bass.IndirectOffsetOnAxis(ap=self.at[0:rows, k, j:j + 1], axis=0),
                                self.now[0:rows, k, j, :], None).then_inc(self.left[k], 16)

    def pair(self, pool, i):
        for k in range(2):
            self.prepare(pool, i * 2 + k, k)
            for j in range(self.SCATTER):
                self.chunk(pool, k, j)

    def some(self, pool, pairs):
        first, end = self.blocks // 2, self.blocks // 2 + pairs
        if not first:
            self.pair(pool, 0)
        with turns(pool, max(first, 1), end, [(self.ready, 4)]) as i:
            self.pair(pool, i)
        self.blocks = 2 * end

    def rest(self, pool):
        S = self.SCATTER
        full = CHUNKS // (2 * S)
        with turns(pool, self.blocks // 2, full, [(self.ready, 4)]) as i:
            self.pair(pool, i)
        for k in range(2):
            n = min(S, max(0, CHUNKS - (2 * full + k) * S))
            if n:
                self.prepare(pool, 2 * full + k, k, n)
            for j in range(n):
                self.chunk(pool, k, j, REST if (2 * full + k) * S + j == CHUNKS - 1 else P)
            pool.wait_ge(self.left[k], 16 * (full * S + n))


def sort_by_source(nc, m):
    GROUP = 16
    with ExitStack() as c:
        sem = stage_semaphores(nc, c, "so")
        b_ready, t_done, t_ready, base_done, dg_ready, w_done, w_taken, root = (
            sem(x) for x in ("_b", "_t", "_t_ready", "_base", "_dg", "_w", "_w_taken", "_root"))
        oh_ready, oh_used, dve_own = (sem(x) for x in ("_oh", "_oh_used", "_own"))
        mark = m.mark()
        take = m.take
        cells = CHUNKS * TILES
        hot = m.big[:, 0:(cells + 1) // 2].bitcast(BF16)[:, 0:cells].rearrange("p (c r) -> p c r", r=TILES)
        diag = m.big[:, cells:cells + P * TILES].rearrange("p (c r) -> p c r", r=TILES)
        tile_f, low, tile_i = take([P, TAB]), take([P, TAB]), take([P, TAB], I32)
        place, pairs = take([P, TAB]), m.send.all
        before, before_h = take([P, P]), take([P, P], BF16)
        ones_h, oh = take([P, 2], BF16), take([P, 8, P], BF16)
        counts, base = take([P, 4, TILES]), take([P, 4, TILES])
        lower, lower_sum = take([P, TILES, TILES]), take([P, TILES])
        prod = take([P, 2, GROUP * TILES])
        ps = lambda x: c.enter_context(nc.psum_tensor("so" + x, [P, 512], F32))
        psW, psT, psB, psN = [ps(f"_w{k}") for k in range(4)], ps("_t"), ps("_b"), ps("_n")
        blocks = [(q, min(P, CHUNKS - q * P)) for q in range(4)]
        groups = [(q, c0, min(GROUP, q * P + nq - c0)) for q, nq in blocks for c0 in range(q * P, q * P + nq, GROUP)]
        over_r = lambda ap, n: ap.unsqueeze(2).to_broadcast([P, n, TILES])
        over_c = lambda ap, n: ap.unsqueeze(1).to_broadcast([P, n, TILES])
        with nc.Block() as block:
            @block.vector
            def _(v):
                own = Count(dve_own)
                src = m.idx[:, 1, :]
                own.inc(v.tensor_single_scalar(tile_i[:, :], src, 7, ALU.arith_shift_right))
                own.inc(v.tensor_copy(low[:, :], src))
                own.inc(v.tensor_copy(pairs[:, :, 0:1].rearrange("p c o -> p (c o)"), src))
                own.inc(v.tensor_copy(pairs[:, :, 1:2].rearrange("p c o -> p (c o)"), m.dstT[:, :]))
                own.inc(v.tensor_scalar(before[:, :], m.iotaf[:, :], m.pcol[:, 0:1], None, ALU.is_gt))
                own.inc(v.tensor_scalar(place[:, :], m.dstT[:, :], float(PAD_DST), 64.0, ALU.is_equal, ALU.mult))
                own.inc(v.tensor_scalar(before_h[:, :], m.iotaf[:, :], m.pcol[:, 0:1], None, ALU.is_gt))
                own.inc(v.memset(counts[:, :, :], 0.0))
                own.inc(v.memset(ones_h[:, :], 1.0))
                own.wait(v)
                own.inc(v.tensor_copy(tile_f[:, :], tile_i[:, :]))
                own.wait(v)
                own.inc(v.scalar_tensor_tensor(low[:, :], tile_f[:, :], -float(P), low[:, :], ALU.mult, ALU.add))
                own.inc(v.tensor_tensor(tile_f[:, :], tile_f[:, :], place[:, :], ALU.add))
                own.wait(v)
                for q, nq in blocks:
                    v.tensor_tensor(hot[:, q * P:q * P + nq, :], over_r(tile_f[:, q * P:q * P + nq], nq),
                                    over_c(m.iotaf[:, 0:TILES], nq), ALU.is_equal).then_inc(b_ready, 1)
                v.wait_ge(t_done, 1)
                for q, nq in blocks:
                    own.inc(v.tensor_copy(counts[0:nq, q, :], psT[0:nq, q * TILES:(q + 1) * TILES]))
                own.inc(v.tensor_tensor(lower[:, :, :], over_r(m.iotaf[:, 0:TILES], TILES), over_c(m.iotaf[:, 0:TILES], TILES), ALU.is_gt))
                own.wait(v)
                v.sem_inc(t_ready, 1)
                v.wait_ge(base_done, 1)
                own.inc(v.tensor_tensor(lower[:, :, :], lower[:, :, :], over_c(psB[:, 4 * TILES:5 * TILES], TILES), ALU.mult))
                own.wait(v)
                own.inc(v.tensor_reduce(lower_sum[:, :], lower[:, :, :], AX.X, ALU.add))
                own.wait(v)
                own.inc(v.tensor_tensor(base[:, :, :], psB[:, 0:4 * TILES].rearrange("p (q r) -> p q r", q=4), over_c(lower_sum[:, :], 4), ALU.add))
                own.wait(v)
                g = 0

                def low_hot(d):
                    n = min(4, CHUNKS - 4 * d)
                    if n > 0:
                        v.wait_ge(oh_used, d + 1)
                        v.tensor_tensor(oh[:, 4 * (d % 2):4 * (d % 2) + n, :], m.iotaf[:, :].unsqueeze(1).to_broadcast([P, n, P]),
                                        low[:, 4 * d:4 * d + n].unsqueeze(2).to_broadcast([P, n, P]), ALU.is_equal).then_inc(oh_ready, 1)
                for q, nq in blocks:
                    if g:
                        v.wait_ge(w_done, g)
                    v.tensor_tensor(diag[:, 0:nq, :], over_r(m.ident[:, 0:nq], nq), over_c(base[:, q, :], nq), ALU.mult).then_inc(dg_ready, 1)
                    for _, c0, n in [x for x in groups if x[0] == q]:
                        v.wait_ge(w_done, g + 1)
                        pr = prod[:, g % 2, 0:n * TILES].rearrange("p (c r) -> p c r", r=TILES)
                        v.tensor_tensor(pr, hot[:, c0:c0 + n, :], psW[g % 4][:, 0:n * TILES].rearrange("p (c r) -> p c r", r=TILES),
                                        ALU.mult).then_inc(w_taken, 1)
                        v.wait_ge(w_taken, g + 5)
                        own.inc(v.tensor_reduce(place[:, c0:c0 + n], pr, AX.X, ALU.add))
                        for d in range(4 * g, 4 * g + 4):
                            low_hot(d)
                        g += 1
                own.wait(v)
                v.tensor_copy(m.send.place[:, 0:CHUNKS], place[:, 0:CHUNKS])
                v.wait_ge(root, 1)
                v.reciprocal(m.norm[:, :], m.norm[:, :])

            @block.tensor
            def _(pe):
                pe.sem_inc(w_taken, 4)
                pe.sem_inc(oh_used, 2)
                for q, nq in blocks:
                    pe.wait_ge(b_ready, q + 1)
                    for r in range(TILES):
                        last = pe.matmul(psT[0:nq, q * TILES + r:q * TILES + r + 1], hot[:, q * P:q * P + nq, r:r + 1].rearrange("p c o -> p (c o)"),
                                         ones_h[:, 0:1], start=True, stop=True)
                last.then_inc(t_done, 1)
                pe.wait_ge(t_ready, 1)
                for q in range(4):
                    for k in range(q + 1):
                        pe.matmul(psB[:, q * TILES:(q + 1) * TILES], m.ones[:, :] if k < q else before[:, :], counts[:, k, :], start=(k == 0), stop=(k == q))
                for k in range(4):
                    last = pe.matmul(psB[:, 4 * TILES:5 * TILES], m.ones[:, :], counts[:, k, :], start=(k == 0), stop=(k == 3))
                last.then_inc(base_done, 1)
                for g, (q, c0, n) in enumerate(groups):
                    pe.wait_ge(dg_ready, q + 1)
                    pe.wait_ge(w_taken, g + 1)
                    rows = lambda ap: ap.rearrange("p c r -> p (c r)")
                    pe.matmul(psW[g % 4][:, 0:n * TILES], before_h[:, :], rows(hot[:, c0:c0 + n, :]), start=True, stop=False)
                    pe.matmul(psW[g % 4][:, 0:n * TILES], m.ones[:, :], rows(diag[:, c0 - q * P:c0 - q * P + n, :]), start=False, stop=True).then_inc(w_done, 1)
                    for d in range(4 * g, min(4 * g + 4, (CHUNKS + 3) // 4)):
                        pe.wait_ge(oh_ready, d + 1)
                        for ch in range(4 * d, min(4 * d + 4, CHUNKS)):
                            last = pe.matmul(psN[:, 0:TILES], oh[:, ch % 8, :], hot[:, ch, :], start=(ch == 0), stop=(ch == CHUNKS - 1))
                        last.then_inc(oh_used, 1)

            @block.scalar
            def _(act):
                act.wait_ge(oh_used, 2 + (CHUNKS + 3) // 4)
                act.activation(m.norm[:, :], psN[:, 0:TILES], ACT.Sqrt, bias=m.ones[:, 0:1]).then_inc(root, 1)
        m.release(mark)


def stats(nc, m, source, name):
    with ExitStack() as c:
        s_own, s_var, s_sq, s_woken = map(stage_semaphores(nc, c, name), ("_own", "_var", "_sqrt", "_woken"))
        with nc.Block() as block:
            @block.vector
            def _(v):
                own = Count(s_own)

                def group(t0, n):
                    for j in range(n):
                        own.inc(v.bn_stats(m.bn[:, j, :], tile_of(source, t0 + j)))
                    own.wait(v)
                    v.sem_inc(s_woken, 1)
                    for j in range(n):
                        own.inc(v.bn_aggr(m.mv4[:, j, :], m.bn[:, j, :]))
                    own.wait(v)
                    own.inc(v.tensor_copy(m.mv[:, ds(t0, n), :], m.mv4[:, 0:n, :]))
                with turns(v, 0, TILES // 5, [(own, 11)]) as i:
                    group(i * 5, 5)
                own.wait(v)
                v.sem_inc(s_var, 1)
                v.wait_ge(s_sq, 1)
                v.reciprocal(m.rstd[:, :], m.std[:, :])

            @block.scalar
            def _(act):
                act.wait_ge(s_var, 1)
                act.activation(m.std[:, :], m.mv[:, :, 1], ACT.Sqrt, bias=m.eps[:, 0:1]).then_inc(s_sq, 1)


def tile_of(buf, t, cols=D):
    return buf[:, ds(t, 1), 0:cols].rearrange("p o d -> p (o d)")


def is_last(t):
    return isinstance(t, int) and t == TILES - 1


def project(nc, m, name, layer_no, kind, weights, vector=None):
    cols = D * len(weights)
    gcn, layer = kind == "gcn", kind == "layer"
    with ExitStack() as c:
        sem = stage_semaphores(nc, c, name)
        w_in, dve_own, h_ready, h_free = sem("_w_in"), sem("_dve"), sem("_h_ready"), sem("_h_free")
        xt_done, prod_done, st_done = sem("_xt_done"), sem("_prod_done"), sem("_st_done")
        st_out = [sem(f"_st_out{j}") for j in range(4)]
        xt_out = [sem(f"_xt_out{j}") for j in range(4)]
        mark = m.mark()
        w = m.take([P, 2, cols])
        vec = m.take([P, D]) if vector is not None else None
        h = m.take([P, 2, D])
        tmp = m.take([P, 2, D])
        xt = m.take([P, 4, D])
        stage = None if gcn else m.take([P, 4, cols])
        psT = [c.enter_context(nc.psum_tensor(f"{name}_t{k}", [P, 512], F32)) for k in range(2)]
        psW = [c.enter_context(nc.psum_tensor(f"{name}_w{k}", [P, 512], F32)) for k in range(2)]
        n_in = 16 * (len(weights) + (vector is not None))
        with nc.Block() as block:
            if not gcn:
                @block.gpsimd
                def _(pool):
                    m.send.some(pool, 4)

            @block.sync
            def _(sp):
                for k, wk in enumerate(weights):
                    sp.dma_start(w[:, :, k * D:(k + 1) * D], by_half(wk)).then_inc(w_in, 16)
                if vector is not None:
                    sp.dma_start(vec[:, :], row(vector)).then_inc(w_in, 16)

                def body(t, j):
                    sp.wait_ge(xt_done, t + 3)
                    sp.sem_inc(m.woken_sp, 1)
                    sp.dma_start(m.xt_dram[layer_no, ds(t, 1), :, :].rearrange("o p d -> (o p) d"), xt[:, j, :]).then_inc(xt_out[j], 16)
                    sp.wait_ge(st_done, t + 3)
                    sp.sem_inc(m.woken_sp, 1)
                    if gcn:
                        sp.dma_start(m.t_dram[0, ds(t, 1), :, :].rearrange("o p d -> (o p) d"), tile_of(m.AGG, t)).then_inc(st_out[j], 16)
                    else:
                        sp.dma_start(m.t_dram[:, ds(t, 1), :, :].rearrange("r o p d -> p (r o) d"),
                                     stage[:, j, :].rearrange("p (r d) -> p r d", r=2)).then_inc(st_out[j], 16)
                tiles4(sp, body)
                for j in range(4):
                    sp.wait_ge(xt_out[j], 16 * (TURNS // 4 + (j == 0) + 1))
                    sp.wait_ge(st_out[j], 16 * (TURNS // 4 + (j == 0) + 1))

            @block.vector
            def _(v):
                own = Count(dve_own)
                v.wait_ge(w_in, n_in)
                if gcn:
                    v.sem_inc(st_done, 2)

                def make_h(t, j):
                    src = tile_of(m.AGG if layer else m.X, t)
                    v.wait_ge(h_free, t + 1)
                    if layer:
                        own.inc(v.tensor_scalar(tmp[:, 0, :], src, m.mean(t), m.rstd_of(t), ALU.subtract, ALU.mult))
                        own.wait(v)
                        own.inc(v.tensor_tensor(tmp[:, 1, :], tmp[:, 0, :], vec[:, :], ALU.mult))
                        v.tensor_copy(tile_of(m.AGG, t), m.zeros[:, 0:D])
                        own.wait(v)
                        v.tensor_tensor(h[:, j % 2, :], tmp[:, 1, :], tile_of(m.L, t), ALU.add).then_inc(h_ready, 1)
                    else:
                        v.tensor_scalar(h[:, j % 2, :], src, m.mean(t), m.rstd_of(t), ALU.subtract, ALU.mult).then_inc(h_ready, 1)

                def scale_rows(t, j):
                    if not is_last(t):
                        make_h(t + 1, (j + 1) % 4)
                    v.wait_ge(prod_done, t + 1)
                    own.inc(v.tensor_tensor(tmp[:, j % 2, :], psW[j % 2][:, 0:D], vec[:, :], ALU.add))
                    own.wait(v)
                    v.tensor_scalar(tile_of(m.AGG, t), tmp[:, j % 2, :], m.norm_of(t), None, ALU.mult).then_inc(st_done, 1)

                if gcn:
                    make_h(0, 0)
                    tiles4(v, scale_rows, [(own, 1)])
                else:
                    tiles4(v, make_h, [(own, 2)] if layer else [])

            @block.tensor
            def _(pe):
                pe.sem_inc(h_free, 2)
                pe.wait_ge(w_in, n_in)

                def transposes(t, j):
                    pe.wait_ge(h_ready, t + 1)
                    pe.wait_ge(xt_done, t + 1)
                    for k in range(2):
                        last = pe.transpose(psT[j % 2][:, k * P:(k + 1) * P], h[:, j % 2, k * P:(k + 1) * P], m.ident[:, :])
                    last.then_inc(h_free, 1)

                def product(t, j):
                    if not is_last(t) and not gcn:
                        transposes(t + 1, (j + 1) % 4)
                    pe.wait_ge(xt_done, t + 3)
                    pe.wait_ge(st_done, t + 1)
                    for k in range(2):
                        last = pe.matmul(psW[j % 2][:, 0:cols], xt[:, j, k * P:(k + 1) * P], w[:, k, :], start=(k == 0), stop=(k == 1))
                    last.then_inc(prod_done, 1)
                    if not is_last(t) and gcn:
                        transposes(t + 1, (j + 1) % 4)
                transposes(0, 0)
                tiles4(pe, product)

            @block.scalar
            def _(act):
                act.sem_inc(xt_done, 2)
                if not gcn:
                    act.sem_inc(st_done, 2)
                for j in range(4):
                    act.sem_inc(xt_out[j], 16)
                    act.sem_inc(st_out[j], 16)

                def copy_xt(t, j):
                    act.wait_ge(h_free, t + 3)
                    act.wait_ge(xt_out[j], 16 * (t // 4 + 1) if isinstance(t, int) else (t - j) * 4 + 16)
                    act.activation(xt[:, j, :], psT[j % 2][:, 0:D], ACT.Relu if layer else ACT.Copy).then_inc(xt_done, 1)

                def copy_rows(t, j):
                    if not is_last(t):
                        copy_xt(t + 1, (j + 1) % 4)
                    if not gcn:
                        act.wait_ge(prod_done, t + 1)
                        act.wait_ge(st_out[j], 16 * (t // 4 + 1) if isinstance(t, int) else (t - j) * 4 + 16)
                        act.activation(stage[:, j, :], psW[j % 2][:, :], ACT.Copy).then_inc(st_done, 1)
                    else:
                        act.wait_ge(prod_done, t + 1)
                copy_xt(0, 0)
                tiles4(act, copy_rows)
        m.release(mark)


def gather_sum(nc, m, name, src_col, side, general=True, banks=2):
    width = D
    gathered = m.gathered
    with ExitStack() as c:
        sem = stage_semaphores(nc, c, name)
        oh_ready, mm_done, agg_done = sem("_oh_ready"), sem("_mm_done"), sem("_agg_done")
        pool_own, woken = sem("_pool"), sem("_woken")
        g_woken, g_idx, g_in, g_oh, g_mm, g_add = (sem(x) for x in ("_g_woken", "_g_idx", "_g_in", "_g_oh", "_g_mm", "_g_add"))
        mark = m.mark()
        pp = [c.enter_context(nc.psum_tensor(f"{name}_pair{k}", [P, 512], F32))[:, 0:width] for k in range(banks)]
        bank = [j % banks if STEP % banks == 0 or j < STEP - 1 else 1 for j in range(STEP)]
        ago = [next(n for n in range(1, STEP) if bank[(j - n) % STEP] == bank[j]) for j in range(STEP)]
        side = side(nc, m, name, c)
        rows = m.t_dram.rearrange("r t p d -> (r t p) d")
        base = [m.gather_count[j] for j in range(STEP)]
        for j in range(STEP):
            m.gather_count[j] += 16 * (CHUNKS // STEP + (j < CHUNKS % STEP))
        with nc.Block() as block:
            @block.gpsimd
            def _(pool):
                own = Count(pool_own)

                def half(c0, k, n):
                    pool.wait_ge(mm_done, c0 + 1)
                    pool.sem_inc(woken, 1)
                    own.inc(pool.tensor_copy(m.ir[:, k * STEP:(k + 1) * STEP], m.idx[:, src_col, ds(c0, STEP)]))
                    own.wait(pool)
                    for j in range(n):
                        pool.wait_ge(mm_done, c0 + j + 1)
                        pool.sem_inc(woken, 1)
                        pool.indirect_dma_start(m.ring[:, k * STEP + j, 0:D], None, rows,
                                                bass.IndirectOffsetOnAxis(ap=m.ir[:, k * STEP + j:k * STEP + j + 1], axis=0)
                                                ).then_inc(gathered[j], 16)
                with turns(pool, 0, CHUNKS // RING, [(own, 2)]) as i:
                    half(i * RING, 0, STEP)
                    half(i * RING + STEP, 1, STEP)
                half(CHUNKS // RING * RING, 0, CHUNKS % RING)

                if general:
                    unsorted = pool.value_load(m.tab[0:1, 2, 0:1], min_val=0, max_val=1)
                    with pool.If(unsorted > 0):
                        pool.wait_ge(g_add, 1)
                        with pool.Fori(0, CHUNKS) as ch:
                            pool.wait_ge(g_mm, ch * (TILES - 1) + 1)
                            pool.sem_inc(woken, 1)
                            pool.tensor_copy(m.ir[:, 0:1], m.idx[:, src_col, ds(ch, 1)]).then_inc(g_idx, 1)
                            pool.wait_ge(g_idx, ch + 1)
                            pool.sem_inc(woken, 1)
                            pool.indirect_dma_start(m.ring[:, 0, 0:D], None, rows,
                                                    bass.IndirectOffsetOnAxis(ap=m.ir[:, 0:1], axis=0)).then_inc(g_in, 16)

            @block.vector
            def _(v):
                v.sem_inc(agg_done, 4)

                def one_hots(p, g):
                    v.tensor_tensor(m.oh[:, 4 * (g % 2):4 * (g % 2) + 4, :], m.iotaf[:, :].unsqueeze(1).to_broadcast([P, 4, P]),
                                    m.dloc[:, ds(p, 4)].unsqueeze(2).to_broadcast([P, 4, P]), ALU.is_equal).then_inc(oh_ready, 1)

                def add(p, j, t):
                    v.wait_ge(mm_done, p + 9)
                    v.wait_ge(agg_done, p + 4)
                    v.tensor_tensor(tile_of(m.AGG, t, width), tile_of(m.AGG, t, width), pp[bank[j % STEP]], ALU.add).then_inc(agg_done, 1)

                def pairs(i, n):
                    p = i * STEP
                    tiles = load_row(nc, v, m.tab[0:1, 1, ds(p, STEP)], TILES - 1)
                    for j in range(n):
                        if j % 4 == 0 and (not isinstance(i, int) or p + j + 4 < PAIRS):
                            one_hots(p + j + 4, j // 4 + 1)
                        add(p + j, j, tiles[j])
                        if side and not (isinstance(i, int) and i > TURNS):
                            side.vector(v, i, j)
                one_hots(0, 0)
                if side:
                    side.before_vector(v)
                with turns(v, 0, TURNS, side.vector_counts if side else []) as i:
                    pairs(i, STEP)
                pairs(TURNS, STEP)
                pairs(TURNS + 1, TAIL - STEP)
                if side:
                    side.after_vector(v)
                v.wait_ge(agg_done, PAIRS + 4)

                if general:
                    unsorted = v.value_load(m.tab[0:1, 2, 0:1], min_val=0, max_val=1)
                    with v.If(unsorted > 0):
                        v.sem_inc(g_add, 1)
                        with v.Fori(0, CHUNKS) as ch:
                            with v.Fori(0, TILES - 1) as r:
                                done = ch * (TILES - 1) + r
                                v.wait_ge(g_mm, done + 1)
                                v.tensor_scalar(m.oh[:, 0, :], m.iota[:, ds(r * P + P, P)], m.dstT[:, ds(ch, 1)], None,
                                                ALU.is_equal).then_inc(g_oh, 1)
                                v.wait_ge(g_mm, done + 2)
                                v.wait_ge(g_add, done + 1)
                                v.tensor_tensor(tile_of(m.AGG, r + 1, width), tile_of(m.AGG, r + 1, width), pp[0], ALU.add).then_inc(g_add, 1)

            @block.tensor
            def _(pe):
                pe.sem_inc(mm_done, 8)

                def pair(p, i, j, slot):
                    if j % 4 == 0:
                        pe.wait_ge(oh_ready, i * (STEP // 4) + j // 4 + 1)
                    if not isinstance(p, int) or p < CHUNKS:
                        pe.wait_ge(gathered[j % STEP], base[j % STEP] + 16 * (i + j // STEP + 1))
                    pe.wait_ge(agg_done, p + 5 - ago[j % STEP])
                    pe.matmul(pp[bank[j % STEP]], m.oh[:, j % 8, :], m.ring[:, ds(slot, 1), 0:width].rearrange("p o d -> p (o d)"),
                              start=True, stop=True).then_inc(mm_done, 1)

                if side:
                    side.before_tensor(pe)
                with turns(pe, 0, TURNS, []) as i:
                    slots = load_row(nc, pe, m.tab[0:1, 3, ds(i * STEP, STEP)], RING - 1)
                    for j in range(STEP):
                        pair(i * STEP + j, i, j, slots[j])
                        if side:
                            side.tensor(pe, i, j)
                for j in range(TAIL):
                    if j % STEP == 0:
                        slots = load_row(nc, pe, m.tab[0:1, 3, ds(TURNS * STEP + j, STEP)], RING - 1)
                    pair(TURNS * STEP + j, TURNS, j, slots[j % STEP])
                    if side and j < STEP:
                        side.tensor(pe, TURNS, j)
                if side:
                    side.after_tensor(pe)

                if general:
                    unsorted = pe.value_load(m.tab[0:1, 2, 0:1], min_val=0, max_val=1)
                    with pe.If(unsorted > 0):
                        pe.sem_inc(g_mm, 1)
                        with pe.Fori(0, CHUNKS) as ch:
                            pe.wait_ge(g_in, 16 * ch + 16)
                            pe.sem_inc(g_woken, 1)
                            with pe.Fori(0, TILES - 1) as r:
                                done = ch * (TILES - 1) + r
                                pe.wait_ge(g_oh, done + 1)
                                pe.wait_ge(g_add, done + 1)
                                pe.matmul(pp[0], m.oh[:, 0, :], m.ring[:, 0, 0:width], start=True, stop=True).then_inc(g_mm, 1)

            if side:
                @block.scalar
                def _(act):
                    side.before_scalar(act)
                    with turns(act, 0, TURNS, side.scalar_counts) as i:
                        for j in range(STEP):
                            side.scalar(act, i, j)
                    for j in range(STEP):
                        side.scalar(act, TURNS, j)

                @block.sync
                def _(sp):
                    side.before_sync(sp)
                    with sp.Fori(0, TURNS) as i:
                        side.sync(sp, i)
                    side.sync(sp, TURNS)
        m.release(mark)


def load_row(nc, eng, ap, top):
    return nc.values_load_multi_w_load_instructions(ap, engines=(eng.engine,), min_val=0, max_val=top,
                                                      skip_runtime_bounds_check_because="the tables hold clipped values")[1]


def one_row(ap):
    return ap.rearrange("(o n) -> o n", o=1)


class Side:
    vector_counts, scalar_counts = (), ()

    def __init__(self, *parts):
        self.parts = parts
        self.vector_counts = [x for p in parts for x in p.vector_counts]
        self.scalar_counts = [x for p in parts for x in p.scalar_counts]

    def before_sync(self, sp):
        for p in self.parts:
            p.before_sync(sp)

    def sync(self, sp, i):
        for p in self.parts:
            p.sync(sp, i)

    def before_tensor(self, pe):
        for p in self.parts:
            p.before_tensor(pe)

    def tensor(self, pe, i, j):
        for p in self.parts:
            p.tensor(pe, i, j)

    def after_tensor(self, pe):
        for p in self.parts:
            p.after_tensor(pe)

    def before_vector(self, v):
        for p in self.parts:
            p.before_vector(v)

    def vector(self, v, i, j):
        for p in self.parts:
            p.vector(v, i, j)

    def after_vector(self, v):
        for p in self.parts:
            p.after_vector(v)

    def before_scalar(self, act):
        for p in self.parts:
            p.before_scalar(act)

    def scalar(self, act, i, j):
        for p in self.parts:
            p.scalar(act, i, j)


class LoopPart(Side):

    def __init__(self, nc, m, name, c, layer, loop_w, beta, bias, bank, step):
        super().__init__()
        self.step, self.bank_taken = step, None
        sem = stage_semaphores(nc, c, name)
        self.m, self.layer, self.loop_w, self.beta, self.bias, self.bank = m, layer, loop_w, beta, bias, bank
        self.w_in, self.tile_in, self.tile_used = sem("_lw_in"), sem("_lt_in"), sem("_lt_used")
        self.l_ready, self.l_copied = sem("_l_ready"), sem("_l_copied")
        self.w, self.xt, self.bb = m.take([P, 2, D]), m.take([P, D]), m.take([P, D])

    def before_sync(self, sp):
        sp.dma_start(self.w[:, :, :], by_half(self.loop_w)).then_inc(self.w_in, 16)
        sp.dma_start(self.bb[0:1, :], one_row(self.beta)).then_inc(self.w_in, 16)
        sp.dma_start(self.bb[1:2, :], one_row(self.bias)).then_inc(self.w_in, 16)

    def sync(self, sp, i):
        sp.wait_ge(self.tile_used, i + 1)
        sp.sem_inc(self.m.woken_sp, 1)
        sp.dma_start(self.xt[:, :], self.m.xt_dram[self.layer, ds(i, 1), :, :].rearrange("o p d -> (o p) d")).then_inc(self.tile_in, 16)

    def before_tensor(self, pe):
        pe.wait_ge(self.w_in, 48)

    def tensor(self, pe, i, j):
        if j == self.step:
            pe.wait_ge(self.tile_in, 16 * (i + 1))
            if self.bank_taken:
                sem, per, first = self.bank_taken
                pe.wait_ge(sem, i * per + first)
            else:
                pe.wait_ge(self.l_copied, i + 1)
            for k in range(2):
                pe.matmul(self.bank[:, 0:D], self.xt[:, k * P:(k + 1) * P], self.w[:, k, :], start=(k == 0), stop=False)
            pe.matmul(self.bank[:, 0:D], self.m.ones[0:2, :], self.bb[0:2, :], start=False, stop=True).then_inc(self.l_ready, 1)

    def after_tensor(self, pe):
        pass

    before_vector = after_vector = lambda self, v: None

    def vector(self, v, i, j):
        pass

    def before_scalar(self, act):
        act.sem_inc(self.tile_used, 1)
        act.sem_inc(self.l_copied, 1)

    def scalar(self, act, i, j):
        if j == self.step:
            act.wait_ge(self.l_ready, i + 1)
            act.sem_inc(self.tile_used, 1)
            act.activation(tile_of(self.m.L, i), self.bank[:, 0:D], ACT.Copy).then_inc(self.l_copied, 1)


HEADS, HD = 8, 32
DIST = HD // 2 + 1
FEAT = (DIST + 1) * HD
BLOCKS = HEADS * FEAT // P
VW = HD + 1
WIN = 2 * VW
PER_BANK = 512 // WIN
HSCALE = float(HD) ** 0.25
MIX_A, MIX_B, MIX_C = 0.5, 1.0, 1.0


def window(b):
    return min(b * P // FEAT, HEADS - 2)


def blocks_of(h):
    return [b for b in range(BLOCKS) if (b * P + P - 1) // FEAT == h]


def map_coefficients(np):
    co = np.zeros((P, BLOCKS, WIN), np.float32)
    for b in range(BLOCKS):
        for p in range(P):
            h, f = divmod(b * P + p, FEAT)
            d = f // HD
            if d == DIST:
                x = MIX_B * HSCALE ** 2
            else:
                x = MIX_A * (2.0 if 0 < d < HD // 2 else 1.0)
            at = (h - window(b)) * VW
            co[p, b, at:at + VW] = x
    return co.reshape(P, BLOCKS * WIN)


def make_map(v, own, m, ext, phi, h):
    e = ext[:, h, :]
    window_ap = bass.AP(e.tensor, e.offset, [list(e.ap[0]), [1, DIST], [1, HD]])
    base = e[:, 0:HD].unsqueeze(1).to_broadcast([P, DIST, HD])
    out = phi[:, h * FEAT:h * FEAT + DIST * HD].rearrange("p (d i) -> p d i", d=DIST)
    return v.tensor_tensor(out, base, window_ap, ALU.mult)


def extend(v, own, ext, phi, heads):
    own.inc(v.tensor_copy(ext[:, :, HD:48], ext[:, :, 0:16]))
    own.inc(v.tensor_copy(phi[:, :].rearrange("p (h f) -> p h f", h=heads)[:, :, DIST * HD:FEAT], ext[:, :, 0:HD]))


class MixKeys(Side):

    def __init__(self, nc, m, name, c, a, bank, loop):
        super().__init__()
        sem = stage_semaphores(nc, c, name)
        self.m, self.a, self.bank, self.loop = m, a, bank, loop
        self.w_in, self.coef_in = sem("_kw_in"), sem("_coef_in")
        self.kv_ready, self.kv_taken, self.phi_ready, self.phi_used = sem("_kv_ready"), sem("_kv_taken"), sem("_phi_ready"), sem("_phi_used")
        self.k_taken, self.sq_ready, self.ss_ready, self.n_ready, self.v_ready = sem("_k_taken"), sem("_sq_ready"), sem("_ss_ready"), sem("_n_ready"), sem("_v_ready")
        self.tail_ready, self.tail_taken, self.sums_ready = sem("_tail_ready"), sem("_tail_taken"), sem("_sums_ready")
        self.own, self.cleared = Count(sem("_k_own")), sem("_cleared")
        self.vector_counts = [(self.own, 8)]
        self.w = m.take([P, 2, 2 * D])
        self.b = m.take([P, 2 * D])
        self.kb, self.sq, self.vb = m.take([P, D]), m.take([P, D]), m.take([P, D])
        self.ss, self.n, self.r = m.take([P, HEADS]), m.take([P, HEADS]), m.take([P, HEADS])
        self.ext = m.take([P, HEADS, 48])
        self.v1 = m.take([P, HEADS * VW])
        self.phi = m.take([P, HEADS * FEAT])
        self.sums = [c.enter_context(nc.psum_tensor(f"{name}_sum{k}", [P, 512], F32)) for k in range(BLOCKS // PER_BANK)]

    def before_sync(self, sp):
        sp.dma_start(self.w[:, :, :], by_half(self.a["L0_mix_Wqkv"][:, D:3 * D])).then_inc(self.w_in, 16)
        sp.dma_start(self.b[:, :], row(self.a["L0_mix_bqkv"][D:3 * D])).then_inc(self.w_in, 16)
        sp.dma_start(self.m.kvs[:, :], self.a["coef"]).then_inc(self.coef_in, 16)
        sp.wait_ge(self.coef_in, 16)

    def sync(self, sp, i):
        pass

    def before_tensor(self, pe):
        pe.wait_ge(self.w_in, 32)
        for s in self.sums:
            pe.matmul(s[:, 0:PER_BANK * WIN], self.m.zeros[:, 0:P], self.w[:, 0, 0:PER_BANK * WIN], start=True, stop=False, skip_group_check=True)

    def tensor(self, pe, i, j):
        xt, bank, m = self.loop.xt, self.bank, self.m
        if j == 0:
            pe.wait_ge(self.loop.tile_in, 16 * (i + 1))
            pe.wait_ge(self.tail_taken, i + 1)
        if j in (0, 2):
            half = j // 2
            if half:
                pe.wait_ge(self.kv_taken, 2 * i + 1)
            for k in range(2):
                last = pe.matmul(bank[:, 0:D], xt[:, k * P:(k + 1) * P], self.w[:, k, half * D:(half + 1) * D], start=(k == 0), stop=(k == 1))
            last.then_inc(self.kv_ready, 1)
        h = j - 7
        if 0 <= h < HEADS:
            pe.wait_ge(self.phi_ready, i * HEADS + h + 1)
            for b in blocks_of(h):
                if b < PER_BANK * len(self.sums):
                    at = (b % PER_BANK) * WIN
                    w = window(b) * VW
                    pe.matmul(self.sums[b // PER_BANK][:, at:at + WIN], self.phi[:, b * P:(b + 1) * P], self.v1[:, w:w + WIN],
                              start=False, stop=False, skip_group_check=True)
        if h == HEADS - 1:
            pe.wait_ge(self.loop.l_copied, i + 2)
            pe.matmul(bank[:, 0:HEADS * VW], m.ones[:, :], self.v1[:, :], start=True, stop=True, skip_group_check=True)
            w = window(BLOCKS - 1) * VW
            pe.matmul(bank[:, HEADS * VW:HEADS * VW + WIN], self.phi[:, (BLOCKS - 1) * P:BLOCKS * P], self.v1[:, w:w + WIN],
                      start=True, stop=True, skip_group_check=True).then_inc(self.tail_ready, 1)

    def after_tensor(self, pe):
        for s in self.sums:
            last = pe.matmul(s[:, 0:PER_BANK * WIN], self.m.zeros[:, 0:P], self.w[:, 0, 0:PER_BANK * WIN], start=False, stop=True, skip_group_check=True)
        last.then_inc(self.sums_ready, 1)

    def before_vector(self, v):
        v.sem_inc(self.tail_taken, 1)
        v.wait_ge(self.w_in, 32)
        v.memset(self.m.kvtail[:, :], 0.0).then_inc(self.cleared, 1)
        v.wait_ge(self.cleared, 1)

    def vector(self, v, i, j):
        own, m = self.own, self.m
        if j == 1:
            v.wait_ge(self.kv_ready, 2 * i + 1)
            v.tensor_tensor(self.kb[:, :], self.bank[:, 0:D], self.b[:, 0:D], ALU.add).then_inc(self.kv_taken, 1)
        if j == 2:
            v.wait_ge(self.sq_ready, i + 1)
            v.tensor_reduce(self.ss[:, :], self.sq[:, :].rearrange("p (h d) -> p h d", h=HEADS), AX.X, ALU.add).then_inc(self.ss_ready, 1)
        if j == 3:
            v.wait_ge(self.kv_ready, 2 * i + 2)
            v.tensor_tensor(self.vb[:, :], self.bank[:, 0:D], self.b[:, D:2 * D], ALU.add).then_inc(self.kv_taken, 1)
        if j == 4:
            v.wait_ge(self.n_ready, i + 1)
            own.inc(v.tensor_scalar(self.r[:, :], self.n[:, :], 1e-12, None, ALU.max))
            own.wait(v)
            own.inc(v.reciprocal(self.r[:, :], self.r[:, :]))
            own.wait(v)
            v.wait_ge(self.phi_used, i + 1)
            own.inc(v.tensor_scalar(self.r[:, :], self.r[:, :], HSCALE, None, ALU.mult))
            own.wait(v)
            own.inc(v.tensor_tensor(self.ext[:, :, 0:HD], self.kb[:, :].rearrange("p (h d) -> p h d", h=HEADS),
                                    self.r[:, :].unsqueeze(2).to_broadcast([P, HEADS, HD]), ALU.mult))
            v1 = self.v1[:, :].rearrange("p (h e) -> p h e", h=HEADS)
            own.wait(v)
            extend(v, own, self.ext, self.phi, HEADS)
            v.wait_ge(self.kv_taken, 2 * i + 2)
            own.inc(v.tensor_scalar(v1[:, :, 1:VW], self.vb[:, :].rearrange("p (h d) -> p h d", h=HEADS),
                                    m.valid[:, ds(i, 1)], 1.0 / N, ALU.mult, ALU.mult))
            own.inc(v.tensor_scalar(v1[:, :, 0:1], m.ones[:, 0:HEADS].unsqueeze(2), m.valid[:, ds(i, 1)], 1.0 / N, ALU.mult, ALU.mult))
            own.wait(v)
        if 5 <= j < 5 + HEADS:
            make_map(v, own, m, self.ext, self.phi, j - 5).then_inc(self.phi_ready, 1)
        if j == 15:
            v.wait_ge(self.tail_ready, i + 1)
            v.wait_ge(self.tail_taken, i + 1)
            v.tensor_tensor(m.kvtail[:, :], m.kvtail[:, :], self.bank[:, 0:HEADS * VW + WIN], ALU.add).then_inc(self.tail_taken, 1)

    def after_vector(self, v):
        m = self.m
        v.wait_ge(self.coef_in, 16)
        v.wait_ge(self.sums_ready, 1)
        v.wait_ge(self.tail_taken, TILES + 1)
        for k, s in enumerate(self.sums):
            kv = m.kvs[:, k * PER_BANK * WIN:(k + 1) * PER_BANK * WIN]
            v.tensor_tensor(kv, s[:, 0:PER_BANK * WIN], kv, ALU.mult)
        kv = m.kvs[:, (BLOCKS - 1) * WIN:BLOCKS * WIN]
        v.tensor_tensor(kv, m.kvtail[:, HEADS * VW:], kv, ALU.mult)
        v.tensor_scalar(m.kvconst[0:1, :], m.kvtail[0:1, 0:HEADS * VW], MIX_C * HSCALE ** 4, None, ALU.mult)

    def before_scalar(self, act):
        act.sem_inc(self.phi_used, 1)

    def scalar(self, act, i, j):
        if j == 1:
            act.wait_ge(self.kv_taken, 2 * i + 1)
            act.activation(self.sq[:, :], self.kb[:, :], ACT.Square).then_inc(self.sq_ready, 1)
        if j == 2:
            act.wait_ge(self.ss_ready, i + 1)
            act.activation(self.n[:, :], self.ss[:, :], ACT.Sqrt).then_inc(self.n_ready, 1)
        if j == 15:
            act.wait_ge(self.tail_ready, i + 1)
            act.sem_inc(self.phi_used, 1)


class MixQueries(Side):
    QH = HEADS // 2
    QD = QH * HD
    GROUP = 2
    GROUPS = BLOCKS // 2 // GROUP
    QUERIES = 6
    FRONT = (7, 8, 10, 12)

    EARLY = 2

    def __init__(self, nc, m, name, c, a, bank, loop, part):
        super().__init__()
        sem = stage_semaphores(nc, c, name)
        self.m, self.a, self.bank, self.loop = m, a, bank, loop
        self.w_in, self.q_in, self.q_used = sem("_qw_in"), sem("_q_in"), sem("_q_used")
        self.q_ready, self.q_taken, self.sq_ready, self.ss_ready, self.n_ready = (sem(x) for x in ("_q_ready", "_q_taken", "_sq_ready", "_ss_ready", "_n_ready"))
        self.phi_ready, self.t_ready, self.t_copied, self.t_used = (sem(x) for x in ("_phi_ready", "_t_ready", "_t_copied", "_t_used"))
        self.o_ready, self.ot_ready, self.ot_copied, self.out_ready, self.x_done = (sem(x) for x in ("_o_ready", "_ot_ready", "_ot_copied", "_out_ready", "_x_done"))
        self.own = Count(sem("_q_own"))
        self.vector_counts = [(self.own, 7)]
        QH, QD = self.QH, self.QD
        self.part, self.head0, self.block0 = part, part * QH, part * BLOCKS // 2
        self.w, self.wp = m.take([P, 2, QD]), m.take([P, D])
        self.b, self.bp = m.take([P, QD]), m.take([P, D])
        self.temp = m.take([P, QH])
        self.xt = m.take([P, D])
        self.qb, self.sq = m.take([P, QD]), m.take([P, QD])
        self.ss, self.n, self.r, self.yr = (m.take([P, QH]) for _ in range(4))
        self.ext = m.take([P, QH, 48])
        self.phi = m.take([P, QH * FEAT])
        self.phiT = m.take([P, 2, self.GROUP * P])
        self.o, self.oT = m.take([P, QD]), m.take([P, QD])
        ps = lambda x: c.enter_context(nc.psum_tensor(name + x, [P, 512], F32))
        self.psT, self.y, self.out = [ps("_pt0"), ps("_pt1")], ps("_y"), ps("_out")

    def before_sync(self, sp):
        a = self.a
        at = self.head0 * HD
        sp.dma_start(self.w[:, :, :], by_half(a["L0_mix_Wqkv"][:, at:at + self.QD])).then_inc(self.w_in, 16)
        sp.dma_start(self.wp[:, :], a["L0_mix_Wproj"][at:at + self.QD, :]).then_inc(self.w_in, 16)
        sp.dma_start(self.b[:, :], row(a["L0_mix_bqkv"][at:at + self.QD])).then_inc(self.w_in, 16)
        sp.dma_start(self.bp[0:1, :], one_row(a["L0_mix_bproj"])).then_inc(self.w_in, 16)
        sp.dma_start(self.temp[:, :], row(a["L0_mix_temperature"].rearrange("a h b c -> (a h b c)")[self.head0:self.head0 + self.QH])).then_inc(self.w_in, 16)
        self.load(sp, 0)

    def load(self, sp, t):
        sp.wait_ge(self.q_used, t + 1)
        sp.sem_inc(self.m.woken_sp, 1)
        sp.dma_start(self.xt[:, :], self.m.xt_dram[0, ds(t, 1), :, :].rearrange("o p d -> (o p) d")).then_inc(self.q_in, 16)

    def sync(self, sp, i):
        if not is_last(i):
            self.load(sp, i + 1)

    def project_queries(self, pe, t):
        pe.wait_ge(self.q_in, 16 * (t + 1))
        pe.wait_ge(self.loop.l_copied, t + 1)
        for k in range(2):
            last = pe.matmul(self.bank[:, 0:self.QD], self.xt[:, k * P:(k + 1) * P], self.w[:, k, :], start=(k == 0), stop=(k == 1))
        last.then_inc(self.q_ready, 1)

    def before_tensor(self, pe):
        pe.wait_ge(self.w_in, 80)
        self.project_queries(pe, 0)
        pe.sem_inc(self.t_used, 1)

    def tensor(self, pe, i, j):
        m, G = self.m, self.GROUPS
        g = j - 1
        if 0 <= g < G:
            head_of = lambda g: ((g + 1) * self.GROUP * P - 1) // FEAT
            if g == 0 or head_of(g) > head_of(g - 1):
                pe.wait_ge(self.phi_ready, i * self.QH + head_of(g) + 1)
            if g == 0:
                pe.wait_ge(self.t_copied, i * G + 1)
            for k in range(self.GROUP):
                b = g * self.GROUP + k
                last = pe.transpose(self.psT[g % 2][:, k * P:(k + 1) * P], self.phi[:, b * P:(b + 1) * P], m.ident[:, :])
            last.then_inc(self.t_ready, 1)
        g = j - 2
        if 0 <= g < G:
            if g == 0:
                pe.wait_ge(self.o_ready, i + 1)
                c0, c1 = self.head0 * VW, min(self.head0 + self.QH + 1, HEADS) * VW
                pe.matmul(self.y[:, 0:c1 - c0], m.ones[0:1, :], m.kvconst[0:1, c0:c1], start=True, stop=False, skip_group_check=True)
            pe.wait_ge(self.t_copied, i * G + g + 2)
            for k in range(self.GROUP):
                b = self.block0 + g * self.GROUP + k
                w = (window(b) - self.head0) * VW
                last = pe.matmul(self.y[:, w:w + WIN], self.phiT[:, g % 2, k * P:(k + 1) * P], m.kvs[:, b * WIN:(b + 1) * WIN],
                                 start=False, stop=(b + 1 == self.block0 + BLOCKS // 2), skip_group_check=True)
            last.then_inc(self.t_used, 1)
        if j == self.QUERIES and not is_last(i):
            self.project_queries(pe, i + 1)
        if j == 12:
            pe.wait_ge(self.o_ready, i + 2)
            pe.wait_ge(self.x_done, i + 1)
            pe.transpose(self.out[:, 0:P], self.o[:, :], m.ident[:, :]).then_inc(self.ot_ready, 1)
        if j == 14:
            pe.wait_ge(self.ot_copied, i + 1)
            last = pe.matmul(self.out[:, 0:D], self.oT[:, :], self.wp[:, :], start=True, stop=(self.part == 1))
            if self.part == 0:
                last = pe.matmul(self.out[:, 0:D], m.ones[0:1, :], self.bp[0:1, :], start=False, stop=True)
            last.then_inc(self.out_ready, 1)

    def front(self, v, step, t):
        own = self.own
        if step == 0:
            v.wait_ge(self.q_ready, t + 1)
            v.tensor_tensor(self.qb[:, :], self.bank[:, 0:self.QD], self.b[:, :], ALU.add).then_inc(self.q_taken, 1)
        if step == 1:
            v.wait_ge(self.sq_ready, t + 1)
            v.tensor_reduce(self.ss[:, :], self.sq[:, :].rearrange("p (h d) -> p h d", h=self.QH), AX.X, ALU.add).then_inc(self.ss_ready, 1)
        if step == 2:
            v.wait_ge(self.n_ready, t + 1)
            own.inc(v.tensor_scalar(self.r[:, :], self.n[:, :], 1e-12, None, ALU.max))
            own.wait(v)
            own.inc(v.reciprocal(self.r[:, :], self.r[:, :]))
            own.wait(v)
            own.inc(v.tensor_tensor(self.r[:, :], self.r[:, :], self.temp[:, :], ALU.mult))
            own.wait(v)
        if step == 3:
            own.inc(v.tensor_tensor(self.ext[:, :, 0:HD], self.qb[:, :].rearrange("p (h d) -> p h d", h=self.QH),
                                    self.r[:, :].unsqueeze(2).to_broadcast([P, self.QH, HD]), ALU.mult))
            own.wait(v)
            extend(v, own, self.ext, self.phi, self.QH)
            own.wait(v)

    def before_vector(self, v):
        v.sem_inc(self.o_ready, 1)
        v.sem_inc(self.x_done, 1)
        v.wait_ge(self.w_in, 80)
        self.own.inc(v.tensor_scalar(self.temp[:, :], self.temp[:, :], HSCALE ** 2, None, ALU.mult))
        self.own.wait(v)
        for step in range(4):
            self.front(v, step, 0)
        for h in range(self.EARLY):
            self.map(v, h)

    def map(self, v, h):
        make_map(v, self.own, self.m, self.ext, self.phi, h).then_inc(self.phi_ready, 1)

    def vector(self, v, i, j):
        own, m = self.own, self.m
        if j + self.EARLY < self.QH:
            self.map(v, j + self.EARLY)
        if j == 11:
            v.wait_ge(self.t_used, (i + 1) * self.GROUPS + 1)
            y = self.y[:, 0:self.QH * VW].rearrange("p (h e) -> p h e", h=self.QH)
            own.inc(v.reciprocal(self.yr[:, :].unsqueeze(2), y[:, :, 0:1]))
            own.wait(v)
            v.tensor_tensor(self.o[:, :].rearrange("p (h d) -> p h d", h=self.QH), y[:, :, 1:VW],
                            self.yr[:, :].unsqueeze(2).to_broadcast([P, self.QH, HD]), ALU.mult).then_inc(self.o_ready, 1)
        if j in self.FRONT and not is_last(i):
            self.front(v, self.FRONT.index(j), i + 1)
        early = j - self.FRONT[-1] - 1
        if 0 <= early < self.EARLY and not is_last(i):
            self.map(v, early)
        if j == 15:
            v.wait_ge(self.out_ready, i + 1)
            v.tensor_tensor(tile_of(m.X, i), tile_of(m.X, i), self.out[:, 0:D], ALU.add).then_inc(self.x_done, 1)

    def before_scalar(self, act):
        act.sem_inc(self.q_used, 1)
        act.sem_inc(self.t_copied, 1)
        self.square(act, 0)
        self.root(act, 0)

    def square(self, act, t):
        act.wait_ge(self.q_taken, t + 1)
        act.sem_inc(self.q_used, 1)
        act.activation(self.sq[:, :], self.qb[:, :], ACT.Square).then_inc(self.sq_ready, 1)

    def root(self, act, t):
        act.wait_ge(self.ss_ready, t + 1)
        act.activation(self.n[:, :], self.ss[:, :], ACT.Sqrt, scale=HSCALE ** 2).then_inc(self.n_ready, 1)

    def scalar(self, act, i, j):
        G, g = self.GROUPS, j - 1
        if 0 <= g < G:
            act.wait_ge(self.t_ready, i * G + g + 1)
            act.activation(self.phiT[:, g % 2, :], self.psT[g % 2][:, 0:self.GROUP * P], ACT.Copy).then_inc(self.t_copied, 1)
        if j == self.FRONT[0] and not is_last(i):
            self.square(act, i + 1)
        if j == self.FRONT[1] and not is_last(i):
            self.root(act, i + 1)
        if j == 12:
            act.wait_ge(self.ot_ready, i + 1)
            act.activation(self.oT[:, :], self.out[:, 0:P], ACT.Copy).then_inc(self.ot_copied, 1)


def finish(nc, m, name, gamma, beta=None):
    with ExitStack() as c:
        v_in, dve, added = map(stage_semaphores(nc, c, name), ("_in", "_dve", "_added"))
        mark = m.mark()
        gam, bet, tmp = m.take([P, D]), m.take([P, D]), m.take([P, 5, D])
        with nc.Block() as block:
            @block.sync
            def _(sp):
                sp.dma_start(gam[:, :], row(gamma)).then_inc(v_in, 16)
                if beta is not None:
                    sp.dma_start(bet[:, :], row(beta)).then_inc(v_in, 16)

            @block.vector
            def _(v):
                own = Count(dve)
                v.wait_ge(v_in, 16 if beta is None else 32)

                def group(t0, n):
                    for j in range(n):
                        own.inc(v.tensor_scalar(tmp[:, j, :], tile_of(m.AGG, t0 + j), m.mean(t0 + j), m.rstd_of(t0 + j), ALU.subtract, ALU.mult))
                    own.wait(v)
                    for j in range(n):
                        own.inc(v.tensor_tensor(tmp[:, j, :], tmp[:, j, :], gam[:, :], ALU.mult))
                    own.wait(v)
                    v.wait_ge(added, t0 + n)
                    for j in range(n):
                        own.inc(v.tensor_tensor(tile_of(m.X, t0 + j), tile_of(m.X, t0 + j), tmp[:, j, :], ALU.add))
                    own.wait(v)
                with turns(v, 0, TILES // 5, [(own, 15)]) as i:
                    group(i * 5, 5)

            @block.gpsimd
            def _(pool):
                if beta is not None:
                    pool.wait_ge(v_in, 32)
                tiles4(pool, lambda t, j: pool.tensor_tensor(tile_of(m.X, t), tile_of(m.X, t), bet[:, :] if beta is not None else tile_of(m.L, t),
                                                             ALU.add).then_inc(added, 1))
        m.release(mark)


EXPERTS, FF, TOP = 8, 512, 2
FB = FF // P
CAPACITY = float(-(-N * 5 // (4 * EXPERTS)))


def route(nc, m, a):
    with ExitStack() as c:
        sem = stage_semaphores(nc, c, "rt")
        w_in, x_in, dve_own, h_ready = sem("_w"), sem("_x"), sem("_dve"), sem("_h_ready")
        sums, mean_ready, logits, e_ready, ex_done, idx_ready = sem("_sums"), sem("_mean"), sem("_logits"), sem("_e"), sem("_exp"), sem("_idx")
        b1_ready = sem("_b1")
        wr, br = m.take([P, 2, EXPERTS]), m.take([P, EXPERTS])
        rv, mu, mc, mb = m.take([P, TILES]), m.take([P, TILES]), m.take([P, 2]), m.take([P, 2, P])
        lg, ex, col = m.take([P, EXPERTS]), m.take([P, EXPERTS]), m.take([P, 16])
        top, idx = m.take([P, EXPERTS]), m.take([P, EXPERTS], U32)
        b1n, b2r = m.take([P, P]), m.take([P, 2, D])
        psS = [c.enter_context(nc.psum_tensor(f"rt_s{k}", [P, 512], F32)) for k in range(2)]
        psL = c.enter_context(nc.psum_tensor("rt_l", [P, 512], F32))
        psB = c.enter_context(nc.psum_tensor("rt_b", [P, 512], F32))
        with nc.Block() as block:
            @block.gpsimd
            def _(pool):
                m.send.some(pool, 3)

            @block.sync
            def _(sp):
                sp.dma_start(wr[:, :, :], by_half(a["L0_ffn_Wr"])).then_inc(w_in, 16)
                sp.dma_start(br[:, :], row(a["L0_ffn_br"])).then_inc(w_in, 16)
                sp.wait_ge(idx_ready, 1)
                for k in range(TOP):
                    e = sp.value_load(idx[0:1, k:k + 1], min_val=0, max_val=EXPERTS - 1)
                    one = lambda ap: ap[ds(e, 1)]
                    sp.dma_start(m.w1[:, k, :, :], one(a["L0_ffn_W1"]).rearrange("o (k p) f -> p (o k) f", p=P)).then_inc(x_in, 16)
                    sp.dma_start(m.w2[:, k, :, :], one(a["L0_ffn_W2"]).rearrange("o (b p) d -> p (o b) d", p=P)).then_inc(x_in, 16)
                    sp.dma_start(b1n[k * FB:(k + 1) * FB, :], one(a["L0_ffn_b1"]).rearrange("o (b p) -> (o b) p", p=P)).then_inc(x_in, 16)
                    sp.dma_start(b2r[:, k, :], one(a["L0_ffn_b2"]).to_broadcast([P, D])).then_inc(x_in, 16)

            @block.vector
            def _(v):
                own = Count(dve_own)

                def step(ins):
                    own.inc(ins)
                    own.wait(v)

                step(v.tensor_tensor(rv[:, :], m.rstd[:, :], m.valid[:, :], ALU.mult))
                v.sem_inc(h_ready, 1)
                step(v.tensor_tensor(mu[:, :], rv[:, :], m.mv[:, :, 0], ALU.mult))
                step(v.tensor_reduce(col[:, 8:9], mu[:, :], AX.X, ALU.add))
                v.sem_inc(h_ready, 1)
                v.wait_ge(sums, 1)
                step(v.tensor_copy(col[:, 9:10], psL[:, EXPERTS:EXPERTS + 1]))
                for k in range(2):
                    own.inc(v.tensor_scalar(mc[:, k:k + 1], psS[k][:, 0:1], col[:, 9:10], 1.0 / N, ALU.subtract, ALU.mult))
                own.wait(v)
                v.tensor_copy(mb[:, :, :], mc[:, :].unsqueeze(2).to_broadcast([P, 2, P])).then_inc(mean_ready, 1)
                v.wait_ge(logits, 1)
                step(v.tensor_tensor(lg[:, :], psL[:, 0:EXPERTS], br[:, :], ALU.add))

                def softmax(turn):
                    step(v.tensor_reduce(col[:, 0:1], lg[:, :], AX.X, ALU.max))
                    step(v.tensor_scalar(lg[:, :], lg[:, :], col[:, 0:1], None, ALU.subtract))
                    v.sem_inc(e_ready, 1)
                    v.wait_ge(ex_done, turn)
                    step(v.tensor_reduce(col[:, 1:2], ex[:, :], AX.X, ALU.add))
                    step(v.reciprocal(col[:, 2:3], col[:, 1:2]))
                    step(v.tensor_scalar(lg[:, :], ex[:, :], col[:, 2:3], None, ALU.mult))
                softmax(1)
                step(v.tensor_scalar(ex[:, :], lg[:, :], float(N), None, ALU.mult))
                step(v.reciprocal(ex[:, :], ex[:, :]))
                step(v.tensor_scalar(ex[:, :], ex[:, :], CAPACITY, 1.0, ALU.mult, ALU.min))
                step(v.tensor_tensor(lg[:, :], lg[:, :], ex[:, :], ALU.mult))
                softmax(2)
                step(v.max(top[:, :], lg[:, :]))
                v.max_index(idx[:, :], top[:, :], lg[:, :]).then_inc(idx_ready, 1)
                v.wait_ge(idx_ready, 1)
                step(v.tensor_scalar(lg[:, :], top[:, :], top[:, 0:1], None, ALU.subtract))
                v.sem_inc(e_ready, 1)
                v.wait_ge(ex_done, 3)
                step(v.tensor_tensor(col[:, 3:4], ex[:, 0:1], ex[:, 1:2], ALU.add))
                step(v.reciprocal(col[:, 4:5], col[:, 3:4]))
                step(v.tensor_scalar(m.gate[:, :], ex[:, 0:TOP], col[:, 4:5], None, ALU.mult))
                v.wait_ge(x_in, 16 * 4 * TOP)
                for k in range(TOP):
                    own.inc(v.tensor_scalar(m.w2[:, k, :, :], m.w2[:, k, :, :], m.gate[:, k:k + 1], None, ALU.mult))
                own.inc(v.tensor_scalar(b2r[:, 0, :], b2r[:, 0, :], m.gate[:, 0:1], None, ALU.mult))
                own.wait(v)
                v.scalar_tensor_tensor(m.b2[:, :], b2r[:, 1, :], m.gate[:, 1:2], b2r[:, 0, :], ALU.mult, ALU.add)
                v.wait_ge(b1_ready, 1)
                v.tensor_copy(m.b1[:, :], psB[:, 0:TOP * FB])

            @block.scalar
            def _(act):
                for turn in range(3):
                    act.wait_ge(e_ready, turn + 1)
                    act.activation(ex[:, :], lg[:, :], ACT.Exp).then_inc(ex_done, 1)

            @block.tensor
            def _(pe):
                pe.wait_ge(h_ready, 1)
                for t in range(TILES):
                    for k in range(2):
                        pe.matmul(psS[k][:, 0:1], m.X[:, t, k * P:(k + 1) * P], rv[:, t:t + 1], start=(t == 0), stop=(t == TILES - 1))
                pe.wait_ge(h_ready, 2)
                pe.matmul(psL[:, EXPERTS:EXPERTS + 1], m.ones[:, :], col[:, 8:9], start=True, stop=True).then_inc(sums, 1)
                pe.wait_ge(mean_ready, 1)
                pe.wait_ge(w_in, 32)
                for k in range(2):
                    last = pe.matmul(psL[:, 0:EXPERTS], mb[:, k, :], wr[:, k, :], start=(k == 0), stop=(k == 1))
                last.then_inc(logits, 1)
                pe.wait_ge(x_in, 16 * 4 * TOP)
                pe.transpose(psB[:, 0:TOP * FB], b1n[0:TOP * FB, :], m.ident[0:TOP * FB, 0:TOP * FB]).then_inc(b1_ready, 1)


def experts(nc, m):
    HB = TOP * FB
    with ExitStack() as c:
        sem = stage_semaphores(nc, c, "ex")
        h_ready, h_free, xt_done, hid_ready, hid_done, y_ready, y_taken, dve_own = (
            sem(x) for x in ("_h_ready", "_h_free", "_xt", "_hid_ready", "_hid_done", "_y_ready", "_y_taken", "_dve"))
        mark = m.mark()
        h, xt, tmp = m.take([P, 2, D]), m.take([P, 2, D]), m.take([P, 2, D])
        hid = m.take([P, 2, HB * P])
        ps = lambda x: c.enter_context(nc.psum_tensor("ex" + x, [P, 512], F32))
        psT, psY = [ps("_t0"), ps("_t1")], [ps("_y0"), ps("_y1")]
        psH = [[ps(f"_h{s}{k}") for k in range(2)] for s in range(2)]
        with nc.Block() as block:
            @block.gpsimd
            def _(pool):
                m.send.rest(pool)

            @block.vector
            def _(v):
                own = Count(dve_own)
                v.sem_inc(y_taken, 2)

                def make_h(t, j):
                    v.wait_ge(h_free, t + 1)
                    v.tensor_scalar(h[:, j % 2, :], tile_of(m.X, t), m.mean(t), m.rstd_of(t), ALU.subtract, ALU.mult).then_inc(h_ready, 1)

                def body(t, j):
                    if not is_last(t):
                        make_h(t + 1, j + 1)
                    v.wait_ge(y_ready, t + 1)
                    v.tensor_tensor(tmp[:, j % 2, :], psY[j % 2][:, 0:D], h[:, j % 2, :], ALU.add).then_inc(y_taken, 1)
                    v.wait_ge(y_taken, t + 3)
                    v.tensor_tensor(tile_of(m.AGG, t), tmp[:, j % 2, :], m.b2[:, :], ALU.add)
                make_h(0, 0)
                tiles4(v, body)

            @block.tensor
            def _(pe):
                pe.sem_inc(h_free, 2)

                def transposes(t, j):
                    pe.wait_ge(h_ready, t + 1)
                    pe.wait_ge(xt_done, t + 1)
                    for k in range(2):
                        last = pe.transpose(psT[j % 2][:, k * P:(k + 1) * P], h[:, j % 2, k * P:(k + 1) * P], m.ident[:, :])
                    last.then_inc(h_free, 1)

                def hidden(t, j):
                    pe.wait_ge(xt_done, t + 3)
                    pe.wait_ge(hid_done, HB * t + HB)
                    for b in range(HB):
                        e, f = divmod(b, FB)
                        for k in range(2):
                            last = pe.matmul(psH[j % 2][e][:, f * P:(f + 1) * P], m.w1[:, e, k, f * P:(f + 1) * P],
                                             xt[:, j % 2, k * P:(k + 1) * P], start=(k == 0), stop=(k == 1))
                        if f == FB - 1:
                            last.then_inc(hid_ready, 1)

                def out(t, j):
                    pe.wait_ge(hid_done, HB * t + 3 * HB)
                    pe.wait_ge(y_taken, t + 1)
                    for b in range(HB):
                        e, f = divmod(b, FB)
                        last = pe.matmul(psY[j % 2][:, 0:D], hid[:, j % 2, b * P:(b + 1) * P], m.w2[:, e, f, :], start=(b == 0), stop=(b == HB - 1))
                    last.then_inc(y_ready, 1)

                def body(t, j):
                    if not is_last(t):
                        transposes(t + 1, j + 1)
                    out(t, j)
                    if not is_last(t):
                        hidden(t + 1, j + 1)
                transposes(0, 0)
                hidden(0, 0)
                tiles4(pe, body)

            @block.scalar
            def _(act):
                act.sem_inc(xt_done, 2)
                act.sem_inc(hid_done, 2 * HB)

                def copy_xt(t, j):
                    act.wait_ge(h_free, t + 3)
                    act.activation(xt[:, j % 2, :], psT[j % 2][:, 0:D], ACT.Copy).then_inc(xt_done, 1)

                def gelu(t, j):
                    for b in range(HB):
                        e, f = divmod(b, FB)
                        if f == 0:
                            act.wait_ge(hid_ready, TOP * t + e + 1)
                        act.activation(hid[:, j % 2, b * P:(b + 1) * P], psH[j % 2][e][:, f * P:(f + 1) * P], ACT.Gelu,
                                       bias=m.b1[:, b:b + 1]).then_inc(hid_done, 1)

                def body(t, j):
                    gelu(t, j)
                    if not is_last(t):
                        copy_xt(t + 1, j + 1)
                copy_xt(0, 0)
                tiles4(act, body)
        m.release(mark)


HEADS1, HD1 = 4, 64
HALF = P // 2


def use16(t, j):
    return 16 * (t // 4 + 1) if isinstance(t, int) else (t - j) * 4 + 16


class LinearMix(Side):

    def __init__(self, nc, m, name, c, a):
        super().__init__()
        sem = stage_semaphores(nc, c, name)
        self.m, self.a = m, a
        self.w_in, self.w_ready, self.t_in, self.t_used = sem("_w_in"), sem("_w_ready"), sem("_t_in"), sem("_t_used")
        self.p_ready, self.p_taken, self.sq_ready, self.ss_ready, self.sd_ready = (
            sem("_p_ready"), sem("_p_taken"), sem("_sq_ready"), sem("_ss_ready"), sem("_sd_ready"))
        self.kv_ready, self.kv_used, self.sum_ready = sem("_kv_ready"), sem("_kv_used"), sem("_sum_ready")
        self.own = Count(sem("_own"))
        self.vector_counts = [(self.own, 4)]
        self.w, self.mean = m.take([P, 2, 2 * D]), m.take([P, 2, 2 * HEADS1])
        self.g, self.b = m.take([P, 2 * D]), m.take([P, 2 * D])
        self.xt, self.sq, self.kv = m.take([P, D]), m.take([P, 2 * D]), m.take([P, 2 * D])
        self.ss, self.sd, self.r = m.take([P, 2 * HEADS1]), m.take([P, 2 * HEADS1]), m.take([P, 2 * HEADS1])
        ps = lambda x: c.enter_context(nc.psum_tensor(name + x, [P, 512], F32))
        self.p, self.sum = ps("_kv"), ps("_sum")

    def heads(self, ap):
        return ap.rearrange("p (h d) -> p h d", d=HD1)

    def before_sync(self, sp):
        a = self.a
        sp.dma_start(self.w[:, :, 0:D], by_half(a["L1_mix_wk"])).then_inc(self.w_in, 16)
        sp.dma_start(self.w[:, :, D:2 * D], by_half(a["L1_mix_wv"])).then_inc(self.w_in, 16)
        for vec, k, v in ((self.g, "L1_mix_ln_k_g", "L1_mix_ln_v_g"), (self.b, "L1_mix_ln_k_b", "L1_mix_ln_v_b")):
            for at, name in ((0, k), (D, v)):
                for h in range(HEADS1):
                    sp.dma_start(vec[:, at + h * HD1:at + (h + 1) * HD1], row(a[name])).then_inc(self.w_in, 16)

    def sync(self, sp, i):
        sp.wait_ge(self.t_used, i + 1)
        sp.sem_inc(self.m.woken_sp, 1)
        sp.dma_start(self.xt[:, :], self.m.xt_dram[3, ds(i, 1), :, :].rearrange("o p d -> (o p) d")).then_inc(self.t_in, 16)

    def before_tensor(self, pe):
        pe.wait_ge(self.w_ready, 1)
        pe.matmul(self.sum[:, 0:D], self.m.zeros[:, 0:P], self.m.zeros[:, 0:D], start=True, stop=False, skip_group_check=True)

    def tensor(self, pe, i, j):
        if j == 0:
            pe.wait_ge(self.t_in, 16 * (i + 1))
            pe.wait_ge(self.p_taken, i + 1)
            for k in range(2):
                last = pe.matmul(self.p[:, :], self.xt[:, k * P:(k + 1) * P], self.w[:, k, :], start=(k == 0), stop=(k == 1))
            last.then_inc(self.p_ready, 1)
        if j == 10:
            pe.wait_ge(self.kv_ready, i + 2)
            for k in range(2):
                last = pe.matmul(self.sum[:, k * P:(k + 1) * P], self.kv[:, k * P:(k + 1) * P], self.kv[:, D + k * P:D + (k + 1) * P],
                                 start=False, stop=False, skip_group_check=True)
            last.then_inc(self.kv_used, 1)

    def after_tensor(self, pe):
        pe.matmul(self.sum[:, 0:D], self.m.zeros[:, 0:P], self.m.zeros[:, 0:D], start=False, stop=True,
                  skip_group_check=True).then_inc(self.sum_ready, 1)

    def before_vector(self, v):
        own = self.own
        v.sem_inc(self.p_taken, 1)
        v.sem_inc(self.kv_used, 1)
        v.sem_inc(self.kv_ready, 1)
        v.memset(self.m.kv[:, :, :], 0.0)
        v.wait_ge(self.w_in, 16 * (2 + 4 * HEADS1))
        for k in range(2):
            own.inc(v.tensor_reduce(self.mean[:, k, :], self.heads(self.w[:, k, :]), AX.X, ALU.add))
        own.wait(v)
        own.inc(v.tensor_scalar(self.mean[:, :, :], self.mean[:, :, :], -1.0 / HD1, None, ALU.mult))
        own.wait(v)
        for k in range(2):
            own.inc(v.tensor_tensor(self.heads(self.w[:, k, :]), self.heads(self.w[:, k, :]),
                                    self.mean[:, k, :].unsqueeze(2).to_broadcast([P, 2 * HEADS1, HD1]), ALU.add))
        own.wait(v)
        v.sem_inc(self.w_ready, 1)

    def vector(self, v, i, j):
        own, m = self.own, self.m
        if j == 3:
            v.wait_ge(self.sq_ready, i + 1)
            v.tensor_reduce(self.ss[:, :], self.heads(self.sq[:, :]), AX.X, ALU.add).then_inc(self.ss_ready, 1)
        if j == 5:
            v.wait_ge(self.sd_ready, i + 1)
            own.inc(v.reciprocal(self.r[:, :], self.sd[:, :]))
            own.wait(v)
            own.inc(v.tensor_tensor(self.heads(self.sq[:, :]), self.heads(self.p[:, :]),
                                    self.r[:, :].unsqueeze(2).to_broadcast([P, 2 * HEADS1, HD1]), ALU.mult))
            own.wait(v)
            v.sem_inc(self.p_taken, 1)
        if j == 6:
            v.wait_ge(self.kv_used, i + 1)
            own.inc(v.tensor_tensor(self.kv[:, :], self.sq[:, :], self.g[:, :], ALU.mult))
            own.wait(v)
        if j == 7:
            own.inc(v.tensor_tensor(self.kv[:, :], self.kv[:, :], self.b[:, :], ALU.add))
            own.wait(v)
            v.tensor_scalar(self.kv[:, 0:D], self.kv[:, 0:D], m.valid[:, ds(i, 1)], 1.0 / N, ALU.mult, ALU.mult).then_inc(self.kv_ready, 1)

    def after_vector(self, v):
        v.wait_ge(self.sum_ready, 1)
        for k in range(2):
            for r in (0, HALF):
                v.tensor_copy(self.m.kv[r:r + HALF, k, r:r + HALF], self.sum[r:r + HALF, k * P + r:k * P + r + HALF])

    def before_scalar(self, act):
        act.sem_inc(self.t_used, 1)

    def scalar(self, act, i, j):
        if j == 1:
            act.wait_ge(self.p_ready, i + 1)
            act.sem_inc(self.t_used, 1)
            act.wait_ge(self.kv_ready, i + 1)
            act.activation(self.sq[:, :], self.p[:, :], ACT.Square).then_inc(self.sq_ready, 1)
        if j == 4:
            act.wait_ge(self.ss_ready, i + 1)
            act.activation(self.sd[:, :], self.ss[:, :], ACT.Sqrt, bias=self.m.eps[:, 0:1], scale=1.0 / HD1).then_inc(self.sd_ready, 1)


def combine(nc, m, a):
    with ExitStack() as c:
        sem = stage_semaphores(nc, c, "cb")
        w_in, a_ready, a_taken, out_ready, x_done, own_sem = (sem(x) for x in ("_w_in", "_a_ready", "_a_taken", "_out_ready", "_x_done", "_own"))
        t_in = [sem(f"_t_in{j}") for j in range(4)]
        mark = m.mark()
        wq, wo, bo = m.take([P, 2, D]), m.take([P, 2, D]), m.take([P, D])
        kq, prod = m.take([P, 2, D]), m.take([P, 2, D])
        xt = m.take([P, 4, D])
        ps = [c.enter_context(nc.psum_tensor(f"cb_a{k}", [P, 512], F32)) for k in range(2)]
        out = [c.enter_context(nc.psum_tensor(f"cb_o{k}", [P, 512], F32)) for k in range(4)]
        with nc.Block() as block:
            @block.sync
            def _(sp):
                sp.dma_start(wq[:, :, :], by_half(a["L1_mix_wq"])).then_inc(w_in, 16)
                sp.dma_start(wo[:, :, :], by_half(a["L1_mix_wo"])).then_inc(w_in, 16)
                sp.dma_start(bo[:, :], row(a["L1_mix_bo"])).then_inc(w_in, 16)

                def load(t, j):
                    sp.wait_ge(out_ready, t + 1)
                    sp.sem_inc(m.woken_sp, 1)
                    sp.dma_start(xt[:, j, :], m.xt_dram[3, ds(t, 1), :, :].rearrange("o p d -> (o p) d")).then_inc(t_in[j], 16)
                tiles4(sp, load)

            @block.tensor
            def _(pe):
                pe.sem_inc(out_ready, 4)
                pe.wait_ge(w_in, 48)
                for k in range(2):
                    last = pe.matmul(ps[0][:, k * D:(k + 1) * D], m.kv[:, k, :], wq[:, k, :], start=True, stop=True)
                last.then_inc(a_ready, 1)
                pe.wait_ge(a_taken, 1)
                for half in range(2):
                    for k in range(2):
                        last = pe.matmul(ps[1][:, half * D:(half + 1) * D], kq[:, k, half * P:(half + 1) * P], wo[:, k, :],
                                         start=(k == 0), stop=(k == 1))
                last.then_inc(a_ready, 1)
                pe.wait_ge(a_taken, 2)

                def product(t, j):
                    pe.wait_ge(t_in[j], use16(t, j))
                    pe.wait_ge(x_done, t + 1)
                    for k in range(2):
                        last = pe.matmul(out[j][:, 0:D], xt[:, j, k * P:(k + 1) * P], prod[:, k, :], start=(k == 0), stop=(k == 1))
                    last.then_inc(out_ready, 1)
                tiles4(pe, product)

            @block.scalar
            def _(act):
                for turn, to in ((1, kq), (2, prod)):
                    act.wait_ge(a_ready, turn)
                    act.activation(to.rearrange("p k d -> p (k d)"), ps[turn - 1][:, :], ACT.Copy).then_inc(a_taken, 1)

            @block.vector
            def _(v):
                own = Count(own_sem)
                v.sem_inc(x_done, 4)
                v.wait_ge(w_in, 48)

                def group(t0, n):
                    for j in range(n):
                        x = tile_of(m.X, t0 + j)
                        own.inc(v.scalar_tensor_tensor(x, tile_of(m.AGG, t0 + j), m.norm_of(t0 + j), x, ALU.mult, ALU.add))
                    own.wait(v)
                    for j in range(n):
                        own.inc(v.tensor_tensor(tile_of(m.X, t0 + j), tile_of(m.X, t0 + j), bo[:, :], ALU.add))
                    own.wait(v)
                    for j in range(n):
                        v.wait_ge(out_ready, t0 + j + 5)
                        v.tensor_tensor(tile_of(m.X, t0 + j), tile_of(m.X, t0 + j), out[j][:, 0:D], ALU.add).then_inc(x_done, 1)
                with turns(v, 0, TURNS // 4, [(own, 8)]) as i:
                    group(i * 4, 4)
                group(TURNS, 1)
        m.release(mark)


HEADS2, HD2, SLICES = 8, 64, 64
INNER = HEADS2 * HD2
QUARTERS = INNER // P


def slice_weights(nc, m, a):
    with ExitStack() as c:
        sem = stage_semaphores(nc, c, "sw")
        w_in, clear, ready, bias_ready, own_sem = (sem(x) for x in ("_in", "_clear", "_ready", "_bias", "_own"))
        mark = m.mark()
        wx, ws = m.take([P, QUARTERS, D]), m.take([P, P])
        bx, bxb = m.take([P, QUARTERS]), m.take([P, QUARTERS, P])
        bs, temp = m.take([P, SLICES]), m.take([P, HEADS2])
        ps = [c.enter_context(nc.psum_tensor(f"sw_{k}", [P, 512], F32)) for k in range(3)]
        with nc.Block() as block:
            @block.sync
            def _(sp):
                sp.dma_start(wx[:, :, :], a["L1_ffn_W_x"].rearrange("(q p) c -> p q c", p=P)).then_inc(w_in, 16)
                sp.dma_start(bx[:, :], a["b_x_pairs"]).then_inc(w_in, 16)
                sp.dma_start(bs[:, :], row(a["L1_ffn_b_slice"])).then_inc(w_in, 16)
                sp.dma_start(temp[:, :], row(a["L1_ffn_temperature"].rearrange("a h b c -> (a h b c)"))).then_inc(w_in, 16)
                sp.wait_ge(clear, 1)
                for r in (0, HALF):
                    sp.dma_start(ws[r:r + HALF, r:r + HALF], a["L1_ffn_W_slice"]).then_inc(w_in, 16)

            @block.vector
            def _(v):
                own = Count(own_sem)
                v.memset(ws[:, :], 0.0).then_inc(clear, 1)
                v.wait_ge(w_in, 96)
                v.tensor_copy(bxb[:, :, :], bx[:, :].unsqueeze(2).to_broadcast([P, QUARTERS, P])).then_inc(bias_ready, 1)
                own.inc(v.tensor_scalar(temp[:, :], temp[:, :], 0.1, 5.0, ALU.max, ALU.min))
                own.wait(v)
                own.inc(v.reciprocal(temp[:, :], temp[:, :]))
                own.wait(v)
                v.wait_ge(ready, 1)
                by_head = lambda ap: ap.rearrange("p (h g) -> p h g", h=HEADS2)
                scale = temp[:, :].unsqueeze(2).to_broadcast([P, HEADS2, SLICES])
                for k in range(2):
                    v.tensor_tensor(by_head(m.wxs[:, k, :]), by_head(ps[k][:, :]), scale, ALU.mult)
                own.inc(v.tensor_tensor(by_head(m.bxs[:, :]), by_head(ps[2][:, :]),
                                        bs[:, :].unsqueeze(1).to_broadcast([P, HEADS2, SLICES]), ALU.add))
                own.wait(v)
                v.tensor_tensor(by_head(m.bxs[:, :]), by_head(m.bxs[:, :]), scale, ALU.mult)

            @block.tensor
            def _(pe):
                pe.wait_ge(w_in, 96)
                for q in range(QUARTERS):
                    for k in range(2):
                        pe.matmul(ps[k][:, q * P:(q + 1) * P], wx[:, q, k * P:(k + 1) * P], ws[:, :], start=True, stop=True)
                pe.wait_ge(bias_ready, 1)
                for q in range(QUARTERS):
                    last = pe.matmul(ps[2][:, q * P:(q + 1) * P], bxb[:, q, :], ws[:, :], start=True, stop=True)
                last.then_inc(ready, 1)
        m.release(mark)


def slice_sums(nc, m, name="ss"):
    with ExitStack() as c:
        sem = stage_semaphores(nc, c, name)
        h_ready, t_ready, xt_ready, l_ready, l_taken, e_ready, ex_ready, sw_ready, swt_ready, swt_taken, g_done, own_sem, sums = (
            sem(x) for x in ("_h_ready", "_t_ready", "_xt_ready", "_l_ready", "_l_taken", "_e_ready", "_ex_ready", "_sw_ready",
                             "_swt_ready", "_swt_taken", "_g_done", "_own", "_sums"))
        mark = m.mark()
        h, xt = m.take([P, 4, D + 1]), m.take([P, 2, D])
        lg, ex, sw = m.take([P, INNER]), m.take([P, INNER]), m.take([P, 2, INNER])
        mx, sm = m.take([P, HEADS2]), m.take([P, HEADS2])
        ps = lambda x: c.enter_context(nc.psum_tensor(name + x, [P, 512], F32))
        psT, psL, psW, psG = ps("_t"), [ps("_l0"), ps("_l1")], ps("_w"), [ps(f"_g{q}") for q in range(QUARTERS)]
        by_head = lambda ap: ap.rearrange("p (h g) -> p h g", h=HEADS2)
        per_head = lambda ap: ap.unsqueeze(2).to_broadcast([P, HEADS2, SLICES])
        with nc.Block() as block:
            @block.vector
            def _(v):
                own = Count(own_sem)
                own.inc(v.memset(h[:, :, D:D + 1], 1.0))
                own.wait(v)
                v.sem_inc(l_taken, 2)

                def make_h(t, j):
                    v.wait_ge(g_done, t + 1)
                    v.tensor_scalar(h[:, j, 0:D], tile_of(m.X, t), m.mean(t), m.rstd_of(t), ALU.subtract, ALU.mult).then_inc(h_ready, 1)

                def body(t, j):
                    if is_tile(t + 2):
                        make_h(t + 2, (j + 2) % 4)
                    v.wait_ge(l_ready, t + 1)
                    v.tensor_tensor(lg[:, :], psL[j % 2][:, :], m.bxs[:, :], ALU.add).then_inc(l_taken, 1)
                    v.wait_ge(l_taken, t + 3)
                    own.inc(v.tensor_reduce(mx[:, :], by_head(lg[:, :]), AX.X, ALU.max))
                    own.wait(v)
                    v.tensor_tensor(by_head(lg[:, :]), by_head(lg[:, :]), per_head(mx[:, :]), ALU.subtract).then_inc(e_ready, 1)
                    v.wait_ge(ex_ready, t + 1)
                    own.inc(v.tensor_reduce(sm[:, :], by_head(ex[:, :]), AX.X, ALU.add))
                    own.wait(v)
                    own.inc(v.reciprocal(sm[:, :], sm[:, :]))
                    own.wait(v)
                    own.inc(v.tensor_scalar(sm[:, :], sm[:, :], m.valid[:, ds(t, 1)], None, ALU.mult))
                    own.wait(v)
                    v.wait_ge(g_done, t + 3)
                    v.tensor_tensor(by_head(sw[:, j % 2, :]), by_head(ex[:, :]), per_head(sm[:, :]), ALU.mult).then_inc(sw_ready, 1)
                make_h(0, 0)
                make_h(1, 1)
                tiles4(v, body, [(own, 4)], peel=5)
                v.wait_ge(sums, 1)
                for q in range(QUARTERS):
                    v.tensor_copy(m.G[:, q, :], psG[q][:, 0:D + 1])

            @block.tensor
            def _(pe):
                pe.sem_inc(g_done, 4)
                for q in range(QUARTERS):
                    pe.matmul(psG[q][:, 0:D + 1], m.zeros[:, 0:P], m.zeros[:, :], start=True, stop=False, skip_group_check=True)

                def transposes(t, j):
                    pe.wait_ge(h_ready, t + 1)
                    pe.wait_ge(xt_ready, t + 1)
                    for k in range(2):
                        last = pe.transpose(psT[:, k * P:(k + 1) * P], h[:, j, k * P:(k + 1) * P], m.ident[:, :])
                    last.then_inc(t_ready, 1)

                def logits(t, j):
                    pe.wait_ge(xt_ready, t + 2)
                    pe.wait_ge(l_taken, t + 1)
                    for k in range(2):
                        last = pe.matmul(psL[j % 2][:, :], xt[:, j % 2, k * P:(k + 1) * P], m.wxs[:, k, :], start=(k == 0), stop=(k == 1))
                    last.then_inc(l_ready, 1)

                def body(t, j):
                    if is_tile(t + 2):
                        transposes(t + 2, (j + 2) % 4)
                    pe.wait_ge(sw_ready, t + 1)
                    pe.wait_ge(swt_taken, t + 1)
                    for q in range(QUARTERS):
                        last = pe.transpose(psW[:, q * P:(q + 1) * P], sw[:, j % 2, q * P:(q + 1) * P], m.ident[:, :])
                    last.then_inc(swt_ready, 1)
                    for q in range(QUARTERS):
                        last = pe.matmul(psG[q][:, 0:D + 1], sw[:, j % 2, q * P:(q + 1) * P], h[:, j, :], start=False, stop=False, skip_group_check=True)
                    last.then_inc(g_done, 1)
                    if is_tile(t + 2):
                        logits(t + 2, (j + 2) % 4)
                for t in range(2):
                    transposes(t, t)
                    logits(t, t)
                tiles4(pe, body, peel=5)
                for q in range(QUARTERS):
                    last = pe.matmul(psG[q][:, 0:D + 1], m.zeros[:, 0:P], m.zeros[:, :], start=False, stop=True, skip_group_check=True)
                last.then_inc(sums, 1)

            @block.scalar
            def _(act):
                act.sem_inc(xt_ready, 1)
                act.sem_inc(swt_taken, 1)

                def copy_xt(t, j):
                    act.wait_ge(t_ready, t + 1)
                    act.activation(xt[:, j % 2, :], psT[:, 0:D], ACT.Copy).then_inc(xt_ready, 1)

                def body(t, j):
                    act.wait_ge(e_ready, t + 1)
                    act.activation(ex[:, :], lg[:, :], ACT.Exp).then_inc(ex_ready, 1)
                    if is_tile(t + 2):
                        copy_xt(t + 2, (j + 2) % 4)
                    act.wait_ge(swt_ready, t + 1)
                    act.activation(m.swT[:, ds(t, 1), :].rearrange("p o n -> p (o n)"), psW[:, :], ACT.Copy).then_inc(swt_taken, 1)
                copy_xt(0, 0)
                copy_xt(1, 1)
                tiles4(act, body, peel=5)
        m.release(mark)


def slice_attention(nc, m, a):
    with ExitStack() as c:
        sem = stage_semaphores(nc, c, "sa")
        w_in, clear, pe_done, cp_done, e_ready, ex_ready, own_sem = (sem(x) for x in ("_in", "_clear", "_pe", "_cp", "_e", "_ex", "_own"))
        mark = m.mark()
        wfx, bfx, wout = m.take([P, 2, INNER]), m.take([P, INNER]), m.take([P, QUARTERS, D])
        wq, wk, wv = m.take([P, P]), m.take([P, P]), m.take([P, P])
        block4 = lambda: m.take([P, QUARTERS, P])
        gT = m.take([P, 2, INNER])
        tok, tokT, qT, kT, val, attn, attnT, osT = (block4() for _ in range(8))
        raw, dots, ex = block4(), m.take([P, QUARTERS, SLICES]), m.take([P, QUARTERS, SLICES])
        rn, mx = m.take([P, QUARTERS]), m.take([P, QUARTERS])
        ps = [c.enter_context(nc.psum_tensor(f"sa_{k}", [P, 512], F32)) for k in range(8)]
        flat = lambda ap: ap.rearrange("p q n -> p (q n)")
        quarter = lambda ap, q: ap[:, q * P:(q + 1) * P]
        with nc.Block() as block:
            @block.sync
            def _(sp):
                sp.dma_start(wfx[:, :, :], by_half(a["L1_ffn_W_fx"])).then_inc(w_in, 16)
                sp.dma_start(bfx[:, :], row(a["L1_ffn_b_fx"])).then_inc(w_in, 16)
                sp.dma_start(wout[:, :, :], a["L1_ffn_W_out"].rearrange("(q p) d -> p q d", p=P)).then_inc(w_in, 16)
                sp.wait_ge(clear, 3)
                for w, name in ((wq, "L1_ffn_W_q"), (wk, "L1_ffn_W_k"), (wv, "L1_ffn_W_v")):
                    for r in (0, HALF):
                        sp.dma_start(w[r:r + HALF, r:r + HALF], a[name]).then_inc(w_in, 16)

            @block.tensor
            def _(pe):
                pe.wait_ge(w_in, 16 * 9)
                for k in range(2):
                    for q in range(QUARTERS):
                        last = pe.transpose(quarter(ps[k], q), m.G[:, q, k * P:(k + 1) * P], m.ident[:, :])
                last.then_inc(pe_done, 1)
                pe.wait_ge(cp_done, 1)
                for q in range(QUARTERS):
                    for k in range(2):
                        last = pe.matmul(quarter(ps[2], q), gT[:, k, q * P:(q + 1) * P], wfx[:, k, q * P:(q + 1) * P], start=(k == 0), stop=(k == 1))
                last.then_inc(pe_done, 1)
                pe.wait_ge(cp_done, 2)
                for q in range(QUARTERS):
                    last = pe.transpose(quarter(ps[3], q), tok[:, q, :], m.ident[:, :])
                last.then_inc(pe_done, 1)
                pe.wait_ge(cp_done, 3)
                pe.matmul(ps[4][:, :], wq[:, :], flat(tokT), start=True, stop=True)
                pe.matmul(ps[5][:, :], wk[:, :], flat(tokT), start=True, stop=True)
                for q in range(QUARTERS):
                    last = pe.matmul(quarter(ps[6], q), tokT[:, q, :], wv[:, :], start=True, stop=True)
                last.then_inc(pe_done, 1)
                pe.wait_ge(cp_done, 4)
                for q in range(QUARTERS):
                    last = pe.matmul(quarter(ps[7], q), qT[:, q, :], kT[:, q, :], start=True, stop=True)
                last.then_inc(pe_done, 1)
                pe.wait_ge(cp_done, 5)
                for q in range(QUARTERS):
                    last = pe.transpose(quarter(ps[0], q), attn[:, q, :], m.ident[:, :])
                last.then_inc(pe_done, 1)
                pe.wait_ge(cp_done, 6)
                for q in range(QUARTERS):
                    last = pe.matmul(quarter(ps[1], q), val[:, q, :], attnT[:, q, :], start=True, stop=True)
                last.then_inc(pe_done, 1)
                pe.wait_ge(cp_done, 7)
                for q in range(QUARTERS):
                    last = pe.matmul(ps[2 + q // 2][:, (q % 2) * D:(q % 2 + 1) * D], osT[:, q, :], wout[:, q, :], start=True, stop=True)
                last.then_inc(pe_done, 1)

            @block.vector
            def _(v):
                own = Count(own_sem)
                for w in (wq, wk, wv):
                    v.memset(w[:, :], 0.0).then_inc(clear, 1)
                own.inc(v.memset(flat(tok), 0.0))
                own.inc(v.memset(flat(attn), 0.0))
                own.inc(v.tensor_scalar(rn[:, :].unsqueeze(2), m.G[:, :, D:D + 1], 1e-5, None, ALU.add))
                own.wait(v)
                own.inc(v.reciprocal(rn[:, :], rn[:, :]))
                own.wait(v)
                v.wait_ge(pe_done, 1)
                for k in range(2):
                    own.inc(v.tensor_copy(gT[:, k, :], ps[k][:, :]))
                own.wait(v)
                v.sem_inc(cp_done, 1)
                v.wait_ge(pe_done, 2)
                for q in range(QUARTERS):
                    own.inc(v.scalar_tensor_tensor(raw[:, q, :], bfx[:, q * P:(q + 1) * P], m.G[:, q, D:D + 1], quarter(ps[2], q), ALU.mult, ALU.add))
                own.wait(v)
                for q in range(QUARTERS):
                    for r in (0, HALF):
                        own.inc(v.tensor_scalar(tok[r:r + HALF, q, r:r + HALF], raw[r:r + HALF, q, r:r + HALF], rn[r:r + HALF, q:q + 1], None, ALU.mult))
                own.wait(v)
                v.sem_inc(cp_done, 1)
                v.wait_ge(pe_done, 3)
                v.tensor_copy(flat(tokT), ps[3][:, :]).then_inc(cp_done, 1)
                v.wait_ge(pe_done, 4)
                own.inc(v.tensor_copy(flat(qT), ps[4][:, :]))
                own.inc(v.tensor_copy(flat(kT), ps[5][:, :]))
                own.inc(v.tensor_copy(flat(val), ps[6][:, :]))
                own.wait(v)
                v.sem_inc(cp_done, 1)
                v.wait_ge(pe_done, 5)
                scores = ps[7][:, :].rearrange("p (q n) -> p q n", q=QUARTERS)
                for r in (0, HALF):
                    own.inc(v.tensor_copy(dots[r:r + HALF, :, :], scores[r:r + HALF, :, r:r + HALF]))
                own.wait(v)
                own.inc(v.tensor_reduce(mx[:, :], dots[:, :, :], AX.X, ALU.max))
                own.wait(v)
                per = lambda ap: ap.unsqueeze(2).to_broadcast([P, QUARTERS, SLICES])
                v.tensor_tensor(dots[:, :, :], dots[:, :, :], per(mx[:, :]), ALU.subtract).then_inc(e_ready, 1)
                v.wait_ge(ex_ready, 1)
                own.inc(v.tensor_reduce(mx[:, :], ex[:, :, :], AX.X, ALU.add))
                own.wait(v)
                own.inc(v.reciprocal(mx[:, :], mx[:, :]))
                own.wait(v)
                for r in (0, HALF):
                    own.inc(v.tensor_tensor(attn[r:r + HALF, :, r:r + HALF], ex[r:r + HALF, :, :], per(mx[:, :])[r:r + HALF, :, :], ALU.mult))
                own.wait(v)
                v.sem_inc(cp_done, 1)
                v.wait_ge(pe_done, 6)
                v.tensor_copy(flat(attnT), ps[0][:, :]).then_inc(cp_done, 1)
                v.wait_ge(pe_done, 7)
                v.tensor_copy(flat(osT), ps[1][:, :]).then_inc(cp_done, 1)
                v.wait_ge(pe_done, 8)
                for k in range(2):
                    v.tensor_copy(m.mm[:, 2 * k:2 * k + 2, :].rearrange("p q d -> p (q d)"), ps[2 + k][:, :])

            @block.scalar
            def _(act):
                act.wait_ge(e_ready, 1)
                act.activation(flat(ex), flat(dots), ACT.Exp, scale=float(HD2) ** -0.5).then_inc(ex_ready, 1)
        m.release(mark)


def deslice(nc, m, a, out):
    with ExitStack() as c:
        sem = stage_semaphores(nc, c, "de")
        b_in, sw_ready, out_ready, x_done, own_sem, written = (sem(x) for x in ("_b", "_sw_ready", "_out_ready", "_x_done", "_own", "_written"))
        mark = m.mark()
        bo, sw = m.take([P, D]), m.take([P, 4, INNER])
        ps = [c.enter_context(nc.psum_tensor(f"de_{k}", [P, 512], F32)) for k in range(2)]
        with nc.Block() as block:
            @block.sync
            def _(sp):
                sp.dma_start(bo[:, :], row(a["L1_ffn_b_out"])).then_inc(b_in, 16)
                with sp.Fori(0, TURNS // 4) as i:
                    sp.wait_ge(x_done, i * 4 + 6)
                    sp.sem_inc(m.woken_sp, 1)
                    sp.dma_start(out[ds(i * (4 * P), 4 * P), :].rearrange("(t p) d -> p t d", p=P), m.X[:, ds(i * 4, 4), :]).then_inc(written, 16)
                sp.wait_ge(x_done, TILES + 2)
                sp.dma_start(out[(TILES - 1) * P:N, :], m.X[0:LAST, TILES - 1, :]).then_inc(written, 16)
                sp.wait_ge(written, 16 * (TURNS // 4 + 1))

            @block.scalar
            def _(act):
                def body(t, j):
                    act.wait_ge(out_ready, t + 1)
                    act.activation(sw[:, j, :], m.swT[:, ds(t, 1), :].rearrange("p o n -> p (o n)"), ACT.Copy).then_inc(sw_ready, 1)
                tiles4(act, body)

            @block.tensor
            def _(pe):
                pe.sem_inc(out_ready, 4)

                def body(t, j):
                    pe.wait_ge(sw_ready, t + 1)
                    pe.wait_ge(x_done, t + 1)
                    for q in range(QUARTERS):
                        last = pe.matmul(ps[j % 2][:, 0:D], sw[:, j, q * P:(q + 1) * P], m.mm[:, q, :], start=(q == 0), stop=(q == QUARTERS - 1))
                    last.then_inc(out_ready, 1)
                tiles4(pe, body)

            @block.vector
            def _(v):
                own = Count(own_sem)
                v.sem_inc(x_done, 2)
                v.wait_ge(b_in, 16)

                def body(t, j):
                    own.inc(v.tensor_tensor(tile_of(m.X, t), tile_of(m.X, t), bo[:, :], ALU.add))
                    own.wait(v)
                    v.wait_ge(out_ready, t + 5)
                    v.tensor_tensor(tile_of(m.X, t), tile_of(m.X, t), ps[j % 2][:, 0:D], ALU.add).then_inc(x_done, 1)
                tiles4(v, body, [(own, 1)])
        m.release(mark)


def gps_program(nc, a, out):
    m = Memory(nc)
    with m.stack:
        stages_mark = m.mark()
        m.send = Send(m)
        load_and_index(nc, m, a)
        sort_by_source(nc, m)
        stats(nc, m, m.X, "sx")
        W, lw = a["L0_gnn_W"], a["L0_gnn_loop_w"]
        mark = m.mark()
        m.kvs = m.take([P, BLOCKS * WIN])
        m.kvtail = m.take([P, HEADS * VW + WIN])
        m.kvconst = m.take([P, HEADS * VW])

        def sides(l):
            def make(nc, m, name, c):
                bank = c.enter_context(nc.psum_tensor(name + "_shared", [P, 512], F32))
                loop = LoopPart(nc, m, name, c, l, lw[l], a["L0_gnn_ln_beta"][l], a["L0_gnn_bias"][l], bank, 2 if l else 6)
                if l == 0:
                    mix = MixKeys(nc, m, name, c, a, bank, loop)
                    loop.bank_taken = (mix.kv_taken, 2, 2)
                    return Side(mix, loop)
                mix = MixQueries(nc, m, name, c, a, bank, loop, l - 1)
                loop.bank_taken = (mix.q_taken, 1, 1)
                return Side(loop, mix)
            return make
        for l in range(3):
            if l:
                stats(nc, m, m.AGG, f"s{l}")
            project(nc, m, f"p{l}", l, "layer" if l else "norm", [W[l, 0], W[l, 1]], a["L0_gnn_ln_gamma"][l - 1] if l else None)
            gather_sum(nc, m, f"g{l}", 0, sides(l), banks=3 if l else 2)
        stats(nc, m, m.AGG, "s3")
        finish(nc, m, "f0", a["L0_gnn_ln_gamma"][2])
        m.release(mark)

        stats(nc, m, m.X, "sr")
        m.w1, m.w2 = m.take([P, TOP, 2, FF]), m.take([P, TOP, FB, D])
        m.gate, m.b1, m.b2 = m.take([P, TOP]), m.take([P, TOP * FB]), m.take([P, D])
        experts_mark = m.mark()
        route(nc, m, a)
        m.release(experts_mark)
        experts(nc, m)
        stats(nc, m, m.AGG, "se")
        finish(nc, m, "f1", a["L0_ffn_gamma"], a["L0_ffn_beta"])
        m.release(stages_mark)

        m.kv = m.take([P, 2, P])
        stats(nc, m, m.X, "s4")
        project(nc, m, "p3", 3, "gcn", [a["L1_gnn_W"]], a["L1_gnn_bias"])
        load_and_index(nc, m, a, "li2", second=True)
        gather_sum(nc, m, "g3", 1, lambda nc, m, name, c: Side(LinearMix(nc, m, name, c, a)), general=False, banks=4)
        combine(nc, m, a)
        m.release(stages_mark)
        stats(nc, m, m.X, "s5")
        m.wxs, m.bxs = m.take([P, 2, INNER]), m.take([P, INNER])
        m.G, m.mm = m.take([P, QUARTERS, D + 1]), m.take([P, QUARTERS, D])
        m.swT = m.big[:, 0:TILES * INNER].rearrange("p (t n) -> p t n", t=TILES)
        slice_weights(nc, m, a)
        slice_sums(nc, m)
        slice_attention(nc, m, a)
        deslice(nc, m, a, out)


_INS = [
    "x", "src", "dst", "edge_type_2", "L0_gnn_W", "L0_gnn_bias", "L0_gnn_loop_w", "L0_gnn_ln_gamma",
    "L0_gnn_ln_beta", "L0_mix_Wqkv", "L0_mix_bqkv", "L0_mix_Wproj", "L0_mix_bproj", "L0_mix_temperature",
    "L0_ffn_Wr", "L0_ffn_br", "L0_ffn_W1", "L0_ffn_b1", "L0_ffn_W2", "L0_ffn_b2", "L0_ffn_gamma", "L0_ffn_beta",
    "L1_gnn_W", "L1_gnn_bias", "L1_mix_wq", "L1_mix_wk", "L1_mix_wv", "L1_mix_wo", "L1_mix_bo", "L1_mix_ln_k_g",
    "L1_mix_ln_k_b", "L1_mix_ln_v_g", "L1_mix_ln_v_b", "L1_ffn_W_fx", "L1_ffn_b_fx", "L1_ffn_W_x", "L1_ffn_b_x",
    "L1_ffn_W_slice", "L1_ffn_b_slice", "L1_ffn_W_q", "L1_ffn_W_k", "L1_ffn_W_v", "L1_ffn_W_out", "L1_ffn_b_out",
    "L1_ffn_temperature",
]


def kernel(**inputs):
    import numpy as _np
    import concourse.bacc as _bacc
    from concourse import mybir as _mybir
    from concourse.bass_utils import run_bass_kernel_spmd as _run

    turned = {"L0_mix_Wqkv", "L0_mix_Wproj", "L1_gnn_W", "L1_mix_wk", "L1_mix_wv", "L1_mix_wo", "L1_ffn_W_x"}
    nc = _bacc.Bacc("TRN2", target_bir_lowering=False, num_devices=1)
    arrays, args = {}, {}

    def give(name, x):
        x = _np.ascontiguousarray(x)
        arrays[f"in_{name}_dram"] = x
        args[name] = nc.dram_tensor(f"in_{name}_dram", x.shape, _mybir.dt.from_np(x.dtype), kind="ExternalInput").ap()

    for name in _INS:
        x = _np.asarray(inputs[name])
        give(name, x.T if name in turned else x)
    give("b_x_pairs", _np.asarray(inputs["L1_ffn_b_x"]).reshape(QUARTERS, P).T)
    give("ident", _np.eye(P, dtype=_np.float32))
    give("pcol", _np.arange(4 * P, dtype=_np.float32).reshape(4, P).T)
    give("valid", (_np.arange(TILES * P) < N).astype(_np.float32).reshape(TILES, P).T)
    give("coef", map_coefficients(_np))
    out = nc.dram_tensor("out_0_dram", (N, D), _mybir.dt.float32, kind="ExternalOutput").ap()
    gps_program(nc, args, out)
    r = _run(nc, [arrays], core_ids=[0])
    return r.results[0]["out_0_dram"]
```
